# Optimizing a Trainium2 kernel written in Bass

```python
import numpy as np
import jax
import jax.numpy as jnp

def _softmax(x, axis=-1):
    return jax.nn.softmax(x, axis=axis)

def _gelu(x):
    return jax.nn.gelu(x, approximate=True)

def _silu(x):
    return jax.nn.silu(x)

def _sigmoid(x):
    return jax.nn.sigmoid(x)

def _layernorm(x, axis=-1, eps=1e-05):
    m = jnp.mean(x, axis=axis, keepdims=True)
    v = jnp.var(x, axis=axis, keepdims=True)
    return (x - m) / jnp.sqrt(v + eps)

def _scatter_add(tgt, idx, src, axis=0):
    return tgt.at[idx].add(src)

def _segment_sum(src, seg, n):
    return jax.ops.segment_sum(src, seg, n)
kernel_name = 'mk_gnn_resnorm_d4_gnn_r8_8f13f9'

def setup_inputs(seed: int=0):
    np.random.seed(seed)
    _w = jnp.asarray

    def _rec_inputs():
        import jax
        import jax.numpy as jnp
        _gk = jax.random.key(seed)
        x = -6.415e-05 + 1 * jax.random.normal(jax.random.fold_in(_gk, 1), (1250, 512), jnp.float32)
        _s = jax.random.randint(jax.random.fold_in(_gk, 2), (10000,), 0, 1250, jnp.int32)
        _d = jax.random.randint(jax.random.fold_in(_gk, 3), (10000,), 0, 1250, jnp.int32)
        _loop = jnp.arange(1250, dtype=jnp.int32)
        src = jnp.concatenate([_s, _d, _loop])
        dst = jnp.concatenate([_d, _s, _loop])
        _o = jnp.argsort(dst, stable=True)
        src = src[_o]
        dst = dst[_o]
        edge_type_32 = jax.random.randint(jax.random.fold_in(_gk, 14), (21250,), 0, 32, jnp.int32)
        edge_type_8 = jax.random.randint(jax.random.fold_in(_gk, 15), (21250,), 0, 8, jnp.int32)
        edge_weight = jax.random.uniform(jax.random.fold_in(_gk, 16), (21250,), jnp.float32, 0.0, 0.999998)
        edge_weight1 = jax.random.uniform(jax.random.fold_in(_gk, 17), (21250, 1), jnp.float32, 0.0, 0.999996)
        node_vec1 = jax.random.uniform(jax.random.fold_in(_gk, 18), (1250, 1), jnp.float32, 0.0, 0.999957)
        return (x, src, dst, edge_type_32, edge_type_8, edge_weight, edge_weight1, node_vec1)
    x, src, dst, edge_type_32, edge_type_8, edge_weight, edge_weight1, node_vec1 = _rec_inputs()

    def _L0_gnn_setup():
        import jax, jax.numpy as jnp
        import numpy as np
        N_NODES = 2500
        N_EDGES = 40000
        D = 512
        NUM_RELS = 8
        NUM_BASES = 4

        def _rel_graph_conv(h, src, dst, etypes, norm, basis, comp, bias, loop_w, apply_relu):
            n = h.shape[0]
            hb = jnp.einsum('nd,bdo->bno', h, basis)
            coef = comp[etypes]
            m = coef[:, 0, None] * hb[0][src]
            for b in range(1, basis.shape[0]):
                m = m + coef[:, b, None] * hb[b][src]
            m = m * norm[:, None]
            agg = jax.ops.segment_sum(m, dst, num_segments=n)
            out = agg + bias + h @ loop_w
            if apply_relu:
                out = jax.nn.relu(out)
            return out
        key = jax.random.key(seed)
        ks = jax.random.split(key, 16)
        inp = {'emb': jax.random.normal(ks[0], (N_NODES, D), dtype=jnp.float32), 'src': jax.random.randint(ks[1], (N_EDGES,), 0, N_NODES), 'dst': jax.random.randint(ks[2], (N_EDGES,), 0, N_NODES), 'etypes': jax.random.randint(ks[3], (N_EDGES,), 0, NUM_RELS), 'edge_norm': jax.random.uniform(ks[4], (N_EDGES,), dtype=jnp.float32)}
        s = 1.0 / np.sqrt(D)
        inp['basis0'] = jax.random.normal(ks[5], (NUM_BASES, D, D), dtype=jnp.float32) * s
        inp['comp0'] = jax.random.normal(ks[6], (NUM_RELS, NUM_BASES), dtype=jnp.float32)
        inp['bias0'] = jnp.zeros((D,), dtype=jnp.float32)
        inp['loop0'] = jax.random.normal(ks[7], (D, D), dtype=jnp.float32) * s
        inp['basis1'] = jax.random.normal(ks[8], (NUM_BASES, D, D), dtype=jnp.float32) * s
        inp['comp1'] = jax.random.normal(ks[9], (NUM_RELS, NUM_BASES), dtype=jnp.float32)
        inp['bias1'] = jnp.zeros((D,), dtype=jnp.float32)
        inp['loop1'] = jax.random.normal(ks[10], (D, D), dtype=jnp.float32) * s
        return inp
    _L0_gnn_all = _L0_gnn_setup()
    _L0_gnn_in = {k: v for k, v in _L0_gnn_all.items() if k in ('basis0', 'comp0', 'bias0', 'loop0', 'basis1', 'comp1', 'bias1', 'loop1')}
    del _L0_gnn_all

    def _L1_gnn_setup():
        import jax, jax.numpy as jnp
        import numpy as np
        N_NODES = 2500
        N_EDGES = 40000
        IN_FEAT = 512
        OUT_FEAT = 512
        NUM_RELS = 32
        NUM_BASES = 8
        key = jax.random.key(seed)
        ks = jax.random.split(key, 8)
        x = jax.random.normal(ks[0], (N_NODES, IN_FEAT), dtype=jnp.float32)
        bases = jax.random.normal(ks[1], (NUM_BASES, IN_FEAT, OUT_FEAT), dtype=jnp.float32) * (1.0 / np.sqrt(IN_FEAT))
        w_comp = jax.random.normal(ks[2], (NUM_RELS, NUM_BASES), dtype=jnp.float32) * (1.0 / np.sqrt(NUM_BASES))
        h_bias = jnp.zeros((OUT_FEAT,), dtype=jnp.float32)
        norm = jax.random.uniform(ks[3], (N_EDGES, 1), dtype=jnp.float32)
        src = jax.random.randint(ks[4], (N_EDGES,), 0, N_NODES, dtype=jnp.int32)
        dst = jax.random.randint(ks[5], (N_EDGES,), 0, N_NODES, dtype=jnp.int32)
        etype = jnp.sort(jax.random.randint(ks[6], (N_EDGES,), 0, NUM_RELS, dtype=jnp.int32))
        return {'x': x, 'bases': bases, 'w_comp': w_comp, 'h_bias': h_bias, 'norm': norm, 'src': src, 'dst': dst, 'etype': etype}
    _L1_gnn_all = _L1_gnn_setup()
    _L1_gnn_in = {k: v for k, v in _L1_gnn_all.items() if k in ('bases', 'w_comp', 'h_bias')}
    del _L1_gnn_all

    def _L2_gnn_setup():
        import jax, jax.numpy as jnp
        import numpy as np
        N = 6250
        E = 100000
        F_IN = 512
        F_OUT = 512
        key = jax.random.key(seed)
        k_feat, k_src, k_dst, k_w1, k_b1, k_w2, k_b2 = jax.random.split(key, 7)
        feat = jax.random.normal(k_feat, (N, F_IN), dtype=jnp.float32)
        src_idx = jax.random.randint(k_src, (E,), 0, N, dtype=jnp.int32)
        dst_idx = jax.random.randint(k_dst, (E,), 0, N, dtype=jnp.int32)
        deg = jax.ops.segment_sum(jnp.ones((E,), jnp.float32), dst_idx, num_segments=N)
        in_deg = jnp.maximum(deg, 1.0)
        stdv = 1.0 / np.sqrt(F_IN)
        W1 = jax.random.uniform(k_w1, (F_OUT, F_IN), jnp.float32, -stdv, stdv)
        b1 = jax.random.uniform(k_b1, (F_OUT,), jnp.float32, -stdv, stdv)
        W2 = jax.random.uniform(k_w2, (F_OUT, F_IN), jnp.float32, -stdv, stdv)
        b2 = jax.random.uniform(k_b2, (F_OUT,), jnp.float32, -stdv, stdv)
        return {'feat': feat, 'src_idx': src_idx, 'dst_idx': dst_idx, 'in_deg': in_deg, 'W1': W1, 'b1': b1, 'W2': W2, 'b2': b2}
    _L2_gnn_all = _L2_gnn_setup()
    _L2_gnn_in = {k: v for k, v in _L2_gnn_all.items() if k in ('W1', 'b1', 'W2', 'b2')}
    del _L2_gnn_all

    def _L3_gnn_setup():
        import jax, jax.numpy as jnp
        import numpy as np
        N_NODES = 40962
        LATENT_DIM = 512
        N_EDGES = 81924
        NUM_BLOCKS = 4
        NUM_HEADS = 4
        NUM_FREQ = 32
        BASE_PERIOD = 16
        NOISE_EMB_DIM = 16
        EPS = 1e-05

        def _cond_layer_norm(x, cond, sw, sb, bw, bb):
            mu = jnp.mean(x, axis=-1, keepdims=True)
            var = jnp.var(x, axis=-1, keepdims=True)
            xn = (x - mu) * jax.lax.rsqrt(var + EPS)
            scale = cond @ sw + sb
            bias = cond @ bw + bb
            return xn * (1.0 + scale) + bias

        def _sparse_attention(x, src, dst, wq, bq, wk, bk, wv, bv, wo, bo):
            N, D = x.shape
            H, Dh = (NUM_HEADS, D // NUM_HEADS)
            q = (x @ wq + bq).reshape(N, H, Dh) * Dh ** (-0.5)
            k = (x @ wk + bk).reshape(N, H, Dh)
            v = (x @ wv + bv).reshape(N, H, Dh)
            scores = jnp.einsum('ehd,ehd->eh', q[src], k[dst])
            smax = jax.ops.segment_max(scores, src, num_segments=N)
            ex = jnp.exp(scores - smax[src])
            denom = jax.ops.segment_sum(ex, src, num_segments=N)
            attn = ex / denom[src]
            out = jax.ops.segment_sum(attn[:, :, None] * v[dst], src, num_segments=N)
            return out.reshape(N, D) @ wo + bo

        def _forward(x, edge_index, noise_levels, f_w1, f_b1, f_w2, f_b2, s1_w, s1_b, b1_w, b1_b, wq, bq, wk, bk, wv, bv, wo, bo, s2_w, s2_b, b2_w, b2_b, m_w1, m_b1, m_w2, m_b2):
            src, dst = (edge_index[0], edge_index[1])
            freqs = jnp.arange(1, NUM_FREQ + 1, dtype=x.dtype) * (2.0 * np.pi / BASE_PERIOD)
            ph = noise_levels * freqs
            emb = jnp.concatenate([jnp.sin(ph), jnp.cos(ph)], axis=-1)
            cond = jax.nn.silu(emb @ f_w1 + f_b1) @ f_w2 + f_b2
            for i in range(NUM_BLOCKS):
                y = _cond_layer_norm(x, cond, s1_w[i], s1_b[i], b1_w[i], b1_b[i])
                y = _sparse_attention(y, src, dst, wq[i], bq[i], wk[i], bk[i], wv[i], bv[i], wo[i], bo[i])
                x = x + y
                y = _cond_layer_norm(x, cond, s2_w[i], s2_b[i], b2_w[i], b2_b[i])
                y = jax.nn.relu(y @ m_w1[i] + m_b1[i]) @ m_w2[i] + m_b2[i]
                x = x + y
            return x
        key = jax.random.key(seed)
        ks = jax.random.split(key, 20)

        def w(k, shape, s=0.02):
            return jax.random.normal(k, shape, dtype=jnp.float32) * s
        D, B, C = (LATENT_DIM, NUM_BLOCKS, NOISE_EMB_DIM)
        z = lambda *s: jnp.zeros(s, jnp.float32)
        return {'latent_mesh_nodes': jax.random.normal(ks[0], (N_NODES, D), dtype=jnp.float32), 'edge_index': jax.random.randint(ks[1], (2, N_EDGES), 0, N_NODES, dtype=jnp.int32), 'noise_levels': jax.random.uniform(ks[2], (N_NODES, 1), dtype=jnp.float32), 'f_w1': w(ks[3], (2 * NUM_FREQ, C)), 'f_b1': z(C), 'f_w2': w(ks[4], (C, C)), 'f_b2': z(C), 's1_w': w(ks[5], (B, C, D)), 's1_b': z(B, D), 'b1_w': w(ks[6], (B, C, D)), 'b1_b': z(B, D), 'wq': w(ks[7], (B, D, D)), 'bq': z(B, D), 'wk': w(ks[8], (B, D, D)), 'bk': z(B, D), 'wv': w(ks[9], (B, D, D)), 'bv': z(B, D), 'wo': w(ks[10], (B, D, D)), 'bo': z(B, D), 's2_w': w(ks[11], (B, C, D)), 's2_b': z(B, D), 'b2_w': w(ks[12], (B, C, D)), 'b2_b': z(B, D), 'm_w1': w(ks[13], (B, D, D)), 'm_b1': z(B, D), 'm_w2': w(ks[14], (B, D, D)), 'm_b2': z(B, D)}
    _L3_gnn_all = _L3_gnn_setup()
    _L3_gnn_in = {k: v for k, v in _L3_gnn_all.items() if k in ('f_w1', 'f_b1', 'f_w2', 'f_b2', 's1_w', 's1_b', 'b1_w', 'b1_b', 'wq', 'bq', 'wk', 'bk', 'wv', 'bv', 'wo', 'bo', 's2_w', 's2_b', 'b2_w', 'b2_b', 'm_w1', 'm_b1', 'm_w2', 'm_b2')}
    del _L3_gnn_all
    return {'x': x, 'src': src, 'dst': dst, 'edge_type_32': edge_type_32, 'edge_type_8': edge_type_8, 'edge_weight': edge_weight, 'edge_weight1': edge_weight1, 'node_vec1': node_vec1, 'L0_gnn_basis0': _L0_gnn_in['basis0'], 'L0_gnn_comp0': _L0_gnn_in['comp0'], 'L0_gnn_bias0': _L0_gnn_in['bias0'], 'L0_gnn_loop0': _L0_gnn_in['loop0'], 'L0_gnn_basis1': _L0_gnn_in['basis1'], 'L0_gnn_comp1': _L0_gnn_in['comp1'], 'L0_gnn_bias1': _L0_gnn_in['bias1'], 'L0_gnn_loop1': _L0_gnn_in['loop1'], 'L1_gnn_bases': _L1_gnn_in['bases'], 'L1_gnn_w_comp': _L1_gnn_in['w_comp'], 'L1_gnn_h_bias': _L1_gnn_in['h_bias'], 'L2_gnn_W1': _L2_gnn_in['W1'], 'L2_gnn_b1': _L2_gnn_in['b1'], 'L2_gnn_W2': _L2_gnn_in['W2'], 'L2_gnn_b2': _L2_gnn_in['b2'], 'L3_gnn_f_w1': _L3_gnn_in['f_w1'], 'L3_gnn_f_b1': _L3_gnn_in['f_b1'], 'L3_gnn_f_w2': _L3_gnn_in['f_w2'], 'L3_gnn_f_b2': _L3_gnn_in['f_b2'], 'L3_gnn_s1_w': _L3_gnn_in['s1_w'], 'L3_gnn_s1_b': _L3_gnn_in['s1_b'], 'L3_gnn_b1_w': _L3_gnn_in['b1_w'], 'L3_gnn_b1_b': _L3_gnn_in['b1_b'], 'L3_gnn_wq': _L3_gnn_in['wq'], 'L3_gnn_bq': _L3_gnn_in['bq'], 'L3_gnn_wk': _L3_gnn_in['wk'], 'L3_gnn_bk': _L3_gnn_in['bk'], 'L3_gnn_wv': _L3_gnn_in['wv'], 'L3_gnn_bv': _L3_gnn_in['bv'], 'L3_gnn_wo': _L3_gnn_in['wo'], 'L3_gnn_bo': _L3_gnn_in['bo'], 'L3_gnn_s2_w': _L3_gnn_in['s2_w'], 'L3_gnn_s2_b': _L3_gnn_in['s2_b'], 'L3_gnn_b2_w': _L3_gnn_in['b2_w'], 'L3_gnn_b2_b': _L3_gnn_in['b2_b'], 'L3_gnn_m_w1': _L3_gnn_in['m_w1'], 'L3_gnn_m_b1': _L3_gnn_in['m_b1'], 'L3_gnn_m_w2': _L3_gnn_in['m_w2'], 'L3_gnn_m_b2': _L3_gnn_in['m_b2']}

def reference(x, src, dst, edge_type_32, edge_type_8, edge_weight, edge_weight1, node_vec1, L0_gnn_basis0, L0_gnn_comp0, L0_gnn_bias0, L0_gnn_loop0, L0_gnn_basis1, L0_gnn_comp1, L0_gnn_bias1, L0_gnn_loop1, L1_gnn_bases, L1_gnn_w_comp, L1_gnn_h_bias, L2_gnn_W1, L2_gnn_b1, L2_gnn_W2, L2_gnn_b2, L3_gnn_f_w1, L3_gnn_f_b1, L3_gnn_f_w2, L3_gnn_f_b2, L3_gnn_s1_w, L3_gnn_s1_b, L3_gnn_b1_w, L3_gnn_b1_b, L3_gnn_wq, L3_gnn_bq, L3_gnn_wk, L3_gnn_bk, L3_gnn_wv, L3_gnn_bv, L3_gnn_wo, L3_gnn_bo, L3_gnn_s2_w, L3_gnn_s2_b, L3_gnn_b2_w, L3_gnn_b2_b, L3_gnn_m_w1, L3_gnn_m_b1, L3_gnn_m_w2, L3_gnn_m_b2):
    import jax
    import jax.numpy as jnp

    def _L0_gnn_ref(emb, src, dst, etypes, edge_norm, basis0, comp0, bias0, loop0, basis1, comp1, bias1, loop1):
        import jax, jax.numpy as jnp
        import numpy as np
        N_NODES = 2500
        N_EDGES = 40000
        D = 512
        NUM_RELS = 8
        NUM_BASES = 4

        def _rel_graph_conv(h, src, dst, etypes, norm, basis, comp, bias, loop_w, apply_relu):
            n = h.shape[0]
            hb = jnp.einsum('nd,bdo->bno', h, basis)
            coef = comp[etypes]
            m = coef[:, 0, None] * hb[0][src]
            for b in range(1, basis.shape[0]):
                m = m + coef[:, b, None] * hb[b][src]
            m = m * norm[:, None]
            agg = jax.ops.segment_sum(m, dst, num_segments=n)
            out = agg + bias + h @ loop_w
            if apply_relu:
                out = jax.nn.relu(out)
            return out
        h = _rel_graph_conv(emb, src, dst, etypes, edge_norm, basis0, comp0, bias0, loop0, True)
        h = _rel_graph_conv(h, src, dst, etypes, edge_norm, basis1, comp1, bias1, loop1, False)
        return h

    def _L1_gnn_ref(x, bases, w_comp, h_bias, norm, src, dst, etype):
        import jax, jax.numpy as jnp
        import numpy as np
        N_NODES = 2500
        N_EDGES = 40000
        IN_FEAT = 512
        OUT_FEAT = 512
        NUM_RELS = 32
        NUM_BASES = 8
        n_nodes = x.shape[0]
        weight = jnp.einsum('rb,bio->rio', w_comp, bases)
        h_rel = jnp.einsum('ni,rio->rno', x, weight)
        msg = h_rel[etype, src] * norm
        out = jax.ops.segment_sum(msg, dst, num_segments=n_nodes)
        out = out + h_bias
        return out

    def _L2_gnn_ref(feat, src_idx, dst_idx, in_deg, W1, b1, W2, b2):
        import jax, jax.numpy as jnp
        import numpy as np
        N = 6250
        E = 100000
        F_IN = 512
        F_OUT = 512
        num_dst = in_deg.shape[0]
        agg = jax.ops.segment_sum(feat[src_idx], dst_idx, num_segments=num_dst)
        ah = agg / in_deg[:, None]
        out = jnp.einsum('nf,of->no', feat[:num_dst], W1) + b1 + jnp.einsum('nf,of->no', ah, W2) + b2
        return out

    def _L3_gnn_ref(latent_mesh_nodes, edge_index, noise_levels, f_w1, f_b1, f_w2, f_b2, s1_w, s1_b, b1_w, b1_b, wq, bq, wk, bk, wv, bv, wo, bo, s2_w, s2_b, b2_w, b2_b, m_w1, m_b1, m_w2, m_b2):
        import jax, jax.numpy as jnp
        import numpy as np
        N_NODES = 40962
        LATENT_DIM = 512
        N_EDGES = 81924
        NUM_BLOCKS = 4
        NUM_HEADS = 4
        NUM_FREQ = 32
        BASE_PERIOD = 16
        NOISE_EMB_DIM = 16
        EPS = 1e-05

        def _cond_layer_norm(x, cond, sw, sb, bw, bb):
            mu = jnp.mean(x, axis=-1, keepdims=True)
            var = jnp.var(x, axis=-1, keepdims=True)
            xn = (x - mu) * jax.lax.rsqrt(var + EPS)
            scale = cond @ sw + sb
            bias = cond @ bw + bb
            return xn * (1.0 + scale) + bias

        def _sparse_attention(x, src, dst, wq, bq, wk, bk, wv, bv, wo, bo):
            N, D = x.shape
            H, Dh = (NUM_HEADS, D // NUM_HEADS)
            q = (x @ wq + bq).reshape(N, H, Dh) * Dh ** (-0.5)
            k = (x @ wk + bk).reshape(N, H, Dh)
            v = (x @ wv + bv).reshape(N, H, Dh)
            scores = jnp.einsum('ehd,ehd->eh', q[src], k[dst])
            smax = jax.ops.segment_max(scores, src, num_segments=N)
            ex = jnp.exp(scores - smax[src])
            denom = jax.ops.segment_sum(ex, src, num_segments=N)
            attn = ex / denom[src]
            out = jax.ops.segment_sum(attn[:, :, None] * v[dst], src, num_segments=N)
            return out.reshape(N, D) @ wo + bo

        def _forward(x, edge_index, noise_levels, f_w1, f_b1, f_w2, f_b2, s1_w, s1_b, b1_w, b1_b, wq, bq, wk, bk, wv, bv, wo, bo, s2_w, s2_b, b2_w, b2_b, m_w1, m_b1, m_w2, m_b2):
            src, dst = (edge_index[0], edge_index[1])
            freqs = jnp.arange(1, NUM_FREQ + 1, dtype=x.dtype) * (2.0 * np.pi / BASE_PERIOD)
            ph = noise_levels * freqs
            emb = jnp.concatenate([jnp.sin(ph), jnp.cos(ph)], axis=-1)
            cond = jax.nn.silu(emb @ f_w1 + f_b1) @ f_w2 + f_b2
            for i in range(NUM_BLOCKS):
                y = _cond_layer_norm(x, cond, s1_w[i], s1_b[i], b1_w[i], b1_b[i])
                y = _sparse_attention(y, src, dst, wq[i], bq[i], wk[i], bk[i], wv[i], bv[i], wo[i], bo[i])
                x = x + y
                y = _cond_layer_norm(x, cond, s2_w[i], s2_b[i], b2_w[i], b2_b[i])
                y = jax.nn.relu(y @ m_w1[i] + m_b1[i]) @ m_w2[i] + m_b2[i]
                x = x + y
            return x
        return _forward(latent_mesh_nodes, edge_index, noise_levels, f_w1, f_b1, f_w2, f_b2, s1_w, s1_b, b1_w, b1_b, wq, bq, wk, bk, wv, bv, wo, bo, s2_w, s2_b, b2_w, b2_b, m_w1, m_b1, m_w2, m_b2)
    edge_index = jnp.stack([src, dst])
    deg = jnp.maximum(jax.ops.segment_sum(jnp.ones(dst.shape, jnp.float32), dst, num_segments=1250), 1.0)
    x = _layernorm(x + _L0_gnn_ref(x, src, dst, edge_type_8, edge_weight, L0_gnn_basis0, L0_gnn_comp0, L0_gnn_bias0, L0_gnn_loop0, L0_gnn_basis1, L0_gnn_comp1, L0_gnn_bias1, L0_gnn_loop1), axis=-1)
    x = _layernorm(x + _L1_gnn_ref(x, L1_gnn_bases, L1_gnn_w_comp, L1_gnn_h_bias, edge_weight1, src, dst, edge_type_32), axis=-1)
    x = _layernorm(x + _L2_gnn_ref(x, src, dst, deg, L2_gnn_W1, L2_gnn_b1, L2_gnn_W2, L2_gnn_b2), axis=-1)
    x = _layernorm(x + _L3_gnn_ref(x, edge_index, node_vec1, L3_gnn_f_w1, L3_gnn_f_b1, L3_gnn_f_w2, L3_gnn_f_b2, L3_gnn_s1_w, L3_gnn_s1_b, L3_gnn_b1_w, L3_gnn_b1_b, L3_gnn_wq, L3_gnn_bq, L3_gnn_wk, L3_gnn_bk, L3_gnn_wv, L3_gnn_bv, L3_gnn_wo, L3_gnn_bo, L3_gnn_s2_w, L3_gnn_s2_b, L3_gnn_b2_w, L3_gnn_b2_b, L3_gnn_m_w1, L3_gnn_m_b1, L3_gnn_m_w2, L3_gnn_m_b2), axis=-1)
    return x

_drawn_inputs = setup_inputs


def setup_inputs(seed=0):
    import zlib

    import numpy as np

    out = dict(_drawn_inputs(seed))
    spreads = {'L0_gnn_bias0': (0.0, 0.365),
     'L0_gnn_bias1': (0.0, 0.8),
     'L1_gnn_h_bias': (0.0, 0.1),
     'L3_gnn_f_b1': (0.0, 0.8),
     'L3_gnn_f_b2': (0.0, 0.8),
     'L3_gnn_s1_b': (0.0, 0.656),
     'L3_gnn_b1_b': (0.0, 0.389),
     'L3_gnn_bq': (0.0, 0.8),
     'L3_gnn_bk': (0.0, 0.8),
     'L3_gnn_bv': (0.0, 0.1),
     'L3_gnn_bo': (0.0, 0.1),
     'L3_gnn_s2_b': (0.0, 0.575),
     'L3_gnn_b2_b': (0.0, 0.538),
     'L3_gnn_m_b1': (0.0, 0.1),
     'L3_gnn_m_b2': (0.0, 0.1)}
    factors = {'node_vec1': 8.0,
     'L2_gnn_b1': 2.708,
     'L3_gnn_f_w1': 8.0,
     'L3_gnn_f_w2': 8.0,
     'L3_gnn_s1_w': 8.0,
     'L3_gnn_b1_w': 8.0,
     'L3_gnn_wq': 6.996,
     'L3_gnn_wk': 6.801,
     'L3_gnn_s2_w': 8.0,
     'L3_gnn_b2_w': 8.0}
    for name, (base, spread) in spreads.items():
        noise = np.random.default_rng([zlib.crc32(name.encode()), seed]).standard_normal(out[name].shape)
        drawn = base * np.exp(spread * noise) if base else spread * noise
        out[name] = jnp.asarray(drawn.astype(out[name].dtype))
    for name, factor in factors.items():
        out[name] = (out[name] * factor).astype(out[name].dtype)
    return out
```

```python
import concourse.bass as bass
from concourse import mybir

F32, I32, BF16 = mybir.dt.float32, mybir.dt.int32, mybir.dt.bfloat16
ALU = mybir.AluOpType
ACT = mybir.ActivationFunctionType
AX = mybir.AxisListType
ds = bass.ds

P = 128
N = 1250
NT = -(-N // P)
NP = NT * P
D = 512
KC = D // P
E = 21250
T = -(-E // (4 * P)) * 4
PAD_DST = NP - 1
HEADS, BLOCKS = 4, 4
DH = D // HEADS
HALF = NT // 2
EPS = 1e-5
NEG = 1e30
U = 4
FREQ, COND = 32, 16


class Path:

    def __init__(self, shift, tiles=1):
        self.shift, self.nodes, self.tiles = shift, 1 << shift, tiles
        self.windows = NP >> shift
        self.groups = T // tiles
        self.steps = -(-(self.groups + self.windows - 1) // U) * U


PATH0, PATH1, PATHC = Path(5), Path(4), Path(7, 4)


class Token:

    def __init__(self, track, frame, base, off):
        self.track, self.frame, self.base, self.off = track, frame, base, off


class Track:

    def __init__(self, sync, name, unit):
        self.sync, self.name, self.unit = sync, name, unit
        self.sem = sync.nc.alloc_semaphore(name)
        self.base, self.off = 0, 0
        sync.tracks.append(self)

    def done(self, instruction, label=None):
        instruction.then_inc(self.sem, self.unit)
        self.off += self.unit
        frame = self.sync.frames[-1]
        if label is not None:
            self.sync.marks[frame, self.name, label] = self.off
        return Token(self, frame, self.base, self.off)


class Sync:

    def __init__(self, nc, counts):
        self.nc, self.counts, self.tracks = nc, counts, []
        self.frames, self.marks, self.waited, self.loops = ["top"], {}, {}, 0
        self.idle = nc.alloc_semaphore("idle")
        self.pe, self.act = Track(self, "pe_done", 1), Track(self, "act_done", 1)
        self.dve, self.pool = Track(self, "dve_done", 1), Track(self, "pool_done", 1)

    def wait(self, engine, *tokens):
        for t in tokens:
            key = (id(engine), t.track.name, t.frame, self.frames[-1])
            if self.waited.get(key, -1) < t.off:
                self.waited[key] = t.off
                self.wait_value(engine, t.track.sem, t.base + t.off)

    def wait_value(self, engine, sem, value):
        engine.wait_ge(sem, value)
        if not isinstance(value, int):
            engine.sem_inc(self.idle, 1)

    def wait_previous(self, engine, track, label):
        frame = self.frames[-1]
        per = self.counts.get(("per", frame, track.name), 1)
        mark = self.counts.get(("mark", frame, track.name, label), 1)
        self.wait_value(engine, track.sem, track.base + (mark - per))

    def meet(self):
        for engine in (self.nc.tensor, self.nc.scalar, self.nc.vector, self.nc.gpsimd, self.nc.sync):
            for t in self.tracks:
                if t.off:
                    self.wait(engine, Token(t, self.frames[-1], t.base, t.off))

    def loop(self, trips):
        return _Loop(self, trips)


class _Loop:
    def __init__(self, sync, trips):
        self.sync, self.trips = sync, trips

    def __enter__(self):
        s = self.sync
        s.loops += 1
        self.frame = f"loop{s.loops}"
        self.fori = s.nc.Fori(0, self.trips)
        i = self.fori.__enter__()
        s.frames.append(self.frame)
        self.saved = [(t, t.base, t.off) for t in s.tracks]
        for t in s.tracks:
            per = s.counts.get(("per", self.frame, t.name), 0)
            t.base = (t.base + t.off) + i * per if per else t.base + t.off
            t.off = 0
        return i

    def __exit__(self, *exc):
        s = self.sync
        known = {t for t, _, _ in self.saved}
        for t, base, off in self.saved:
            s.counts["per", self.frame, t.name] = t.off
            t.base, t.off = base, off + self.trips * t.off
        for (frame, name, label), off in s.marks.items():
            s.counts["mark", frame, name, label] = off
        assert all(t in known for t in s.tracks), "make tracks outside loops"
        s.frames.pop()
        return self.fori.__exit__(*exc)


class Arena:

    def __init__(self, nc):
        self.nc, self.at, self.n = nc, -(-nc.sbuf_base // 64) * 64, 0
        self.end = nc.sbuf_usable_end

    def new(self, name, shape, dtype=F32):
        size = mybir.dt.size(dtype)
        for d in shape[1:]:
            size *= d
        self.n += 1
        t = self.nc.alloc_sbuf_tensor_at(f"{name}_{self.n}", shape, dtype, offset=self.at)
        self.at += -(-size // 32) * 32
        assert self.at <= self.end, (name, self.at, self.end)
        return t


def build(nc, A, out, counts):
    S = Sync(nc, counts)
    wait, prev = S.wait, S.wait_previous
    pe, act, dve, pool, sp = nc.tensor, nc.scalar, nc.vector, nc.gpsimd, nc.sync
    M = Arena(nc)
    gather_in = [Track(S, f"gather{u}_in", 16) for u in range(U)]
    chunk_in = [Track(S, f"weight_chunk{u}_in", 16) for u in range(4)]
    tile_in = [Track(S, f"tile{u}_in", 16) for u in range(2)]
    tile_out = [Track(S, f"tile{u}_out", 16) for u in range(2)]
    head_in = Track(S, "head_weights_in", 16)
    block_in = Track(S, "block_weights_in", 16)
    misc_in = Track(S, "misc_in", 16)
    x_in = Track(S, "x_in", 16)
    out_done = Track(S, "out_done", 16)

    bank = [nc.alloc_psum_tensor(f"bank{b}", [P, 512], F32) for b in range(8)]

    hidden_rows = nc.dram_tensor("hidden_rows", (NP, D), F32, kind="Internal").ap()
    x1_rows = nc.dram_tensor("x1_rows", (NP, D), F32, kind="Internal").ap()
    x2_rows = nc.dram_tensor("x2_rows", (NP, D), F32, kind="Internal").ap()

    ident = M.new("ident", [P, P])
    ones = M.new("ones", [P, P])
    sched = {p: (M.new("tile_of_step", [1, p.steps], I32), M.new("window_of_step", [1, p.steps], I32))
             for p in (PATH0, PATH1, PATHC)}
    brow = M.new("bias_row", [1, D])
    stat = M.new("ln_stats", [P, HALF, 6])
    mv = M.new("ln_mean_var", [P, HALF, 2])
    rstd = M.new("ln_rstd", [P, HALF, 1])
    after_constants = M.at
    iota = M.new("node_iota", [P, NP + P])
    src_i = M.new("src_index", [P, T], I32)
    src_f = M.new("src_float", [P, T])
    dst_f = M.new("dst_float", [P, T])
    coef = {"L0a": M.new("coef_L0a", [P, 4, T]), "L0b": M.new("coef_L0b", [P, 4, T]),
            "L1": M.new("coef_L1", [P, 8, T])}
    after_edges = M.at

    c0 = S.dve.done(dve.memset(ident[:], 0.0))
    c1 = S.dve.done(dve.memset(ones[:], 1.0))
    wait(pool, c0)
    ident_ready = S.pool.done(pool.affine_select(
        out=ident[:], in_=ident[:], compare_op=ALU.not_equal, fill=1.0, base=0, pattern=[[-1, P]],
        channel_multiplier=1))
    iota_i = M.new("iota_int", [P, NP + P], I32)
    k1 = S.pool.done(pool.iota(iota_i[:], pattern=[[1, NP + P]], base=0, channel_multiplier=0))
    wait(dve, k1)
    iota_ready = S.dve.done(dve.tensor_copy(iota[:], iota_i[:]))

    dst_i = M.new("dst_int", [P, T], I32)
    et = M.new("types_int", [P, 2, T], I32)
    et_f = M.new("types_float", [P, 2, T])
    w = M.new("weights", [P, 2, T])
    comp = M.new("comp", [P, 8 * 4 * 2 + 32 * 8])
    last_i = M.new("last_dst", [P, 2], I32)
    for d, s in ((src_i[:], A["src"]), (dst_i[:], A["dst"]), (et[:, 0, :], A["edge_type_8"]),
                 (et[:, 1, :], A["edge_type_32"]), (w[:, 0, :], A["edge_weight"]),
                 (w[:, 1, :], A["edge_weight1"])):
        t = S_in = misc_in.done(sp.dma_start(d, s))
    at = 0
    for name, n in (("L0_gnn_comp0", 32), ("L0_gnn_comp1", 32), ("L1_gnn_w_comp", 256)):
        row = A[name].rearrange("r b -> (r b)").rearrange("(a n) -> a n", a=1)
        t = misc_in.done(sp.dma_start(comp[:, at:at + n], bass.AP(
            tensor=row.tensor, offset=row.offset, ap=[[0, P], [1, n]])))
        at += n
    edges_in = t
    wait(dve, edges_in)
    S.dve.done(dve.tensor_copy(src_f[:], src_i[:]))
    S.dve.done(dve.tensor_copy(dst_f[:], dst_i[:]))
    et_ready = S.dve.done(dve.tensor_copy(et_f[:], et[:]))
    wait(dve, et_ready)

    mask = M.new("relation_mask", [P, 2, T])

    def coefficients(kind, relations, outs):
        first = [S.dve.done(dve.memset(o[:], 0.0)) for o, _, _ in outs]
        wait(dve, *first)
        for r in range(relations):
            m = S.dve.done(dve.scalar_tensor_tensor(mask[:, r % 2, :], et_f[:, kind, :], float(r),
                                                    w[:, kind, :], ALU.is_equal, ALU.mult))
            wait(dve, m)
            for o, table, nb in outs:
                for b in range(nb):
                    at = table + r * nb + b
                    t = S.dve.done(dve.scalar_tensor_tensor(o[:, b, :], mask[:, r % 2, :], comp[:, at:at + 1],
                                                            o[:, b, :], ALU.mult, ALU.add))
        return t

    wait(dve, coefficients(0, 8, [(coef["L0a"], 0, 4), (coef["L0b"], 32, 4)]))
    wait(dve, coefficients(1, 32, [(coef["L1"], 64, 8)]))

    for n, path in enumerate((PATH0, PATH1, PATHC)):
        G, span = path.groups, path.tiles * P
        last = M.new("last", [P, 2], I32)
        key = M.new("key", [P, 2])
        hit = M.new("hit", [P, 2, path.steps])
        tf = M.new("tf", [1, path.steps])
        clear = S.dve.done(dve.memset(last[:], 0))
        wait(sp, clear)
        flat = A["dst_flat"].rearrange("(g s) -> g s", s=span)
        for c in range(-(-G // P)):
            rows = min(P, G - c * P)
            t = misc_in.done(sp.dma_start(last[0:rows, c:c + 1], flat[c * P:c * P + rows, span - 1:span],
                                       allow_slow_non_contiguous=True))
        wait(dve, t)
        a = S.dve.done(dve.tensor_single_scalar(last[:], last[:], path.shift, ALU.arith_shift_right))
        wait(dve, a)
        a = S.dve.done(dve.tensor_copy(key[:], last[:]))
        gi = M.new("gi", [P, 2], I32)
        gf = M.new("gf", [P, 2])
        b = S.pool.done(pool.iota(gi[:], pattern=[[P, 2]], base=0, channel_multiplier=1))
        wait(dve, a, b)
        b = S.dve.done(dve.tensor_copy(gf[:], gi[:]))
        wait(dve, b)
        a = S.dve.done(dve.tensor_tensor(key[:], key[:], gf[:], ALU.add))
        wait(dve, a, iota_ready)
        for c in range(-(-G // P)):
            rows = min(P, G - c * P)
            a = S.dve.done(dve.tensor_scalar(hit[0:rows, c, :], iota[0:rows, 0:path.steps], key[0:rows, c:c + 1],
                                             None, ALU.is_gt))
        wait(pe, a, c1)
        for c in range(-(-G // P)):
            rows = min(P, G - c * P)
            ins = pe.matmul(bank[n][0:1, 0:path.steps], ones[0:rows, 0:1], hit[0:rows, c, :],
                            start=c == 0, stop=c == -(-G // P) - 1)
        a = S.pe.done(ins)
        wait(dve, a)
        a = S.dve.done(dve.tensor_scalar(tf[:], bank[n][0:1, 0:path.steps], float(G - 1), None, ALU.min))
        wait(dve, a)
        S.dve.done(dve.tensor_copy(sched[path][0][:], tf[:]))
        a = S.dve.done(dve.tensor_tensor(tf[:], iota[0:1, 0:path.steps], tf[:], ALU.subtract))
        wait(dve, a)
        sched_ready = S.dve.done(dve.tensor_scalar(sched[path][1][:], tf[:], float(path.windows), None, ALU.min))

    M.at = after_edges

    def count_matrix(count):
        oh_src = M.new("onehot_src", [P, PATHC.tiles, NP], BF16)
        src_now = M.new("src_now", [P, PATHC.tiles])
        oh_dst = M.new("onehot_dst", [P, PATHC.tiles, P], BF16)
        wait(dve, sched_ready)
        z = S.dve.done(dve.memset(count[:], 0.0))
        wait(dve, z, sched_ready)
        wait(pool, sched_ready)
        nt = PATHC.tiles
        tiles, windows = sched[PATHC]
        with S.loop(PATHC.steps // 2) as i:
            for u in range(2):
                tg = pool.value_load(tiles[0:1, ds(i * 2 + u, 1)], min_val=0, max_val=PATHC.groups - 1)
                vg = dve.value_load(tiles[0:1, ds(i * 2 + u, 1)], min_val=0, max_val=PATHC.groups - 1)
                vw = dve.value_load(windows[0:1, ds(i * 2 + u, 1)], min_val=0, max_val=PATHC.windows)
                for eng, which, tr in ((pool, (0, 1), S.pool), (dve, (2, 3), S.dve)):
                    if u == 0:
                        prev(eng, S.pe, "step1")
                    else:
                        wait(eng, multiplied)
                    g = tg if eng is pool else vg
                    if eng is pool:
                        made = tr.done(pool.tensor_copy(src_now[:], src_f[:, ds(g * nt, nt)]))
                        wait(pool, made)
                    for q in which:
                        node = src_now[:, q:q + 1] if eng is pool else src_f[:, ds(g * nt + q, 1)]
                        made = tr.done(eng.tensor_scalar(oh_src[:, q, :], iota[:, 0:NP], node, None,
                                                         ALU.is_equal))
                    if eng is pool:
                        made_pool = made
                for q in range(nt):
                    made = S.dve.done(dve.tensor_scalar(oh_dst[:, q, :], iota[:, ds(vw * P, P)],
                                                        dst_f[:, ds(vg * nt + q, 1)], None, ALU.is_equal))
                wait(pe, made_pool, made)
                prev(pe, S.dve, f"added{u}")
                for j in range(NT):
                    for q in range(nt):
                        ins = pe.matmul(bank[4 * u + j // 4][:, (j % 4) * P:(j % 4 + 1) * P],
                                        oh_src[:, q, j * P:(j + 1) * P], oh_dst[:, q, :],
                                        start=q == 0, stop=q == nt - 1)
                multiplied = S.pe.done(ins, f"step{u}")
                wait(dve, multiplied)
                if u == 0:
                    prev(dve, S.dve, "added1")
                else:
                    wait(dve, added)
                for b0, n in ((0, 4), (1, 4), (2, 2)):
                    dst = count[:, 4 * b0:4 * b0 + n, ds(vw * P, P)]
                    added = S.dve.done(dve.tensor_tensor(
                        dst, dst, bank[4 * u + b0][:, 0:n * P].rearrange("p (j n) -> p j n", n=P), ALU.add),
                        f"added{u}")
        return added

    count_rows = nc.dram_tensor("count_rows", (P, NT * (NP + P)), F32, kind="Internal").ap()
    count = M.new("count", [P, NT, NP + P])
    count_done = count_matrix(count)
    wait(sp, count_done)
    count_out = misc_in.done(sp.dma_start(count_rows, count[:].rearrange("p j n -> p (j n)")))

    def transpose_tile(src, dstT, j, b, ready, after=()):
        wait(pe, *ready)
        for k in range(KC):
            ins = pe.transpose(bank[b][:, k * P:(k + 1) * P], src[:, k * P:(k + 1) * P], ident[:])
        a = S.pe.done(ins)
        eng, tr = ((act, S.act), (dve, S.dve))[j % 2]
        wait(eng, a, *after)
        o = dstT[:, :, j * P:(j + 1) * P]
        i = bank[b][:].rearrange("p (k n) -> p k n", k=KC)
        return tr.done(act.copy(o, i) if eng is act else dve.tensor_copy(o, i))

    def normalize(tiles, ready, outs, free=()):
        n = len(tiles)
        wait(dve, *ready)
        for j in range(n):
            a = S.dve.done(dve.bn_stats(stat[:, j, :], tiles[j]))
        wait(dve, a)
        for j in range(n):
            a = S.dve.done(dve.bn_aggr(mv[:, j, :], stat[:, j, :]))
        wait(dve, a)
        a = S.dve.done(dve.tensor_scalar_add(rstd[:, 0:n, :], mv[:, 0:n, 1:2], EPS))
        wait(act, a)
        a = S.act.done(act.activation(rstd[:, 0:n, :], rstd[:, 0:n, :], ACT.Sqrt))
        wait(dve, a)
        a = S.dve.done(dve.reciprocal(rstd[:, 0:n, :], rstd[:, 0:n, :]))
        wait(dve, a, *free)
        return [S.dve.done(dve.tensor_scalar(outs[j], tiles[j], mv[:, j, 0:1], rstd[:, j, :],
                                             ALU.subtract, ALU.mult)) for j in range(n)]

    def aggregate(path, nb, co, rows, G, ready):
        xs = M.new("gathered", [P, U, D])
        sel = M.new("selector", [P, U, P])
        idx = M.new("gather_index", [P, U], I32)
        S.meet()
        z = S.dve.done(dve.memset(G[:], 0.0))
        S.meet()
        tiles, windows = sched[path]
        with S.loop(path.steps // U) as i:
            gathered, selected = [], []
            for u in range(U):
                tg = pool.value_load(tiles[0:1, ds(i * U + u, 1)], min_val=0, max_val=T - 1)
                prev(pool, S.pe, f"step{u}")
                a = S.pool.done(pool.tensor_copy(idx[:, u:u + 1], src_i[:, ds(tg, 1)]))
                wait(pool, a)
                gathered.append(gather_in[u].done(pool.indirect_dma_start(
                    xs[:, u, :], None, rows, bass.IndirectOffsetOnAxis(ap=idx[:, u:u + 1], axis=0))))
            vws = []
            for u in range(U):
                vg = dve.value_load(tiles[0:1, ds(i * U + u, 1)], min_val=0, max_val=T - 1)
                vw = dve.value_load(windows[0:1, ds(i * U + u, 1)], min_val=0, max_val=path.windows)
                vws.append(vw)
                prev(dve, S.pe, f"step{u}")
                selected.append(S.dve.done(dve.scalar_tensor_tensor(
                    sel[:, u, :].rearrange("p (n b) -> p n b", b=nb),
                    iota[:, ds(vw * path.nodes, path.nodes)].rearrange("p (n b) -> p n b", b=1)
                    .to_broadcast([P, path.nodes, nb]),
                    dst_f[:, ds(vg, 1)],
                    co[:, :, ds(vg, 1)].rearrange("p b t -> p t b").to_broadcast([P, path.nodes, nb]),
                    ALU.is_equal, ALU.mult)))
            for u in range(U):
                wait(pe, gathered[u], selected[u])
                prev(pe, S.dve, f"added{u}")
                a = S.pe.done(pe.matmul(bank[u][:], sel[:, u, :], xs[:, u, :], start=True, stop=True), f"step{u}")
                wait(dve, a)
                if u == 0:
                    prev(dve, S.dve, f"added{U - 1}")
                else:
                    wait(dve, added)
                g = G[:, ds(vws[u], 1), :].rearrange("p w d -> p (w d)")
                added = S.dve.done(dve.tensor_tensor(g, g, bank[u][:], ALU.add), f"added{u}")
        S.meet()
        done = []
        per = P // path.nodes
        assert per == nb
        nbk = per // 4
        for n in range(NT * KC):
            j, k = divmod(n, KC)
            b0 = 4 + (n * nbk) % 4
            wait(pe, added, *([done[n - 4 // nbk]] if n >= 4 // nbk else []))
            for v in range(per):
                ins = pe.transpose(bank[b0 + v // 4][:, (v % 4) * P:(v % 4 + 1) * P],
                                   G[:, j * per + v, k * P:(k + 1) * P], ident[:])
            a = S.pe.done(ins)
            eng, tr = ((act, S.act), (dve, S.dve))[n % 2]
            wait(eng, a)
            for q in range(nbk):
                o = G[:, j * nb:(j + 1) * nb, k * P + q * 4 * path.nodes:k * P + (q + 1) * 4 * path.nodes]
                i_ = bank[b0 + q][:].rearrange("p (m b) -> p b m", b=nb)
                t = tr.done(act.copy(o, i_) if eng is act else dve.tensor_copy(o, i_))
            done.append(t)
        S.meet()
        return done[-2:]

    def basis_lhs(path, nb, G, b):
        return lambda k, j: G[:, j * nb + b, k * P:(k + 1) * P]

    def plain_lhs(xT):
        return lambda k, j: xT[:, k, j * P:(j + 1) * P]

    def transform(products, biases, ready, epilogue):
        ring = M.new("weight_ring", [P, 4, D])
        free = [None] * 4
        n, after = 0, list(ready)
        for half in range(2):
            js = range(half * HALF, (half + 1) * HALF)
            for lhs, weight in products:
                for k in range(KC):
                    s = n % 4
                    if free[s]:
                        wait(sp, free[s])
                    else:
                        wait(sp, *ready)
                    a = chunk_in[s].done(sp.dma_start(ring[:, s, :], weight[k * P:(k + 1) * P, :]))
                    wait(pe, a, *after)
                    after = []
                    for j in js:
                        ins = pe.matmul(bank[j % HALF][:], lhs(k, j), ring[:, s, :],
                                        start=k == 0 and lhs is products[0][0], stop=False)
                    free[s] = S.pe.done(ins)
                    n += 1
            for m, bias in enumerate(biases):
                wait(sp, *([free_row] if (half, m) != (0, 0) else ready))
                a = misc_in.done(sp.dma_start(brow[:], bias.rearrange("(a d) -> a d", a=1)))
                wait(pe, a)
                for j in js:
                    ins = pe.matmul(bank[j % HALF][:], ones[0:1, :], brow[:], start=False,
                                    stop=m == len(biases) - 1)
                free_row = S.pe.done(ins)
            after = epilogue(list(js), free_row)
            S.meet()
        return after

    rows_of = lambda r, j: r[j * P:(j + 1) * P, :]

    M.at = after_edges
    x = M.new("x", [P, NT, D])
    xT = M.new("xT", [P, KC, NP])
    keep0 = M.at
    wait(sp, count_out)
    x_loaded = x_in.done(sp.dma_start(x[:], A["x"].rearrange("(j p) d -> p j d", p=P)))
    G = M.new("G", [P, PATH0.windows + 1, D])
    xT_done = []
    wait(dve, count_out)
    wait(act, count_out)
    wait(pool, count_out)
    for j in range(NT):
        xT_done.append(transpose_tile(x[:, j, :], xT, j, 4 + j % 4, [x_loaded, ident_ready] +
                                      xT_done[max(0, j - 4):max(0, j - 3)]))
    GT_done = aggregate(PATH0, 4, coef["L0a"], A["x"], G, [sched_ready])
    h = M.new("h", [P, 2, D])
    hT = M.new("hT", [P, KC, NP])
    h_free = [None, None]
    h_stored, hT_done = [], []

    def hidden(js, ready):
        for j in js:
            s = j % 2
            wait(act, ready, *([h_free[s][0], h_free[s][1]] if h_free[s] else []))
            a = S.act.done(act.activation(h[:, s, :], bank[j % HALF][:], ACT.Relu))
            wait(sp, a)
            o = tile_out[s].done(sp.dma_start(rows_of(hidden_rows, j), h[:, s, :]))
            h_stored.append(o)
            t = transpose_tile(h[:, s, :], hT, j, 6 + s, [a] + (hT_done[-2:-1]))
            hT_done.append(t)
            h_free[s] = (o, t)
        return [a] + hT_done[-2:]

    loop_lhs = plain_lhs(xT)
    products = [(basis_lhs(PATH0, 4, G, b), A["L0_gnn_basis0"][b]) for b in range(4)]
    hid = transform(products + [(loop_lhs, A["L0_gnn_loop0"])], [A["L0_gnn_bias0"]], GT_done + xT_done[-2:], hidden)

    wait(dve, *hid)
    M.at = M.at
    GT_done = aggregate(PATH0, 4, coef["L0b"], hidden_rows, G, h_stored[-2:] + hid)
    x_stored = []

    def residual_norm(rows):
        def epilogue(js, ready):
            wait(dve, ready)
            for j in js:
                a = S.dve.done(dve.tensor_tensor(bank[j % HALF][:], bank[j % HALF][:], x[:, j, :], ALU.add))
            ts = normalize([bank[j % HALF][:] for j in js], [a], [x[:, j, :] for j in js])
            if rows is not None:
                for j, t in zip(js, ts):
                    wait(sp, t)
                    x_stored.append(tile_out[j % 2].done(sp.dma_start(rows_of(rows, j), x[:, j, :])))
            return ts
        return epilogue

    products = [(basis_lhs(PATH0, 4, G, b), A["L0_gnn_basis1"][b]) for b in range(4)]
    nrm = transform(products + [(plain_lhs(hT), A["L0_gnn_loop1"])], [A["L0_gnn_bias1"]], GT_done + hT_done[-2:],
                    residual_norm(x1_rows))

    M.at = after_edges
    S.meet()
    G = M.new("G1", [P, PATH1.windows + 1, D])
    keep1 = M.at
    GT_done = aggregate(PATH1, 8, coef["L1"], x1_rows, G, x_stored[-2:])
    M.at = keep1
    ring_at = M.at
    M.at = after_constants
    xt = M.new("x_tile", [P, 2, D])
    xn = M.new("x_new", [P, 2, D])
    assert M.at <= after_edges
    M.at = ring_at
    state = {"read": [None, None], "stored": [None, None]}
    x2_stored = []

    def layer1(js, ready):
        for j in js:
            s = j % 2
            wait(sp, *(GT_done + [S_last] if state["read"][s] is None else [state["read"][s]]))
            t = tile_in[s].done(sp.dma_start(xt[:, s, :], rows_of(x1_rows, j)))
            wait(dve, ready, t)
            state["read"][s] = S.dve.done(dve.tensor_tensor(bank[j % HALF][:], bank[j % HALF][:], xt[:, s, :], ALU.add))
        last = state["read"][js[-1] % 2]
        ts = []
        for pair in (js[0:2], js[2:4], js[4:5]):
            free = [state["stored"][j % 2] for j in pair if state["stored"][j % 2]]
            t2 = normalize([bank[j % HALF][:] for j in pair], [last], [xn[:, j % 2, :] for j in pair], free)
            for j, t in zip(pair, t2):
                wait(sp, t)
                state["stored"][j % 2] = tile_out[j % 2].done(sp.dma_start(rows_of(x2_rows, j), xn[:, j % 2, :]))
                x2_stored.append(state["stored"][j % 2])
            ts += t2
        return ts

    S_last = GT_done[-1]
    products = [(basis_lhs(PATH1, 8, G, b), A["L1_gnn_bases"][b]) for b in range(8)]
    fin1 = transform(products, [A["L1_gnn_h_bias"]], GT_done, layer1)

    M.at = after_constants
    S.meet()
    count = M.new("count2", [P, NT, NP + P])
    x = M.new("x_L2", [P, NT, D])
    keep2 = M.at
    xT = M.new("xT_L2", [P, KC, NP])
    aggT = M.new("aggT", [P, KC, NP])
    rdeg = M.new("rdeg", [P, NT])
    part = M.new("own_part", [P, HALF, D])
    c_in = misc_in.done(sp.dma_start(count[:].rearrange("p j n -> p (j n)"), count_rows))
    x_loaded = x_in.done(sp.dma_start(x[:], x2_rows.rearrange("(j p) d -> p j d", p=P)))
    xT_done = []
    for j in range(NT):
        xT_done.append(transpose_tile(x[:, j, :], xT, j, 4 + j % 4, [x_loaded] + xT_done[max(0, j - 4):max(0, j - 3)]))
    wait(pe, c_in)
    for j in range(NT):
        for i in range(NT):
            ins = pe.matmul(bank[0][:, j:j + 1], count[:, i, j * P:(j + 1) * P], ones[:, 0:1],
                            start=i == 0, stop=i == NT - 1)
    a = S.pe.done(ins)
    wait(dve, a)
    a = S.dve.done(dve.tensor_scalar(rdeg[:], bank[0][:, 0:NT], 1.0, None, ALU.max))
    wait(dve, a)
    rdeg_ready = S.dve.done(dve.reciprocal(rdeg[:], rdeg[:]))
    spans = [(c, min(512, NP - c)) for c in range(0, NP, 512)]
    free = {}
    n = 0
    for k in range(KC):
        for c, width in spans:
            b = 1 + n % 3
            if b in free:
                wait(pe, free[b])
            for i in range(NT):
                ins = pe.matmul(bank[b][:, 0:width], x[:, i, k * P:(k + 1) * P], count[:, i, c:c + width],
                                start=i == 0, stop=i == NT - 1)
            a = S.pe.done(ins)
            eng, tr = ((act, S.act), (dve, S.dve))[n % 2]
            wait(eng, a)
            o, i_ = aggT[:, k, c:c + width], bank[b][:, 0:width]
            free[b] = tr.done(act.copy(o, i_) if eng is act else dve.tensor_copy(o, i_))
            n += 1
    agg_done = list(free.values())
    part_ready = {}

    def own(js, ready):
        wait(act, ready, *( [part_free[0]] if part_free else []))
        for j in js:
            a = S.act.done(act.copy(part[:, j % HALF, :], bank[j % HALF][:]))
        return [a]

    ring = M.new("weight_ring2", [P, 2, KC, D])
    w1_in = [chunk_in[m].done(sp.dma_start(ring[:, m, :, :], A[name].rearrange("(k p) d -> p k d", p=P)))
             for m, name in enumerate(("L2_gnn_W1", "L2_gnn_W2"))]
    brows = M.new("bias_rows2", [1, 2, D])
    for m, name in enumerate(("L2_gnn_b1", "L2_gnn_b2")):
        b_in = misc_in.done(sp.dma_start(brows[:, m, :], A[name].rearrange("(a d) -> a d", a=1)))
    wait(pe, *w1_in, b_in, rdeg_ready, *agg_done, *xT_done[-2:])
    wait(dve, rdeg_ready)
    last_ln = []
    for half in range(2):
        js = list(range(half * HALF, (half + 1) * HALF))
        wait(pe, *last_ln)
        for j in js:
            for k in range(KC):
                pe.matmul(bank[j % HALF][:], xT[:, k, j * P:(j + 1) * P], ring[:, 0, k, :], start=k == 0, stop=False)
            for m in range(2):
                ins = pe.matmul(bank[j % HALF][:], ones[0:1, :], brows[:, m, :], start=False, stop=m == 1)
        a = S.pe.done(ins)
        wait(dve, a)
        for j in js:
            t = S.dve.done(dve.tensor_tensor(x[:, j, :], x[:, j, :], bank[j % HALF][:], ALU.add))
        for n_, j in enumerate(js):
            b = 5 + n_ % 3
            if n_ >= 3:
                wait(pe, scaled[n_ - 3])
            else:
                scaled = scaled if n_ else []
            for k in range(KC):
                ins = pe.matmul(bank[b][:], aggT[:, k, j * P:(j + 1) * P], ring[:, 1, k, :],
                                start=k == 0, stop=k == KC - 1)
            a = S.pe.done(ins)
            wait(dve, a, t)
            scaled.append(S.dve.done(dve.scalar_tensor_tensor(
                x[:, j, :], bank[b][:], rdeg[:, j:j + 1], x[:, j, :], ALU.mult, ALU.add)))
        last_ln = normalize([x[:, j, :] for j in js], scaled, [x[:, j, :] for j in js])

    M.at = keep2
    S.meet()
    lay3(nc, A, out, S, M, bank, count, x, ident, ones, stat, mv, rstd, after_constants, brow,
         head_in, block_in, misc_in, out_done, last_ln, transpose_tile, normalize)


def lay3(nc, A, out, S, M, bank, count, x, ident, ones, stat, mv, rstd, after_constants, brow,
         head_in, block_in, misc_in, out_done, last_ln, transpose_tile, normalize):
    wait, prev = S.wait, S.wait_previous
    pe, act, dve, pool, sp = nc.tensor, nc.scalar, nc.vector, nc.gpsimd, nc.sync
    scale = DH ** -0.5
    spans = [(c, min(512, NP - c)) for c in range(0, NP, 512)]
    seen = [(c, min(512, N - c)) for c in range(0, N, 512)]
    xin = M.new("x_start", [P, NT, D])
    start = M.at

    tmp = M.new("tmp", [P, N])
    keep = S.dve.done(dve.tensor_copy(xin[:], x[:]))
    prior = keep
    for j in range(NT):
        c = count[:, j, 0:N]
        wait(dve, prior)
        a = S.dve.done(dve.tensor_scalar(tmp[:], c, 1.0, 1.0, ALU.min, ALU.subtract))
        b = S.dve.done(dve.tensor_scalar(c, c, 1.0, None, ALU.max))
        wait(act, b)
        b = S.act.done(act.activation(c, c, ACT.Ln))
        wait(dve, a, b)
        prior = S.dve.done(dve.scalar_tensor_tensor(c, tmp[:], NEG, c, ALU.mult, ALU.add))
    mask_ready = prior

    M.at = start
    condT = M.new("condT", [COND + 1, NP])
    cond_end = M.at
    ang = M.new("angle", [2 * FREQ, NP])
    turn = M.new("turn", [2 * FREQ, NP])
    emb = M.new("embT", [2 * FREQ, NP])
    kf = M.new("k_float", [2 * FREQ, 1])
    ki = M.new("k_int", [2 * FREQ, 1], I32)
    quarter = M.new("quarter", [2 * FREQ, 1])
    fw1 = M.new("f_w1", [2 * FREQ, COND])
    fw2 = M.new("f_w2", [COND, COND])
    fb = M.new("f_b", [COND, 2])
    hid = M.new("cond_hidden", [COND, NP])
    sig = M.new("cond_sigmoid", [COND, NP])
    wait(pool, mask_ready)
    wait(sp, mask_ready)
    for h in range(2):
        a = S.pool.done(pool.iota(ki[h * FREQ:(h + 1) * FREQ, :], pattern=[[0, 1]], base=1, channel_multiplier=1))
    node = A["node_vec1"]
    misc_in.done(sp.dma_start(ang[:], bass.AP(tensor=node.tensor, offset=node.offset, ap=[[0, 2 * FREQ], [1, NP]])))
    misc_in.done(sp.dma_start(fw1[:], A["L3_gnn_f_w1"]))
    misc_in.done(sp.dma_start(fw2[:], A["L3_gnn_f_w2"]))
    misc_in.done(sp.dma_start(fb[:, 0:1], A["L3_gnn_f_b1"].rearrange("(c a) -> c a", a=1)))
    t = misc_in.done(sp.dma_start(fb[:, 1:2], A["L3_gnn_f_b2"].rearrange("(c a) -> c a", a=1)))
    wait(dve, a, t)
    a = S.dve.done(dve.tensor_copy(kf[:], ki[:]))
    b = S.dve.done(dve.memset(quarter[0:FREQ, :], 0.0))
    b = S.dve.done(dve.memset(quarter[FREQ:2 * FREQ, :], 0.25))
    one = S.dve.done(dve.memset(condT[:], 1.0))
    wait(dve, a, b, one)
    a = S.dve.done(dve.tensor_scalar(kf[:], kf[:], 1.0 / 16, None, ALU.mult))
    wait(dve, a)
    a = S.dve.done(dve.tensor_scalar(ang[:], ang[:], kf[:], quarter[:], ALU.mult, ALU.add))
    wait(dve, a)
    magic = 1.5 * 2.0 ** 23
    a = S.dve.done(dve.tensor_scalar(turn[:], ang[:], magic, None, ALU.add))
    wait(dve, a)
    a = S.dve.done(dve.tensor_scalar(turn[:], turn[:], magic, None, ALU.subtract))
    wait(dve, a)
    a = S.dve.done(dve.tensor_tensor(ang[:], ang[:], turn[:], ALU.subtract))
    wait(act, a)
    emb_ready = S.act.done(act.activation(emb[:], ang[:], ACT.Sin, scale=6.283185))
    wait(pe, emb_ready, one)
    for m, (wt, src, K) in enumerate(((fw1, emb, 2 * FREQ), (fw2, hid, COND))):
        for n, (c, width) in enumerate(spans):
            ins = pe.matmul(bank[n][0:COND, 0:width], wt[:], src[:, c:c + width], start=True, stop=True)
        a = S.pe.done(ins)
        wait(act, a)
        dst = hid if m == 0 else condT[0:COND, :]
        for n, (c, width) in enumerate(spans):
            t = S.act.done(act.activation(dst[:, c:c + width], bank[n][0:COND, 0:width], ACT.Identity,
                                          bias=fb[:, m:m + 1]))
        if m == 0:
            wait(act, t)
            t = S.act.done(act.activation(sig[:], hid[:], ACT.Exp, scale=-1.0))
            wait(dve, t)
            a = S.dve.done(dve.tensor_scalar(sig[:], sig[:], 1.0, None, ALU.add))
            wait(dve, a)
            a = S.dve.done(dve.reciprocal(sig[:], sig[:]))
            wait(dve, a)
            t = S.dve.done(dve.tensor_tensor(hid[:], hid[:], sig[:], ALU.mult))
        wait(pe, t)
    cond_ready = t

    S.meet()
    M.at = cond_end
    yT = M.new("yT", [P, KC, NP])
    attnT = M.new("attnT", [P, HEADS, NP])
    big = M.new("block_weight", [P, KC, D])
    modw = M.new("modulation_weights", [COND + 1, 2, D])
    brow2 = M.new("block_bias_row", [1, D])
    hb = M.new("head_bias_cols", [P, 2])
    mb = M.new("mlp_bias_cols", [P, KC])
    y = M.new("y_tile", [P, 2, D])
    hw = M.new("head_weights", [P, 3, KC, DH])
    vrow = M.new("v_bias_row", [1, DH])
    qT, kT = M.new("qT", [P, NP]), M.new("kT", [P, NP])
    v = M.new("v", [P, NT, DH])
    prob = M.new("prob", [P, 2, N])
    PT = M.new("probT", [P, NT, P])
    rmax = M.new("row_max", [P, 2])
    rsum = M.new("row_sum", [P, 2])
    has = M.new("has_edges", [P, 2])
    S.meet()

    def modulate(i, names, ready):
        sw, sb, bw, bb = (A["L3_gnn_" + n] for n in names)
        wait(sp, *ready)
        for m, (wt, bs) in enumerate(((sw, sb), (bw, bb))):
            block_in.done(sp.dma_start(modw[0:COND, m, :], wt[ds(i, 1), :, :].rearrange("a c d -> (a c) d")))
            t = block_in.done(sp.dma_start(modw[COND:COND + 1, m, :], bs[ds(i, 1), :]))
        wait(pe, t, *ready)
        free, y_free, last = {}, [None, None], []
        for half in range(2):
            js = list(range(half * HALF, (half + 1) * HALF))
            nx = [attnT[:, :, :].rearrange("p h n -> p (h n)")[:, j * D:(j + 1) * D] for j in js]
            nd = normalize([x[:, j, :] for j in js], ready, nx)
            for j, xn, t in zip(js, nx, nd):
                s = j % 2
                if s in free:
                    wait(pe, free[s])
                for m in range(2):
                    ins = pe.matmul(bank[2 * s + m][:], condT[:, j * P:(j + 1) * P], modw[:, m, :],
                                    start=True, stop=True)
                a = S.pe.done(ins)
                wait(dve, a, t, *([y_free[s]] if y_free[s] else []))
                a = S.dve.done(dve.scalar_tensor_tensor(y[:, s, :], bank[2 * s][:], 1.0, xn, ALU.add, ALU.mult))
                wait(dve, a)
                a = S.dve.done(dve.tensor_tensor(y[:, s, :], y[:, s, :], bank[2 * s + 1][:], ALU.add))
                free[s] = a
                y_free[s] = transpose_tile(y[:, s, :], yT, j, 4 + s, [a] + last[-2:-1])
                last.append(y_free[s])
        return last[-2:] + [free[0], free[1]]

    def add_product(i, lhs, weight, bias, ready):
        wait(sp, *ready)
        block_in.done(sp.dma_start(big[:], weight[ds(i, 1), :, :].rearrange("a (k p) d -> p (a k) d", p=P)))
        t = block_in.done(sp.dma_start(brow2[:], bias[ds(i, 1), :]))
        wait(pe, t, *ready)
        done = []
        for j in range(NT):
            b = j % 4
            if j >= 4:
                wait(pe, done[j - 4])
            for k in range(KC):
                pe.matmul(bank[b][:], lhs[:, k, j * P:(j + 1) * P], big[:, k, :], start=k == 0, stop=False)
            a = S.pe.done(pe.matmul(bank[b][:], ones[0:1, :], brow2[:], start=False, stop=True))
            wait(dve, a)
            done.append(S.dve.done(dve.tensor_tensor(x[:, j, :], x[:, j, :], bank[b][:], ALU.add)))
        return [done[-1]]

    with S.loop(BLOCKS) as i:
        y_ready = modulate(i, ("s1_w", "s1_b", "b1_w", "b1_b"), [])
        S.meet()
        with S.loop(HEADS) as h:
            prev(sp, S.act, "attended")
            for m, (wn, bn) in enumerate((("wq", "bq"), ("wk", "bk"), ("wv", "bv"))):
                wt = A["L3_gnn_" + wn][ds(i, 1), :, ds(h * DH, DH)].rearrange("a (k p) d -> p (a k) d", p=P)
                head_in.done(sp.dma_start(hw[:, m, :, :], wt))
                bs = A["L3_gnn_" + bn][ds(i, 1), ds(h * DH, DH)]
                t = head_in.done(sp.dma_start(vrow[:] if m == 2 else hb[:, m:m + 1],
                                              bs if m == 2 else bs.rearrange("a d -> d a"),
                                              allow_slow_non_contiguous=True))
            wait(dve, t)
            a = S.dve.done(dve.tensor_scalar(hb[:, 0:1], hb[:, 0:1], scale, None, ALU.mult))
            wait(pe, t)
            prev(pe, S.act, "attended")
            prev(act, S.pe, "values")
            wait(act, a, t)
            n, free = 0, {}
            for m, (dst, sc) in enumerate(((qT, scale), (kT, 1.0))):
                for c, width in spans:
                    b = n % 4
                    if b in free:
                        wait(pe, free[b])
                    for k in range(KC):
                        ins = pe.matmul(bank[b][:, 0:width], hw[:, m, k, :], yT[:, k, c:c + width],
                                        start=k == 0, stop=k == KC - 1)
                    a = S.pe.done(ins)
                    wait(act, a)
                    free[b] = S.act.done(act.activation(dst[:, c:c + width], bank[b][:, 0:width], ACT.Identity,
                                                        bias=hb[:, m:m + 1], scale=sc))
                    n += 1
            for j in range(NT):
                b = n % 4
                wait(pe, free[b])
                for k in range(KC):
                    pe.matmul(bank[b][:, 0:DH], yT[:, k, j * P:(j + 1) * P], hw[:, 2, k, :], start=k == 0, stop=False)
                a = S.pe.done(pe.matmul(bank[b][:, 0:DH], ones[0:1, :], vrow[:], start=False, stop=True))
                wait(act, a)
                free[b] = S.act.done(act.copy(v[:, j, :], bank[b][:, 0:DH]))
                n += 1
            wait(pe, *free.values())

            def scores(j):
                for n_, (c, width) in enumerate(seen):
                    ins = pe.matmul(bank[n_][:, 0:width], qT[:, j * P:(j + 1) * P], kT[:, c:c + width],
                                    start=True, stop=True)
                return S.pe.done(ins)

            scored = scores(0)
            pt_free = None
            for j in range(NT):
                s = j % 2
                wait(dve, scored, *([moved[j - 2]] if j >= 2 else []))
                if j < 2:
                    prev(dve, S.pe, "values")
                for n_, (c, width) in enumerate(seen):
                    a = S.dve.done(dve.tensor_tensor(prob[:, s, c:c + width], bank[n_][:, 0:width],
                                                     count[:, j, c:c + width], ALU.add))
                wait(pe, a)
                if j + 1 < NT:
                    scored = scores(j + 1)
                wait(dve, a)
                a = S.dve.done(dve.reduce_max(rmax[:, s:s + 1], prob[:, s, :], AX.X))
                wait(dve, a)
                S.dve.done(dve.tensor_scalar(has[:, s:s + 1], rmax[:, s:s + 1], -0.5 * NEG, None, ALU.is_gt))
                a = S.dve.done(dve.tensor_scalar(rmax[:, s:s + 1], rmax[:, s:s + 1], -1.0, None, ALU.mult))
                wait(act, a)
                a = S.act.done(act.activation(prob[:, s, :], prob[:, s, :], ACT.Exp, bias=rmax[:, s:s + 1],
                                              accum_out=rsum[:, s:s + 1]))
                wait(dve, a)
                a = S.dve.done(dve.reciprocal(rsum[:, s:s + 1], rsum[:, s:s + 1]))
                wait(dve, a)
                a = S.dve.done(dve.tensor_tensor(rsum[:, s:s + 1], rsum[:, s:s + 1], has[:, s:s + 1], ALU.mult))
                wait(dve, a)
                a = S.dve.done(dve.tensor_scalar(prob[:, s, :], prob[:, s, :], rsum[:, s:s + 1], None, ALU.mult))
                wait(pe, a)
                if j == 0:
                    moved = []
                else:
                    wait(pe, pt_moved)
                for q in range(NT):
                    width = min(P, N - q * P)
                    ins = pe.transpose(bank[3 + q // 4][0:width, (q % 4) * P:(q % 4 + 1) * P],
                                       prob[:, s, q * P:q * P + width], ident[:])
                a = S.pe.done(ins)
                moved.append(a)
                wait(act, a, *([pt_free] if pt_free else []))
                if j == 0:
                    prev(act, S.pe, "values")
                for g, w_ in ((0, 4), (1, 4), (2, 1)):
                    S.act.done(act.copy(PT[:, 4 * g:4 * g + w_, :],
                                        bank[3 + g][:, 0:w_ * P].rearrange("p (q n) -> p q n", n=P)))
                w_ = N - (NT - 1) * P
                pt_moved = S.act.done(act.copy(PT[0:w_, NT - 1, :], bank[5][0:w_, P:2 * P]))
                wait(pe, pt_moved)
                b = 6 + s
                if j >= 2:
                    wait(pe, o_free[s])
                elif j == 0:
                    o_free = {}
                for q in range(NT):
                    width = min(P, N - q * P)
                    ins = pe.matmul(bank[b][:, 0:P], v[0:width, q, :], PT[0:width, q, :],
                                    start=q == 0, stop=q == NT - 1)
                pt_free = S.pe.done(ins, "values")
                wait(act, pt_free)
                o_free[s] = S.act.done(act.copy(attnT[:, ds(h, 1), j * P:(j + 1) * P].rearrange("p a n -> p (a n)"),
                                                bank[b][:, 0:P]), "attended")
        S.meet()
        a = add_product(i, attnT, A["L3_gnn_wo"], A["L3_gnn_bo"], [])
        y_ready = modulate(i, ("s2_w", "s2_b", "b2_w", "b2_b"), a)
        wait(sp, *y_ready)
        block_in.done(sp.dma_start(big[:], A["L3_gnn_m_w1"][ds(i, 1), :, :].rearrange("a (k p) d -> p (a k) d", p=P)))
        t = block_in.done(sp.dma_start(mb[:], A["L3_gnn_m_b1"][ds(i, 1), :].rearrange("a (k p) -> p (a k)", p=P),
                                       allow_slow_non_contiguous=True))
        wait(pe, t, *y_ready)
        wait(act, t, *y_ready)
        n, free = 0, {}
        for o in range(KC):
            for c, width in spans:
                b = n % 4
                if b in free:
                    wait(pe, free[b])
                for k in range(KC):
                    ins = pe.matmul(bank[b][:, 0:width], big[:, k, o * P:(o + 1) * P], yT[:, k, c:c + width],
                                    start=k == 0, stop=k == KC - 1)
                a = S.pe.done(ins)
                wait(act, a)
                free[b] = S.act.done(act.activation(attnT[:, o, c:c + width], bank[b][:, 0:width], ACT.Relu,
                                                    bias=mb[:, o:o + 1]))
                n += 1
        a = add_product(i, attnT, A["L3_gnn_m_w2"], A["L3_gnn_m_b2"], list(free.values()))
        S.meet()

    wait(dve, Token(S.dve, "top", S.dve.base, S.dve.off))
    a = S.dve.done(dve.tensor_tensor(x[:], x[:], xin[:], ALU.add))
    for half in range(2):
        js = list(range(half * HALF, (half + 1) * HALF))
        for j, t in zip(js, normalize([x[:, j, :] for j in js], [a], [x[:, j, :] for j in js])):
            rows = min(P, N - j * P)
            wait(sp, t)
            o = out_done.done(sp.dma_start(out[j * P:j * P + rows, :], x[0:rows, j, :]))
            a = t
    wait(sp, o)


EDGE_INPUTS = ("src", "dst", "edge_type_8", "edge_type_32", "edge_weight", "edge_weight1")


def kernel(**inputs):
    import numpy as np
    import concourse.bacc as bacc
    from concourse.bass_utils import run_bass_kernel_spmd

    arrays = {}
    for name, a in inputs.items():
        a = np.ascontiguousarray(a)
        if name in EDGE_INPUTS:
            flat = np.full(T * P, PAD_DST if name == "dst" else 0, a.dtype)
            flat[:E] = a.reshape(-1)
            if name == "dst":
                arrays["dst_flat"] = flat
            a = np.ascontiguousarray(flat.reshape(T, P).T)
        elif name in ("x", "node_vec1"):
            padded = np.zeros((NP, a.shape[1]), a.dtype)
            padded[:N] = a
            a = padded.reshape(-1) if name == "node_vec1" else padded
        elif name in ("L2_gnn_W1", "L2_gnn_W2"):
            a = np.ascontiguousarray(a.T)
        arrays[name] = a

    counts = {}
    for final in (False, True):
        nc = bacc.Bacc("TRN2", target_bir_lowering=False, num_devices=1)
        A = {n: nc.dram_tensor(f"in_{n}", a.shape, mybir.dt.from_np(a.dtype), kind="ExternalInput").ap()
             for n, a in arrays.items()}
        out = nc.dram_tensor("out_x", (N, D), F32, kind="ExternalOutput").ap()
        build(nc, A, out, counts)
    r = run_bass_kernel_spmd(nc, [{f"in_{n}": a for n, a in arrays.items()}], core_ids=[0])
    return r.results[0]["out_x"]
```

```python
import concourse.bass as bass
from concourse import mybir

F32, I32, BF16, F16 = mybir.dt.float32, mybir.dt.int32, mybir.dt.bfloat16, mybir.dt.float16
ALU = mybir.AluOpType
ACT = mybir.ActivationFunctionType
AX = mybir.AxisListType
ds = bass.ds
ACTE, DVE = mybir.EngineType.Activation, mybir.EngineType.DVE

P = 128
N = 1250
NT = -(-N // P)
NP = NT * P
D = 512
KC = D // P
E = 21250
T = -(-E // (4 * P)) * 4
PAD_DST = NP - 1
HEADS, BLOCKS = 4, 4
DH = D // HEADS
HALF = NT // 2
EPS = 1e-5
NEG = 1e30
FREQ, COND = 32, 16
SPANS = [(c, min(512, NP - c)) for c in range(0, NP, 512)]


class Path:

    def __init__(self, shift, unroll, tiles=1):
        self.shift, self.nodes, self.tiles = shift, 1 << shift, tiles
        self.unroll = unroll
        self.windows = NP >> shift
        self.groups = T // tiles
        self.steps = -(-(self.groups + self.windows - 1) // unroll) * unroll
        assert self.steps - self.groups <= self.windows


PATH0, PATH1, PATHC = Path(5, 8), Path(4, 8), Path(7, 2, 4)


class Token:

    def __init__(self, track, frame, base, off):
        self.track, self.frame, self.base, self.off = track, frame, base, off


class Track:

    def __init__(self, sync, name, unit):
        self.sync, self.name, self.unit = sync, name, unit
        self.sem = sync.nc.alloc_semaphore(name)
        self.base, self.off = 0, 0
        sync.tracks.append(self)

    def prime(self, engine, n):
        engine.sem_inc(self.sem, n)
        self.off += n

    def done(self, instruction, label=None):
        instruction.then_inc(self.sem, self.unit)
        self.off += self.unit
        frame = self.sync.frames[-1]
        if label is not None:
            self.sync.marks[frame, self.name, label] = self.off
        return Token(self, frame, self.base, self.off)


class Sync:

    def __init__(self, nc, counts):
        self.nc, self.counts, self.tracks = nc, counts, []
        self.frames, self.marks, self.waited, self.loops = ["top"], {}, {}, 0
        self.idle = nc.alloc_semaphore("idle")
        self.pe, self.act = Track(self, "pe_done", 1), Track(self, "act_done", 1)
        self.dve, self.pool = Track(self, "dve_done", 1), Track(self, "pool_done", 1)

    def wait(self, engine, *tokens):
        for t in tokens:
            key = (id(engine), t.track.name, t.frame, self.frames[-1])
            if self.waited.get(key, -1) < t.off:
                self.waited[key] = t.off
                self.wait_value(engine, t.track.sem, t.base + t.off)

    def wait_value(self, engine, sem, value):
        engine.wait_ge(sem, value)
        if not isinstance(value, int):
            engine.sem_inc(self.idle, 1)

    def wait_previous(self, engine, track, label):
        frame = self.frames[-1]
        per = self.counts.get(("per", frame, track.name), 1)
        mark = self.counts.get(("mark", frame, track.name, label), 1)
        self.wait_value(engine, track.sem, track.base + (mark - per))

    def meet(self):
        for engine in (self.nc.tensor, self.nc.scalar, self.nc.vector, self.nc.gpsimd, self.nc.sync):
            for t in self.tracks:
                if t.off:
                    self.wait(engine, Token(t, self.frames[-1], t.base, t.off))

    def loop(self, trips):
        return _Loop(self, trips)


class _Loop:
    def __init__(self, sync, trips):
        self.sync, self.trips = sync, trips

    def __enter__(self):
        s = self.sync
        s.loops += 1
        self.frame = f"loop{s.loops}"
        self.fori = s.nc.Fori(0, self.trips)
        i = self.fori.__enter__()
        s.frames.append(self.frame)
        self.saved = [(t, t.base, t.off) for t in s.tracks]
        for t in s.tracks:
            per = s.counts.get(("per", self.frame, t.name), 0)
            t.base = (t.base + t.off) + i * per if per else t.base + t.off
            t.off = 0
        return i

    def __exit__(self, *exc):
        s = self.sync
        known = {t for t, _, _ in self.saved}
        for t, base, off in self.saved:
            s.counts["per", self.frame, t.name] = t.off
            t.base, t.off = base, off + self.trips * t.off
        for (frame, name, label), off in s.marks.items():
            s.counts["mark", frame, name, label] = off
        assert all(t in known for t in s.tracks), "make tracks outside loops"
        s.frames.pop()
        return self.fori.__exit__(*exc)


class Arena:

    def __init__(self, nc):
        self.nc, self.at, self.n = nc, -(-nc.sbuf_base // 64) * 64, 0
        self.end = nc.sbuf_usable_end

    def new(self, name, shape, dtype=F32):
        size = mybir.dt.size(dtype)
        for d in shape[1:]:
            size *= d
        self.n += 1
        t = self.nc.alloc_sbuf_tensor_at(f"{name}_{self.n}", shape, dtype, offset=self.at)
        self.at += -(-size // 32) * 32
        assert self.at <= self.end, (name, self.at, self.end)
        return t


def build(nc, A, out, counts):
    S = Sync(nc, counts)
    wait, prev = S.wait, S.wait_previous
    pe, act, dve, pool, sp = nc.tensor, nc.scalar, nc.vector, nc.gpsimd, nc.sync
    S.pe.prime(pe, 32)
    M = Arena(nc)
    gather_in = [Track(S, f"gather{u}_in", 16) for u in range(PATH0.unroll)]
    chunk_in = [Track(S, f"weight_chunk{u}_in", 16) for u in range(4)]
    tile_in = [Track(S, f"tile{u}_in", 16) for u in range(2)]
    tile_out = [Track(S, f"tile{u}_out", 16) for u in range(2)]
    head_in = Track(S, "head_weights_in", 16)
    block_in = Track(S, "block_weights_in", 16)
    misc_in = Track(S, "misc_in", 16)
    x_in = Track(S, "x_in", 16)
    out_done = Track(S, "out_done", 16)

    bank = [nc.alloc_psum_tensor(f"bank{b}", [P, 512], F32) for b in range(8)]

    hidden_rows = nc.dram_tensor("hidden_rows", (NP, D), F32, kind="Internal").ap()
    x1_rows = nc.dram_tensor("x1_rows", (NP, D), F32, kind="Internal").ap()
    x2_rows = nc.dram_tensor("x2_rows", (NP, D), F32, kind="Internal").ap()

    ident = M.new("ident", [P, P])
    ones = M.new("ones", [P, P])
    sched = {p: M.new("tile_of_step", [1, p.steps], I32) for p in (PATH0, PATH1, PATHC)}
    brow = M.new("bias_row", [1, D])
    stat = M.new("ln_stats", [P, HALF, 6])
    mv = M.new("ln_mean_var", [P, HALF, 2])
    rstd = M.new("ln_rstd", [P, HALF, 1])
    after_constants = M.at
    iota = M.new("node_iota", [P, NP + P])
    src_i = M.new("src_index", [P, T], I32)
    src_f = M.new("src_float", [P, T])
    dst_f = M.new("dst_float", [P, T])
    coef = {"L1": M.new("coef_L1", [P, 8, T])}
    after_layer1_edges = M.at
    coef |= {"L0a": M.new("coef_L0a", [P, 4, T]), "L0b": M.new("coef_L0b", [P, 4, T])}
    et_f = M.new("types_float", [P, 2, T])
    w = M.new("weights", [P, 2, T])
    comp = M.new("comp", [P, 8 * 4 * 2 + 32 * 8])
    mask = M.new("relation_mask", [P, 2, T])
    after_edges = M.at

    c0 = S.dve.done(dve.memset(ident[:], 0.0))
    c1 = S.dve.done(dve.memset(ones[:], 1.0))
    wait(pool, c0)
    ident_ready = S.pool.done(pool.affine_select(
        out=ident[:], in_=ident[:], compare_op=ALU.not_equal, fill=1.0, base=0, pattern=[[-1, P]],
        channel_multiplier=1))
    iota_i = M.new("iota_int", [P, NP + P], I32)
    k1 = S.pool.done(pool.iota(iota_i[:], pattern=[[1, NP + P]], base=0, channel_multiplier=0))
    wait(dve, k1)
    iota_ready = S.dve.done(dve.tensor_copy(iota[:], iota_i[:]))

    dst_i = M.new("dst_int", [P, T], I32)
    et = M.new("types_int", [P, 2, T], I32)
    last_i = M.new("last_dst", [P, 2], I32)
    for d, s in ((src_i[:], A["src"]), (dst_i[:], A["dst"]), (et[:, 0, :], A["edge_type_8"]),
                 (et[:, 1, :], A["edge_type_32"]), (w[:, 0, :], A["edge_weight"]),
                 (w[:, 1, :], A["edge_weight1"])):
        t = S_in = misc_in.done(sp.dma_start(d, s))
    at = 0
    for name, n in (("L0_gnn_comp0", 32), ("L0_gnn_comp1", 32), ("L1_gnn_w_comp", 256)):
        row = A[name].rearrange("r b -> (r b)").rearrange("(a n) -> a n", a=1)
        t = misc_in.done(sp.dma_start(comp[:, at:at + n], bass.AP(
            tensor=row.tensor, offset=row.offset, ap=[[0, P], [1, n]])))
        at += n
    edges_in = t
    wait(dve, edges_in)
    S.dve.done(dve.tensor_copy(src_f[:], src_i[:]))
    S.dve.done(dve.tensor_copy(dst_f[:], dst_i[:]))
    et_ready = S.dve.done(dve.tensor_copy(et_f[:], et[:]))
    wait(dve, et_ready)


    def coefficients(kind, relations, outs):
        first = [S.dve.done(dve.memset(o[:], 0.0)) for o, _, _ in outs]
        wait(dve, *first)
        for r in range(relations):
            m = S.dve.done(dve.scalar_tensor_tensor(mask[:, r % 2, :], et_f[:, kind, :], float(r),
                                                    w[:, kind, :], ALU.is_equal, ALU.mult))
            wait(dve, m)
            for o, table, nb in outs:
                for b in range(nb):
                    at = table + r * nb + b
                    t = S.dve.done(dve.scalar_tensor_tensor(o[:, b, :], mask[:, r % 2, :], comp[:, at:at + 1],
                                                            o[:, b, :], ALU.mult, ALU.add))
        return t

    wait(dve, coefficients(0, 8, [(coef["L0a"], 0, 4), (coef["L0b"], 32, 4)]))

    def layer1_coefficients():
        coefficients(1, 32, [(coef["L1"], 64, 8)])

    for n, path in enumerate((PATH0, PATH1, PATHC)):
        G, span = path.groups, path.tiles * P
        last = M.new("last", [P, 2], I32)
        key = M.new("key", [P, 2])
        hit = M.new("hit", [P, 2, path.steps])
        tf = M.new("tf", [1, path.steps])
        clear = S.dve.done(dve.memset(last[:], 0))
        wait(sp, clear)
        flat = A["dst_flat"].rearrange("(g s) -> g s", s=span)
        for c in range(-(-G // P)):
            rows = min(P, G - c * P)
            t = misc_in.done(sp.dma_start(last[0:rows, c:c + 1], flat[c * P:c * P + rows, span - 1:span],
                                       allow_slow_non_contiguous=True))
        wait(dve, t)
        a = S.dve.done(dve.tensor_single_scalar(last[:], last[:], path.shift, ALU.arith_shift_right))
        wait(dve, a)
        a = S.dve.done(dve.tensor_copy(key[:], last[:]))
        gi = M.new("gi", [P, 2], I32)
        gf = M.new("gf", [P, 2])
        b = S.pool.done(pool.iota(gi[:], pattern=[[P, 2]], base=0, channel_multiplier=1))
        wait(dve, a, b)
        b = S.dve.done(dve.tensor_copy(gf[:], gi[:]))
        wait(dve, b)
        a = S.dve.done(dve.tensor_tensor(key[:], key[:], gf[:], ALU.add))
        wait(dve, a, iota_ready)
        for c in range(-(-G // P)):
            rows = min(P, G - c * P)
            a = S.dve.done(dve.tensor_scalar(hit[0:rows, c, :], iota[0:rows, 0:path.steps], key[0:rows, c:c + 1],
                                             None, ALU.is_gt))
        wait(pe, a, c1)
        for c in range(-(-G // P)):
            rows = min(P, G - c * P)
            ins = pe.matmul(bank[n][0:1, 0:path.steps], ones[0:rows, 0:1], hit[0:rows, c, :],
                            start=c == 0, stop=c == -(-G // P) - 1)
        a = S.pe.done(ins)
        wait(dve, a)
        a = S.dve.done(dve.tensor_scalar(tf[:], bank[n][0:1, 0:path.steps], float(G - 1), None, ALU.min))
        wait(dve, a)
        sched_ready = S.dve.done(dve.tensor_copy(sched[path][:], tf[:]))

    M.at = after_edges

    def tiles_of_steps(engine, path, i):
        n = path.unroll
        return nc.values_load_multi_w_load_instructions(
            sched[path][0:1, ds(i * n, n)], engines=[engine], min_val=0, max_val=path.groups - 1)[1]

    def window_of_step(path, i, u, tile):
        return nc.snap(i * path.unroll + u - tile, engines=[DVE], min_val=0, max_val=path.windows)

    count_rows = nc.dram_tensor("count_rows", (P, NT * NP), F32, kind="Internal").ap()

    class CountSteps:
        def __init__(self):
            self.count = M.new("count", [P, NT + 1, NP])
            self.oh_src = M.new("onehot_src", [P, PATHC.tiles, NP], BF16)
            self.oh_dst = M.new("onehot_dst", [P, PATHC.tiles, P], BF16)
            self.iota16 = M.new("node_iota_16bit", [P, NP + P], F16)
            S.dve.done(dve.tensor_copy(self.iota16[:], iota[:]))
            S.pool.done(pool.memset(self.count[:], 0.0))

        def registers(self, i):
            self.groups = tiles_of_steps(DVE, PATHC, i)
            self.windows = [window_of_step(PATHC, i, u, g) for u, g in enumerate(self.groups)]

        def step(self, u):
            nt, vg, vw = PATHC.tiles, self.groups[u], self.windows[u]
            if u == 0:
                prev(dve, S.pe, "counted")
            else:
                wait(dve, self.counted)
            for q in range(nt):
                edge = vg * nt + q
                S.dve.done(dve.tensor_scalar(self.oh_src[:, q, :], self.iota16[:, 0:NP], src_f[:, ds(edge, 1)],
                                             None, ALU.is_equal))
                made = S.dve.done(dve.tensor_scalar(self.oh_dst[:, q, :], self.iota16[:, ds(vw * P, P)],
                                                    dst_f[:, ds(edge, 1)], None, ALU.is_equal))
            if u == 0:
                prev(pe, S.dve, "count_added")
            wait(pe, made)
            for n_, (c, width) in enumerate(SPANS):
                for q in range(nt):
                    ins = pe.matmul(bank[4 + n_][:, 0:width], self.oh_dst[:, q, :], self.oh_src[:, q, c:c + width],
                                    start=q == 0, stop=q == nt - 1)
            self.counted = S.pe.done(ins, "counted")

        def add(self, u):
            vw = self.windows[u]
            wait(dve, self.counted)
            if u == 0:
                prev(dve, S.dve, "count_added")
            else:
                wait(dve, self.added)
            for n_, (c, width) in enumerate(SPANS):
                dst = self.count[:, ds(vw, 1), c:c + width].rearrange("p a n -> p (a n)")
                self.added = S.dve.done(dve.tensor_tensor(dst, dst, bank[4 + n_][:, 0:width], ALU.add),
                                        "count_added")

    def transpose_tile(src, dstT, j, b, ready, after=()):
        wait(pe, *ready)
        for k in range(KC):
            ins = pe.transpose(bank[b][:, k * P:(k + 1) * P], src[:, k * P:(k + 1) * P], ident[:])
        a = S.pe.done(ins)
        eng, tr = ((act, S.act), (dve, S.dve))[j % 2]
        wait(eng, a, *after)
        o = dstT[:, :, j * P:(j + 1) * P]
        i = bank[b][:].rearrange("p (k n) -> p k n", k=KC)
        return tr.done(act.copy(o, i) if eng is act else dve.tensor_copy(o, i))

    def normalize(tiles, ready, outs, free=()):
        n = len(tiles)
        wait(dve, *ready)
        for j in range(n):
            a = S.dve.done(dve.bn_stats(stat[:, j, :], tiles[j]))
        wait(dve, a)
        for j in range(n):
            a = S.dve.done(dve.bn_aggr(mv[:, j, :], stat[:, j, :]))
        wait(dve, a)
        a = S.dve.done(dve.tensor_scalar_add(rstd[:, 0:n, :], mv[:, 0:n, 1:2], EPS))
        wait(act, a)
        a = S.act.done(act.activation(rstd[:, 0:n, :], rstd[:, 0:n, :], ACT.Sqrt))
        wait(dve, a)
        a = S.dve.done(dve.reciprocal(rstd[:, 0:n, :], rstd[:, 0:n, :]))
        wait(dve, a, *free)
        return [S.dve.done(dve.tensor_scalar(outs[j], tiles[j], mv[:, j, 0:1], rstd[:, j, :],
                                             ALU.subtract, ALU.mult)) for j in range(n)]

    def aggregate(path, nb, co, rows, G, ready, other=None):
        U, space = path.unroll, M.at
        banks = 4 if other else U
        xs = M.new("gathered", [P, U, D])
        sel = M.new("selector", [P, U, P])
        idx = M.new("gather_index", [P, U], I32)
        S.meet()
        part = (path.windows + 1) * 3 // 5
        S.dve.done(dve.memset(G[:, 0:part, :], 0.0))
        S.pool.done(pool.memset(G[:, part:, :], 0.0))
        S.meet()
        with S.loop(path.steps // U) as i:
            gathered, selected, picked = [], [], []
            for u, tile in enumerate(tiles_of_steps(ACTE, path, i)):
                prev(act, S.pe, f"step{u}")
                picked.append(S.act.done(act.copy(idx[:, u:u + 1], src_i[:, ds(tile, 1)])))
            for u in range(U):
                wait(pool, picked[u])
                gathered.append(gather_in[u].done(pool.indirect_dma_start(
                    xs[:, u, :], None, rows, bass.IndirectOffsetOnAxis(ap=idx[:, u:u + 1], axis=0))))
            if other:
                other.registers(i)
            vws = []
            for u, vg in enumerate(tiles_of_steps(DVE, path, i)):
                vw = window_of_step(path, i, u, vg)
                vws.append(vw)
                prev(dve, S.pe, f"step{u}")
                selected.append(S.dve.done(dve.scalar_tensor_tensor(
                    sel[:, u, :].rearrange("p (n b) -> p n b", b=nb),
                    iota[:, ds(vw * path.nodes, path.nodes)].rearrange("p (n b) -> p n b", b=1)
                    .to_broadcast([P, path.nodes, nb]),
                    dst_f[:, ds(vg, 1)],
                    co[:, :, ds(vg, 1)].rearrange("p b t -> p t b").to_broadcast([P, path.nodes, nb]),
                    ALU.is_equal, ALU.mult)))
            for u in range(U):
                wait(pe, gathered[u], selected[u])
                if other and u >= banks:
                    wait(pe, adds[u - banks])
                else:
                    prev(pe, S.dve, f"added{u + U - banks if other else u}")
                a = S.pe.done(pe.matmul(bank[u % banks][:], sel[:, u, :], xs[:, u, :], start=True, stop=True),
                              f"step{u}")
                if other and u % 4 == 0:
                    other.step(u // 4)
                wait(dve, a)
                if u == 0:
                    prev(dve, S.dve, f"added{U - 1}")
                    adds = []
                else:
                    wait(dve, adds[-1])
                g = G[:, ds(vws[u], 1), :].rearrange("p w d -> p (w d)")
                adds.append(S.dve.done(dve.tensor_tensor(g, g, bank[u % banks][:], ALU.add), f"added{u}"))
                if other and u % 4 == 2:
                    other.add(u // 4)
            added = adds[-1]
        S.meet()
        M.at = space
        done = []
        per = P // path.nodes
        assert per == nb
        nbk = per // 4
        for n in range(NT * KC):
            j, k = divmod(n, KC)
            b0 = 4 + (n * nbk) % 4
            wait(pe, added, *([done[n - 4 // nbk]] if n >= 4 // nbk else []))
            for v in range(per):
                ins = pe.transpose(bank[b0 + v // 4][:, (v % 4) * P:(v % 4 + 1) * P],
                                   G[:, j * per + v, k * P:(k + 1) * P], ident[:])
            a = S.pe.done(ins)
            eng, tr = ((act, S.act), (dve, S.dve))[n % 2]
            wait(eng, a)
            for q in range(nbk):
                o = G[:, j * nb:(j + 1) * nb, k * P + q * 4 * path.nodes:k * P + (q + 1) * 4 * path.nodes]
                i_ = bank[b0 + q][:].rearrange("p (m b) -> p b m", b=nb)
                t = tr.done(act.copy(o, i_) if eng is act else dve.tensor_copy(o, i_))
            done.append(t)
        S.meet()
        return done[-2:]

    def basis_lhs(path, nb, G, b):
        return lambda k, j: G[:, j * nb + b, k * P:(k + 1) * P]

    def plain_lhs(xT):
        return lambda k, j: xT[:, k, j * P:(j + 1) * P]

    def transform(products, biases, ready, epilogue):
        ring = M.new("weight_ring", [P, 4, D])
        free = [None] * 4
        n, after = 0, list(ready)
        for half in range(2):
            js = range(half * HALF, (half + 1) * HALF)
            for lhs, weight in products:
                for k in range(KC):
                    s = n % 4
                    if free[s]:
                        wait(sp, free[s])
                    else:
                        wait(sp, *ready)
                    a = chunk_in[s].done(sp.dma_start(ring[:, s, :], weight[k * P:(k + 1) * P, :]))
                    wait(pe, a, *after)
                    after = []
                    for j in js:
                        ins = pe.matmul(bank[j % HALF][:], lhs(k, j), ring[:, s, :],
                                        start=k == 0 and lhs is products[0][0], stop=False)
                    free[s] = S.pe.done(ins)
                    n += 1
            for m, bias in enumerate(biases):
                wait(sp, *([free_row] if (half, m) != (0, 0) else ready))
                a = misc_in.done(sp.dma_start(brow[:], bias.rearrange("(a d) -> a d", a=1)))
                wait(pe, a)
                for j in js:
                    ins = pe.matmul(bank[j % HALF][:], ones[0:1, :], brow[:], start=False,
                                    stop=m == len(biases) - 1)
                free_row = S.pe.done(ins)
            after = epilogue(list(js), free_row)
            S.meet()
        return after

    rows_of = lambda r, j: r[j * P:(j + 1) * P, :]

    M.at = after_edges
    G = M.new("G", [P, PATH0.windows + 1, D])
    after_G = M.at
    S.meet()
    counting = CountSteps()
    GT_done = aggregate(PATH0, 4, coef["L0a"], A["x"], G, [sched_ready], counting)
    count_out = misc_in.done(sp.dma_start(count_rows, counting.count[:, 0:NT, :].rearrange("p j n -> p (j n)")))
    S.meet()
    M.at = after_G
    x = M.new("x", [P, NT, D])
    xT = M.new("xT", [P, KC, NP])
    x_loaded = x_in.done(sp.dma_start(x[:], A["x"].rearrange("(j p) d -> p j d", p=P)))
    xT_done = []
    for j in range(NT):
        xT_done.append(transpose_tile(x[:, j, :], xT, j, 5 + j % 3, [x_loaded, ident_ready] +
                                      xT_done[max(0, j - 3):max(0, j - 2)]))
    layer1_coefficients()
    h = M.new("h", [P, 2, D])
    hT = xT
    h_free = [None, None]
    h_stored, hT_done = [], []

    def hidden(js, ready):
        for j in js:
            s = j % 2
            wait(act, ready, *([h_free[s][0], h_free[s][1]] if h_free[s] else []))
            a = S.act.done(act.activation(h[:, s, :], bank[j % HALF][:], ACT.Relu))
            wait(sp, a)
            o = tile_out[s].done(sp.dma_start(rows_of(hidden_rows, j), h[:, s, :]))
            h_stored.append(o)
            t = transpose_tile(h[:, s, :], hT, j, 6 + s, [a] + (hT_done[-2:-1]))
            hT_done.append(t)
            h_free[s] = (o, t)
        return [a] + hT_done[-2:]

    loop_lhs = plain_lhs(xT)
    products = [(basis_lhs(PATH0, 4, G, b), A["L0_gnn_basis0"][b]) for b in range(4)]
    hid = transform(products + [(loop_lhs, A["L0_gnn_loop0"])], [A["L0_gnn_bias0"]], GT_done + xT_done[-2:], hidden)

    wait(dve, *hid)
    M.at = M.at
    GT_done = aggregate(PATH0, 4, coef["L0b"], hidden_rows, G, h_stored[-2:] + hid)
    x_stored = []

    def residual_norm(rows):
        def epilogue(js, ready):
            wait(dve, ready)
            for j in js:
                a = S.dve.done(dve.tensor_tensor(bank[j % HALF][:], bank[j % HALF][:], x[:, j, :], ALU.add))
            ts = normalize([bank[j % HALF][:] for j in js], [a], [x[:, j, :] for j in js])
            if rows is not None:
                for j, t in zip(js, ts):
                    wait(sp, t)
                    x_stored.append(tile_out[j % 2].done(sp.dma_start(rows_of(rows, j), x[:, j, :])))
            return ts
        return epilogue

    products = [(basis_lhs(PATH0, 4, G, b), A["L0_gnn_basis1"][b]) for b in range(4)]
    nrm = transform(products + [(plain_lhs(hT), A["L0_gnn_loop1"])], [A["L0_gnn_bias1"]], GT_done + hT_done[-2:],
                    residual_norm(x1_rows))

    M.at = after_layer1_edges
    S.meet()
    G = M.new("G1", [P, PATH1.windows + 1, D])
    keep1 = M.at
    GT_done = aggregate(PATH1, 8, coef["L1"], x1_rows, G, x_stored[-2:])
    M.at = keep1
    ring_at = M.at
    M.at = after_constants
    xt = M.new("x_tile", [P, 2, D])
    xn = M.new("x_new", [P, 2, D])
    assert M.at <= after_layer1_edges
    M.at = ring_at
    state = {"read": [None, None], "stored": [None, None]}
    x2_stored = []

    def layer1(js, ready):
        for j in js:
            s = j % 2
            wait(sp, *(GT_done + [S_last] if state["read"][s] is None else [state["read"][s]]))
            t = tile_in[s].done(sp.dma_start(xt[:, s, :], rows_of(x1_rows, j)))
            wait(dve, ready, t)
            state["read"][s] = S.dve.done(dve.tensor_tensor(bank[j % HALF][:], bank[j % HALF][:], xt[:, s, :], ALU.add))
        last = state["read"][js[-1] % 2]
        ts = []
        for pair in (js[0:2], js[2:4], js[4:5]):
            free = [state["stored"][j % 2] for j in pair if state["stored"][j % 2]]
            t2 = normalize([bank[j % HALF][:] for j in pair], [last], [xn[:, j % 2, :] for j in pair], free)
            for j, t in zip(pair, t2):
                wait(sp, t)
                state["stored"][j % 2] = tile_out[j % 2].done(sp.dma_start(rows_of(x2_rows, j), xn[:, j % 2, :]))
                x2_stored.append(state["stored"][j % 2])
            ts += t2
        return ts

    S_last = GT_done[-1]
    products = [(basis_lhs(PATH1, 8, G, b), A["L1_gnn_bases"][b]) for b in range(8)]
    fin1 = transform(products, [A["L1_gnn_h_bias"]], GT_done, layer1)

    M.at = after_constants
    S.meet()
    count = M.new("count_by_src", [P, NT, NP])
    x = M.new("x_L2", [P, NT, D])
    keep2 = M.at
    counted = M.new("count_by_dst", [P, NT, NP])
    c_in = misc_in.done(sp.dma_start(counted[:].rearrange("p j n -> p (j n)"), count_rows))
    x_loaded = x_in.done(sp.dma_start(x[:], x2_rows.rearrange("(j p) d -> p j d", p=P)))
    wait(pe, c_in)
    turned = []
    for j in range(NT):
        for i0 in range(0, NT, 4):
            n, many = len(turned), min(4, NT - i0)
            b = 4 + n % 4
            if n >= 4:
                wait(pe, turned[n - 4])
            for q in range(many):
                ins = pe.transpose(bank[b][:, q * P:(q + 1) * P], counted[:, j, (i0 + q) * P:(i0 + q + 1) * P],
                                   ident[:])
            a = S.pe.done(ins)
            eng, tr = ((act, S.act), (dve, S.dve))[n % 2]
            wait(eng, a)
            o = count[:, i0:i0 + many, j * P:(j + 1) * P]
            i_ = bank[b][:, 0:many * P].rearrange("p (q n) -> p q n", n=P)
            turned.append(tr.done(act.copy(o, i_) if eng is act else dve.tensor_copy(o, i_)))
    S.meet()
    M.at = keep2
    xT = M.new("xT_L2", [P, KC, NP])
    aggT = M.new("aggT", [P, KC, NP])
    rdeg = M.new("rdeg", [P, NT])
    xT_done = []
    for j in range(NT):
        xT_done.append(transpose_tile(x[:, j, :], xT, j, 4 + j % 4, [x_loaded] + xT_done[max(0, j - 4):max(0, j - 3)]))
    for j in range(NT):
        for i in range(NT):
            ins = pe.matmul(bank[0][:, j:j + 1], count[:, i, j * P:(j + 1) * P], ones[:, 0:1],
                            start=i == 0, stop=i == NT - 1)
    a = S.pe.done(ins)
    wait(dve, a)
    a = S.dve.done(dve.tensor_scalar(rdeg[:], bank[0][:, 0:NT], 1.0, None, ALU.max))
    wait(dve, a)
    rdeg_ready = S.dve.done(dve.reciprocal(rdeg[:], rdeg[:]))
    spans = [(c, min(512, NP - c)) for c in range(0, NP, 512)]
    free = {}
    n = 0
    for k in range(KC):
        for c, width in spans:
            b = 1 + n % 3
            if b in free:
                wait(pe, free[b])
            for i in range(NT):
                ins = pe.matmul(bank[b][:, 0:width], x[:, i, k * P:(k + 1) * P], count[:, i, c:c + width],
                                start=i == 0, stop=i == NT - 1)
            a = S.pe.done(ins)
            eng, tr = ((act, S.act), (dve, S.dve))[n % 2]
            wait(eng, a)
            o, i_ = aggT[:, k, c:c + width], bank[b][:, 0:width]
            free[b] = tr.done(act.copy(o, i_) if eng is act else dve.tensor_copy(o, i_))
            n += 1
    agg_done = list(free.values())
    part_ready = {}

    def own(js, ready):
        wait(act, ready, *( [part_free[0]] if part_free else []))
        for j in js:
            a = S.act.done(act.copy(part[:, j % HALF, :], bank[j % HALF][:]))
        return [a]

    ring = M.new("weight_ring2", [P, 2, KC, D])
    w1_in = [chunk_in[m].done(sp.dma_start(ring[:, m, :, :], A[name].rearrange("(k p) d -> p k d", p=P)))
             for m, name in enumerate(("L2_gnn_W1", "L2_gnn_W2"))]
    brows = M.new("bias_rows2", [1, 2, D])
    for m, name in enumerate(("L2_gnn_b1", "L2_gnn_b2")):
        b_in = misc_in.done(sp.dma_start(brows[:, m, :], A[name].rearrange("(a d) -> a d", a=1)))
    wait(pe, *w1_in, b_in, rdeg_ready, *agg_done, *xT_done[-2:])
    wait(dve, rdeg_ready)
    last_ln = []
    for half in range(2):
        js = list(range(half * HALF, (half + 1) * HALF))
        wait(pe, *last_ln)
        for j in js:
            for k in range(KC):
                pe.matmul(bank[j % HALF][:], xT[:, k, j * P:(j + 1) * P], ring[:, 0, k, :], start=k == 0, stop=False)
            for m in range(2):
                ins = pe.matmul(bank[j % HALF][:], ones[0:1, :], brows[:, m, :], start=False, stop=m == 1)
        a = S.pe.done(ins)
        wait(dve, a)
        for j in js:
            t = S.dve.done(dve.tensor_tensor(x[:, j, :], x[:, j, :], bank[j % HALF][:], ALU.add))
        for n_, j in enumerate(js):
            b = 5 + n_ % 3
            if n_ >= 3:
                wait(pe, scaled[n_ - 3])
            else:
                scaled = scaled if n_ else []
            for k in range(KC):
                ins = pe.matmul(bank[b][:], aggT[:, k, j * P:(j + 1) * P], ring[:, 1, k, :],
                                start=k == 0, stop=k == KC - 1)
            a = S.pe.done(ins)
            wait(dve, a, t)
            scaled.append(S.dve.done(dve.scalar_tensor_tensor(
                x[:, j, :], bank[b][:], rdeg[:, j:j + 1], x[:, j, :], ALU.mult, ALU.add)))
        last_ln = normalize([x[:, j, :] for j in js], scaled, [x[:, j, :] for j in js])

    M.at = keep2
    S.meet()
    lay3(nc, A, out, S, M, bank, count, x, ident, ones, stat, mv, rstd, after_constants, brow,
         head_in, block_in, misc_in, out_done, last_ln, transpose_tile, normalize)


def lay3(nc, A, out, S, M, bank, count, x, ident, ones, stat, mv, rstd, after_constants, brow,
         head_in, block_in, misc_in, out_done, last_ln, transpose_tile, normalize):
    wait, prev = S.wait, S.wait_previous
    pe, act, dve, pool, sp = nc.tensor, nc.scalar, nc.vector, nc.gpsimd, nc.sync
    scale = DH ** -0.5
    spans = [(c, min(512, NP - c)) for c in range(0, NP, 512)]
    seen = [(c, min(512, N - c)) for c in range(0, N, 512)]
    xin = M.new("x_start", [P, NT, D])
    start = M.at

    tmp = M.new("tmp", [P, N])
    keep = S.dve.done(dve.tensor_copy(xin[:], x[:]))
    prior = keep
    for j in range(NT):
        c = count[:, j, 0:N]
        wait(dve, prior)
        a = S.dve.done(dve.tensor_scalar(tmp[:], c, 1.0, 1.0, ALU.min, ALU.subtract))
        b = S.dve.done(dve.tensor_scalar(c, c, 1.0, None, ALU.max))
        wait(act, b)
        b = S.act.done(act.activation(c, c, ACT.Ln))
        wait(dve, a, b)
        prior = S.dve.done(dve.scalar_tensor_tensor(c, tmp[:], NEG, c, ALU.mult, ALU.add))
    mask_ready = prior

    M.at = start
    condT = M.new("condT", [COND + 1, NP])
    cond_end = M.at
    ang = M.new("angle", [2 * FREQ, NP])
    turn = M.new("turn", [2 * FREQ, NP])
    emb = M.new("embT", [2 * FREQ, NP])
    kf = M.new("k_float", [2 * FREQ, 1])
    ki = M.new("k_int", [2 * FREQ, 1], I32)
    quarter = M.new("quarter", [2 * FREQ, 1])
    fw1 = M.new("f_w1", [2 * FREQ, COND])
    fw2 = M.new("f_w2", [COND, COND])
    fb = M.new("f_b", [COND, 2])
    hid = M.new("cond_hidden", [COND, NP])
    sig = M.new("cond_sigmoid", [COND, NP])
    wait(pool, mask_ready)
    wait(sp, mask_ready)
    for h in range(2):
        a = S.pool.done(pool.iota(ki[h * FREQ:(h + 1) * FREQ, :], pattern=[[0, 1]], base=1, channel_multiplier=1))
    node = A["node_vec1"]
    misc_in.done(sp.dma_start(ang[:], bass.AP(tensor=node.tensor, offset=node.offset, ap=[[0, 2 * FREQ], [1, NP]])))
    misc_in.done(sp.dma_start(fw1[:], A["L3_gnn_f_w1"]))
    misc_in.done(sp.dma_start(fw2[:], A["L3_gnn_f_w2"]))
    misc_in.done(sp.dma_start(fb[:, 0:1], A["L3_gnn_f_b1"].rearrange("(c a) -> c a", a=1)))
    t = misc_in.done(sp.dma_start(fb[:, 1:2], A["L3_gnn_f_b2"].rearrange("(c a) -> c a", a=1)))
    wait(dve, a, t)
    a = S.dve.done(dve.tensor_copy(kf[:], ki[:]))
    b = S.dve.done(dve.memset(quarter[0:FREQ, :], 0.0))
    b = S.dve.done(dve.memset(quarter[FREQ:2 * FREQ, :], 0.25))
    one = S.dve.done(dve.memset(condT[:], 1.0))
    wait(dve, a, b, one)
    a = S.dve.done(dve.tensor_scalar(kf[:], kf[:], 1.0 / 16, None, ALU.mult))
    wait(dve, a)
    a = S.dve.done(dve.tensor_scalar(ang[:], ang[:], kf[:], quarter[:], ALU.mult, ALU.add))
    wait(dve, a)
    magic = 1.5 * 2.0 ** 23
    a = S.dve.done(dve.tensor_scalar(turn[:], ang[:], magic, None, ALU.add))
    wait(dve, a)
    a = S.dve.done(dve.tensor_scalar(turn[:], turn[:], magic, None, ALU.subtract))
    wait(dve, a)
    a = S.dve.done(dve.tensor_tensor(ang[:], ang[:], turn[:], ALU.subtract))
    wait(act, a)
    emb_ready = S.act.done(act.activation(emb[:], ang[:], ACT.Sin, scale=6.283185))
    wait(pe, emb_ready, one)
    for m, (wt, src, K) in enumerate(((fw1, emb, 2 * FREQ), (fw2, hid, COND))):
        for n, (c, width) in enumerate(spans):
            ins = pe.matmul(bank[n][0:COND, 0:width], wt[:], src[:, c:c + width], start=True, stop=True)
        a = S.pe.done(ins)
        wait(act, a)
        dst = hid if m == 0 else condT[0:COND, :]
        for n, (c, width) in enumerate(spans):
            t = S.act.done(act.activation(dst[:, c:c + width], bank[n][0:COND, 0:width], ACT.Identity,
                                          bias=fb[:, m:m + 1]))
        if m == 0:
            wait(act, t)
            t = S.act.done(act.activation(sig[:], hid[:], ACT.Exp, scale=-1.0))
            wait(dve, t)
            a = S.dve.done(dve.tensor_scalar(sig[:], sig[:], 1.0, None, ALU.add))
            wait(dve, a)
            a = S.dve.done(dve.reciprocal(sig[:], sig[:]))
            wait(dve, a)
            t = S.dve.done(dve.tensor_tensor(hid[:], hid[:], sig[:], ALU.mult))
        wait(pe, t)
    cond_ready = t

    S.meet()
    M.at = cond_end
    yT = M.new("yT", [P, KC, NP])
    attnT = M.new("attnT", [P, HEADS, NP])
    big = M.new("block_weight", [P, KC, D])
    modw = M.new("modulation_weights", [COND + 1, 2, D])
    brow2 = M.new("block_bias_row", [1, D])
    hb = M.new("head_bias_cols", [P, 2])
    mb = M.new("mlp_bias_cols", [P, KC])
    y = M.new("y_tile", [P, 2, D])
    hw = M.new("head_weights", [P, 3, KC, DH])
    vrow = M.new("v_bias_row", [1, DH])
    qT, kT = M.new("qT", [P, NP]), M.new("kT", [P, NP])
    v = M.new("v", [P, NT, DH])
    prob = M.new("prob", [P, 2, N])
    PT = M.new("probT", [P, NT, P])
    rmax = M.new("row_max", [P, 2])
    nmax = M.new("negated_max", [P, 2])
    smax = M.new("span_max", [P, 2, 3])
    rsum = M.new("row_sum", [P, 2])
    has = M.new("has_edges", [P, 2])
    S.meet()

    def modulate(i, names, ready):
        sw, sb, bw, bb = (A["L3_gnn_" + n] for n in names)
        wait(sp, *ready)
        for m, (wt, bs) in enumerate(((sw, sb), (bw, bb))):
            block_in.done(sp.dma_start(modw[0:COND, m, :], wt[ds(i, 1), :, :].rearrange("a c d -> (a c) d")))
            t = block_in.done(sp.dma_start(modw[COND:COND + 1, m, :], bs[ds(i, 1), :]))
        wait(pe, t, *ready)
        free, y_free, last = {}, [None, None], []
        for half in range(2):
            js = list(range(half * HALF, (half + 1) * HALF))
            nx = [attnT[:, :, :].rearrange("p h n -> p (h n)")[:, j * D:(j + 1) * D] for j in js]
            nd = normalize([x[:, j, :] for j in js], ready, nx)
            for j, xn, t in zip(js, nx, nd):
                s = j % 2
                if s in free:
                    wait(pe, free[s])
                for m in range(2):
                    ins = pe.matmul(bank[2 * s + m][:], condT[:, j * P:(j + 1) * P], modw[:, m, :],
                                    start=True, stop=True)
                a = S.pe.done(ins)
                wait(dve, a, t, *([y_free[s]] if y_free[s] else []))
                a = S.dve.done(dve.scalar_tensor_tensor(y[:, s, :], bank[2 * s][:], 1.0, xn, ALU.add, ALU.mult))
                wait(dve, a)
                a = S.dve.done(dve.tensor_tensor(y[:, s, :], y[:, s, :], bank[2 * s + 1][:], ALU.add))
                free[s] = a
                y_free[s] = transpose_tile(y[:, s, :], yT, j, 4 + s, [a] + last[-2:-1])
                last.append(y_free[s])
        return last[-2:] + [free[0], free[1]]

    def add_product(i, lhs, weight, bias, ready):
        wait(sp, *ready)
        block_in.done(sp.dma_start(big[:], weight[ds(i, 1), :, :].rearrange("a (k p) d -> p (a k) d", p=P)))
        t = block_in.done(sp.dma_start(brow2[:], bias[ds(i, 1), :]))
        wait(pe, t, *ready)
        done = []
        for j in range(NT):
            b = j % 4
            if j >= 4:
                wait(pe, done[j - 4])
            for k in range(KC):
                pe.matmul(bank[b][:], lhs[:, k, j * P:(j + 1) * P], big[:, k, :], start=k == 0, stop=False)
            a = S.pe.done(pe.matmul(bank[b][:], ones[0:1, :], brow2[:], start=False, stop=True))
            wait(dve, a)
            done.append(S.dve.done(dve.tensor_tensor(x[:, j, :], x[:, j, :], bank[b][:], ALU.add)))
        return [done[-1]]

    with S.loop(BLOCKS) as i:
        y_ready = modulate(i, ("s1_w", "s1_b", "b1_w", "b1_b"), [])
        S.meet()
        with S.loop(HEADS) as h:
            prev(sp, S.act, "attended")
            for m, (wn, bn) in enumerate((("wq", "bq"), ("wk", "bk"), ("wv", "bv"))):
                wt = A["L3_gnn_" + wn][ds(i, 1), :, ds(h * DH, DH)].rearrange("a (k p) d -> p (a k) d", p=P)
                head_in.done(sp.dma_start(hw[:, m, :, :], wt))
                bs = A["L3_gnn_" + bn][ds(i, 1), ds(h * DH, DH)]
                t = head_in.done(sp.dma_start(vrow[:] if m == 2 else hb[:, m:m + 1],
                                              bs if m == 2 else bs.rearrange("a d -> d a"),
                                              allow_slow_non_contiguous=True))
            wait(dve, t)
            a = S.dve.done(dve.tensor_scalar(hb[:, 0:1], hb[:, 0:1], scale, None, ALU.mult))
            wait(pe, t)
            prev(pe, S.act, "attended")
            prev(act, S.pe, "values")
            wait(act, a, t)
            n, free = 0, {}
            for m, (dst, sc) in enumerate(((qT, scale), (kT, 1.0))):
                for c, width in spans:
                    b = n % 4
                    if b in free:
                        wait(pe, free[b])
                    for k in range(KC):
                        ins = pe.matmul(bank[b][:, 0:width], hw[:, m, k, :], yT[:, k, c:c + width],
                                        start=k == 0, stop=k == KC - 1)
                    a = S.pe.done(ins)
                    wait(act, a)
                    free[b] = S.act.done(act.activation(dst[:, c:c + width], bank[b][:, 0:width], ACT.Identity,
                                                        bias=hb[:, m:m + 1], scale=sc))
                    n += 1
            for j in range(NT):
                b = n % 4
                wait(pe, free[b])
                for k in range(KC):
                    pe.matmul(bank[b][:, 0:DH], yT[:, k, j * P:(j + 1) * P], hw[:, 2, k, :], start=k == 0, stop=False)
                a = S.pe.done(pe.matmul(bank[b][:, 0:DH], ones[0:1, :], vrow[:], start=False, stop=True))
                wait(act, a)
                free[b] = S.act.done(act.copy(v[:, j, :], bank[b][:, 0:DH]))
                n += 1
            wait(pe, *free.values())

            def scores(j):
                for n_, (c, width) in enumerate(seen):
                    ins = pe.matmul(bank[n_][:, 0:width], qT[:, j * P:(j + 1) * P], kT[:, c:c + width],
                                    start=True, stop=True)
                return S.pe.done(ins)

            masked, scaled, turned, moved, mult, left = {}, {}, {}, {}, {}, {}
            for t in range(NT + 2):
                if t >= 2:
                    j, s = t - 2, t % 2
                    wait(pe, scaled[j], *([moved[j - 1]] if j else []))
                    for q in range(NT):
                        width = min(P, N - q * P)
                        ins = pe.transpose(bank[3 + q // 4][0:width, (q % 4) * P:(q % 4 + 1) * P],
                                           prob[:, s, q * P:q * P + width], ident[:])
                    turned[j] = S.pe.done(ins)
                    wait(act, turned[j], *([mult[j - 1]] if j else []))
                    for g, w_ in ((0, 4), (1, 4), (2, 1)):
                        S.act.done(act.copy(PT[:, 4 * g:4 * g + w_, :],
                                            bank[3 + g][:, 0:w_ * P].rearrange("p (q n) -> p q n", n=P)))
                    w_ = N - (NT - 1) * P
                    moved[j] = S.act.done(act.copy(PT[0:w_, NT - 1, :], bank[5][0:w_, P:2 * P]))
                if 1 <= t <= NT:
                    j, s = t - 1, (t - 1) % 2
                    wait(dve, exped_before)
                    a = S.dve.done(dve.reciprocal(rsum[:, s:s + 1], rsum[:, s:s + 1]))
                    wait(dve, a)
                    a = S.dve.done(dve.tensor_tensor(rsum[:, s:s + 1], rsum[:, s:s + 1], has[:, s:s + 1], ALU.mult))
                    wait(dve, a)
                    scaled[j] = S.dve.done(dve.tensor_scalar(prob[:, s, :], prob[:, s, :], rsum[:, s:s + 1], None,
                                                             ALU.mult))
                if t < NT:
                    j, s = t, t % 2
                    wait(pe, *([masked[j - 1]] if j else []))
                    scored = scores(j)
                    wait(dve, scored, *([turned[j - 2]] if j >= 2 else []))
                    for n_, (c, width) in enumerate(seen):
                        S.dve.done(dve.tensor_tensor_reduce(
                            out=prob[:, s, c:c + width], in0=bank[n_][:, 0:width], in1=count[:, j, c:c + width],
                            scale=1.0, scalar=-2.0 * NEG, op0=ALU.add, op1=ALU.max, accum_out=smax[:, s, n_:n_ + 1]))
                    masked[j] = a = Token(S.dve, S.frames[-1], S.dve.base, S.dve.off)
                    wait(dve, a)
                    a = S.dve.done(dve.reduce_max(rmax[:, s:s + 1], smax[:, s, :], AX.X))
                    wait(dve, a)
                    S.dve.done(dve.tensor_scalar(has[:, s:s + 1], rmax[:, s:s + 1], -0.5 * NEG, None, ALU.is_gt))
                    a = S.dve.done(dve.tensor_scalar(nmax[:, s:s + 1], rmax[:, s:s + 1], -1.0, None, ALU.mult))
                    wait(act, a)
                    exped = S.act.done(act.activation(prob[:, s, :], prob[:, s, :], ACT.Exp, bias=nmax[:, s:s + 1],
                                                      accum_out=rsum[:, s:s + 1]))
                exped_before = exped
                if t >= 2:
                    j, s = t - 2, t % 2
                    wait(pe, moved[j], *([left[j - 2]] if j >= 2 else []))
                    for q in range(NT):
                        width = min(P, N - q * P)
                        ins = pe.matmul(bank[6 + s][:, 0:P], v[0:width, q, :], PT[0:width, q, :],
                                        start=q == 0, stop=q == NT - 1)
                    mult[j] = S.pe.done(ins, "values")
                    wait(act, mult[j])
                    left[j] = S.act.done(act.copy(attnT[:, ds(h, 1), j * P:(j + 1) * P].rearrange("p a n -> p (a n)"),
                                                  bank[6 + s][:, 0:P]), "attended")
        S.meet()
        a = add_product(i, attnT, A["L3_gnn_wo"], A["L3_gnn_bo"], [])
        y_ready = modulate(i, ("s2_w", "s2_b", "b2_w", "b2_b"), a)
        wait(sp, *y_ready)
        block_in.done(sp.dma_start(big[:], A["L3_gnn_m_w1"][ds(i, 1), :, :].rearrange("a (k p) d -> p (a k) d", p=P)))
        t = block_in.done(sp.dma_start(mb[:], A["L3_gnn_m_b1"][ds(i, 1), :].rearrange("a (k p) -> p (a k)", p=P),
                                       allow_slow_non_contiguous=True))
        wait(pe, t, *y_ready)
        wait(act, t, *y_ready)
        n, free = 0, {}
        for o in range(KC):
            for c, width in spans:
                b = n % 4
                if b in free:
                    wait(pe, free[b])
                for k in range(KC):
                    ins = pe.matmul(bank[b][:, 0:width], big[:, k, o * P:(o + 1) * P], yT[:, k, c:c + width],
                                    start=k == 0, stop=k == KC - 1)
                a = S.pe.done(ins)
                wait(act, a)
                free[b] = S.act.done(act.activation(attnT[:, o, c:c + width], bank[b][:, 0:width], ACT.Relu,
                                                    bias=mb[:, o:o + 1]))
                n += 1
        a = add_product(i, attnT, A["L3_gnn_m_w2"], A["L3_gnn_m_b2"], list(free.values()))
        S.meet()

    wait(dve, Token(S.dve, "top", S.dve.base, S.dve.off))
    a = S.dve.done(dve.tensor_tensor(x[:], x[:], xin[:], ALU.add))
    for half in range(2):
        js = list(range(half * HALF, (half + 1) * HALF))
        for j, t in zip(js, normalize([x[:, j, :] for j in js], [a], [x[:, j, :] for j in js])):
            rows = min(P, N - j * P)
            wait(sp, t)
            o = out_done.done(sp.dma_start(out[j * P:j * P + rows, :], x[0:rows, j, :]))
            a = t
    wait(sp, o)


EDGE_INPUTS = ("src", "dst", "edge_type_8", "edge_type_32", "edge_weight", "edge_weight1")


def kernel(**inputs):
    import numpy as np
    import concourse.bacc as bacc
    from concourse.bass_utils import run_bass_kernel_spmd

    arrays = {}
    for name, a in inputs.items():
        a = np.ascontiguousarray(a)
        if name in EDGE_INPUTS:
            flat = np.full(T * P, PAD_DST if name == "dst" else 0, a.dtype)
            flat[:E] = a.reshape(-1)
            if name == "dst":
                arrays["dst_flat"] = flat
            a = np.ascontiguousarray(flat.reshape(T, P).T)
        elif name in ("x", "node_vec1"):
            padded = np.zeros((NP, a.shape[1]), a.dtype)
            padded[:N] = a
            a = padded.reshape(-1) if name == "node_vec1" else padded
        elif name in ("L2_gnn_W1", "L2_gnn_W2"):
            a = np.ascontiguousarray(a.T)
        arrays[name] = a

    counts = {}
    for final in (False, True):
        nc = bacc.Bacc("TRN2", target_bir_lowering=False, num_devices=1)
        A = {n: nc.dram_tensor(f"in_{n}", a.shape, mybir.dt.from_np(a.dtype), kind="ExternalInput").ap()
             for n, a in arrays.items()}
        out = nc.dram_tensor("out_x", (N, D), F32, kind="ExternalOutput").ap()
        build(nc, A, out, counts)
    r = run_bass_kernel_spmd(nc, [{f"in_{n}": a for n, a in arrays.items()}], core_ids=[0])
    return r.results[0]["out_x"]
```

```python
import concourse.bass as bass
from concourse import mybir

F32R = mybir.dt.float32r
F32, I32, BF16, F16 = mybir.dt.float32, mybir.dt.int32, mybir.dt.bfloat16, mybir.dt.float16
ALU = mybir.AluOpType
ACT = mybir.ActivationFunctionType
AX = mybir.AxisListType
ds = bass.ds
ACTE, DVE = mybir.EngineType.Activation, mybir.EngineType.DVE

P = 128
N = 1250
NT = -(-N // P)
NP = NT * P
D = 512
KC = D // P
E = 21250
T = -(-E // (4 * P)) * 4
SLOTS = 8
RINGS = 4 * SLOTS * (D + P + 1)
PAD_DST = NP - 1
HEADS, BLOCKS = 4, 4
DH = D // HEADS
HALF = NT // 2
EPS = 1e-5
NEG = 1e30
FREQ, COND = 32, 16
STACK = [0, 32, 64]
STACKED = 96
SPANS = [(c, min(512, NP - c)) for c in range(0, NP, 512)]


class Path:

    def __init__(self, shift, unroll, tiles=1):
        self.shift, self.nodes, self.tiles = shift, 1 << shift, tiles
        self.unroll = unroll
        self.windows = NP >> shift
        self.groups = T // tiles
        self.steps = -(-(self.groups + self.windows - 1) // unroll) * unroll
        assert self.steps - self.groups <= self.windows


PATH0, PATH1, PATHC = Path(5, 16), Path(4, 13), Path(7, 4, 4)


class Token:

    def __init__(self, track, frame, base, off):
        self.track, self.frame, self.base, self.off = track, frame, base, off


class Track:

    def __init__(self, sync, name, unit):
        self.sync, self.name, self.unit = sync, name, unit
        self.sem = sync.nc.alloc_semaphore(name)
        self.base, self.off = 0, 0
        sync.tracks.append(self)

    def prime(self, engine, n):
        engine.sem_inc(self.sem, n)
        self.off += n

    def done(self, instruction, label=None):
        instruction.then_inc(self.sem, self.unit)
        self.off += self.unit
        frame = self.sync.frames[-1]
        if label is not None:
            self.sync.marks[frame, self.name, label] = self.off
        return Token(self, frame, self.base, self.off)


class Sync:

    def __init__(self, nc, counts, prefix=""):
        self.nc, self.counts, self.tracks = nc, counts, []
        self.frames, self.marks, self.waited, self.loops = ["top"], {}, {}, 0
        self.idle = nc.alloc_semaphore(prefix + "idle")
        self.pe, self.act, self.dve, self.pool = (Track(self, f"{prefix}{n}_done", 1) for n in ("pe", "act", "dve", "pool"))

    def wait(self, engine, *tokens):
        for t in tokens:
            key = (id(engine), t.track.name, t.frame, self.frames[-1])
            if self.waited.get(key, -1) < t.off:
                self.waited[key] = t.off
                self.wait_value(engine, t.track.sem, t.base + t.off)

    def wait_value(self, engine, sem, value):
        engine.wait_ge(sem, value)
        if not isinstance(value, int):
            engine.sem_inc(self.idle, 1)

    def wait_previous(self, engine, track, label):
        frame = self.frames[-1]
        per = self.counts.get(("per", frame, track.name), 1)
        mark = self.counts.get(("mark", frame, track.name, label), 1)
        self.wait_value(engine, track.sem, track.base + (mark - per))

    def meet(self):
        for engine in (self.nc.tensor, self.nc.scalar, self.nc.vector, self.nc.gpsimd, self.nc.sync):
            for t in self.tracks:
                if t.off:
                    self.wait(engine, Token(t, self.frames[-1], t.base, t.off))

    def before(self, track):
        return Token(track, self.frames[-1], track.base, 0)

    def now(self, track):
        return Token(track, self.frames[-1], track.base, track.off)

    def loop(self, trips):
        return _Loop(self, trips)


class _Loop:
    def __init__(self, sync, trips):
        self.sync, self.trips = sync, trips

    def __enter__(self):
        s = self.sync
        s.loops += 1
        self.frame = f"loop{s.loops}"
        self.fori = s.nc.Fori(0, self.trips)
        i = self.fori.__enter__()
        s.frames.append(self.frame)
        self.saved = [(t, t.base, t.off) for t in s.tracks]
        for t in s.tracks:
            per = s.counts.get(("per", self.frame, t.name), 0)
            t.base = (t.base + t.off) + i * per if per else t.base + t.off
            t.off = 0
        return i

    def __exit__(self, *exc):
        s = self.sync
        known = {t for t, _, _ in self.saved}
        for t, base, off in self.saved:
            s.counts["per", self.frame, t.name] = t.off
            t.base, t.off = base, off + self.trips * t.off
        for (frame, name, label), off in s.marks.items():
            s.counts["mark", frame, name, label] = off
        assert all(t in known for t in s.tracks), "make tracks outside loops"
        s.frames.pop()
        return self.fori.__exit__(*exc)


class Arena:

    def __init__(self, nc):
        self.nc, self.at, self.n = nc, -(-nc.sbuf_base // 64) * 64, 0
        self.end = nc.sbuf_usable_end

    def new(self, name, shape, dtype=F32):
        size = mybir.dt.size(dtype)
        for d in shape[1:]:
            size *= d
        self.n += 1
        t = self.nc.alloc_sbuf_tensor_at(f"{name}_{self.n}", shape, dtype, offset=self.at)
        self.at += -(-size // 32) * 32
        assert self.at <= self.end, (name, self.at, self.end)
        return t


def split_in_place(M, name, shape):
    at = M.at
    loaded = M.new(name, shape)
    M.at = at
    return loaded, M.new(name + "_lo", shape, F32R)


def sort_edges(nc, A, M, counts, load_edges):
    S = Sync(nc, counts, "sort_")
    wait, dve, pool, sp = S.wait, nc.vector, nc.gpsimd, nc.sync
    stage_in, place_out = Track(S, "sort_stage_in", 16), Track(S, "sort_place_out", 16)
    parts = 8
    width = T * P // parts
    all_dst = M.new("all_dst", [P, T * P], I32)
    all_f = all_dst[:].bitcast(F32)
    number_i, number = M.new("edge_number_int", [P, width], I32), M.new("edge_number", [P, width])
    own_i, own, rel = M.new("own_number_int", [P, 1], I32), M.new("own_number", [P, 1]), M.new("own_relative", [P, 1])
    before, counted = M.new("comes_before", [P, width]), M.new("before_in_part", [P, parts])
    place_f, place = M.new("place_float", [P, 1]), M.new("place", [P, 1], I32)
    stage = {n: M.new("staged", [P, 1], F32 if "weight" in n else I32) for n in EDGE_INPUTS}
    dst = M.new("staged_dst_float", [P, 1])
    lists = {n: nc.dram_tensor(f"sorted_{n}", (T * P,), stage[n].dtype, kind="Internal").ap() for n in EDGE_INPUTS}
    row = A["dst"][0:T * P].rearrange("(a n) -> a n", a=1)
    stage_in.done(sp.dma_start(all_dst[:], bass.AP(tensor=row.tensor, offset=row.offset, ap=[[0, P], [1, T * P]])))
    S.pool.done(pool.iota(number_i[:], pattern=[[1, width]], base=0, channel_multiplier=0))
    S.pool.done(pool.iota(own_i[:], pattern=[[0, 1]], base=0, channel_multiplier=1))
    S.meet()
    S.dve.done(dve.tensor_copy(all_f, all_dst[:]))
    S.dve.done(dve.tensor_copy(number[:], number_i[:]))
    S.dve.done(dve.tensor_copy(own[:], own_i[:]))
    S.meet()
    with S.loop(T) as t:
        for n in EDGE_INPUTS:
            a = stage_in.done(sp.dma_start(stage[n][:], A[n][ds(t * P, P)].rearrange("(e a) -> e a", a=1)))
        wait(dve, a)
        wait(dve, S.dve.done(dve.tensor_copy(dst[:], stage["dst"][:])))
        for q in range(parts):
            part = all_f[:, q * width:(q + 1) * width]
            wait(dve, S.dve.done(dve.tensor_scalar(rel[:], own[:], float(-q * width), None, ALU.add)))
            wait(dve, S.dve.done(dve.tensor_scalar(before[:], number[:], rel[:], None, ALU.is_lt)))
            wait(dve, S.dve.done(dve.scalar_tensor_tensor(before[:], part, dst[:], before[:], ALU.is_equal, ALU.mult)))
            wait(dve, S.dve.done(dve.scalar_tensor_tensor(before[:], part, dst[:], before[:], ALU.is_lt, ALU.add)))
            wait(dve, S.dve.done(dve.reduce_sum(counted[:, q:q + 1], before[:], AX.X)))
        S.dve.done(dve.tensor_scalar(own[:], own[:], float(P), None, ALU.add))
        wait(dve, S.dve.done(dve.reduce_sum(place_f[:], counted[:], AX.X)))
        wait(pool, S.dve.done(dve.tensor_copy(place[:], place_f[:])), a)
        for n in EDGE_INPUTS:
            place_out.done(pool.indirect_dma_start(
                lists[n].rearrange("(e a) -> e a", a=1), bass.IndirectOffsetOnAxis(ap=place[:], axis=0), stage[n][:], None))
        S.meet()
    load_edges(lists, stage_in)
    S.meet()


def build(nc, A, out, counts):
    S = Sync(nc, counts)
    wait, prev = S.wait, S.wait_previous
    pe, act, dve, pool, sp = nc.tensor, nc.scalar, nc.vector, nc.gpsimd, nc.sync
    S.pe.prime(pe, 32)
    M = Arena(nc)
    gather_in = [Track(S, f"gather{u}_in", 16) for u in range(SLOTS)]
    count_out = Track(S, "count_out", 16)
    count_in = [Track(S, f"count_tile{j}_in", 16) for j in range(NT)]
    chunk_in = [Track(S, f"weight_chunk{u}_in", 16) for u in range(4)]
    tile_in = [Track(S, f"tile{u}_in", 16) for u in range(HALF)]
    tile_out = [Track(S, f"tile{u}_out", 16) for u in range(HALF)]
    weights_in = {n: Track(S, f"{n}_in", 16) for n in ("queries_keys", "values", "modulation", "bias",
                                                       "product0", "product1")}
    projected = [Track(S, f"{n}_projected", 1) for n in ("queries_keys", "values")]
    for track in projected:
        track.prime(pe, 1)
    misc_in = Track(S, "misc_in", 16)
    x_out = Track(S, "x_out", 16)
    order_in = Track(S, "order_in", 16)
    x_in = Track(S, "x_in", 16)
    out_done = Track(S, "out_done", 16)

    bank = [nc.alloc_psum_tensor(f"bank{b}", [P, 512], F32) for b in range(8)]

    hidden_rows = nc.dram_tensor("hidden_rows", (NP, D), F32, kind="Internal").ap()
    x1_rows = nc.dram_tensor("x1_rows", (NP, D), F32, kind="Internal").ap()
    x2_rows = nc.dram_tensor("x2_rows", (NP, D), F32, kind="Internal").ap()

    ident = M.new("ident", [P, P])
    ones = M.new("ones", [P, P])
    zero = M.new("zero", [P, 1])
    window_of_step = {p: M.new("window_of_step", [1, p.steps], I32) for p in (PATH0, PATH1, PATHC)}
    flag = M.new("unsorted", [1, 1], I32)
    brow = M.new("bias_row", [1, D])
    stat = M.new("ln_stats", [P, HALF, 6])
    mv = M.new("ln_mean_var", [P, HALF, 2])
    rstd = M.new("ln_rstd", [P, HALF, 1])
    after_constants = M.at
    iota = M.new("iota", [P, 2 * P])
    src_i = {p: M.new("src_index", [P, p.steps], I32) for p in (PATH1,)}
    place = {p: M.new("place_in_window", [P, p.steps]) for p in (PATH1,)}
    coef = {"L1": M.new("coef_L1", [P, 8, PATH1.steps])}
    after_layer1_edges = M.at
    src_i[PATH0] = M.new("src_index", [P, PATH0.steps], I32)
    place |= {PATH0: M.new("place_in_window", [P, PATH0.steps]),
              PATHC: M.new("place_in_window", [P, PATHC.steps * PATHC.tiles])}
    src_f = M.new("src_float", [P, PATHC.steps * PATHC.tiles])
    coef |= {"L0a": M.new("coef_L0a", [P, 4, PATH0.steps]), "L0b": M.new("coef_L0b", [P, 4, PATH0.steps])}
    types = {p: M.new("types", [P, p.steps]) for p in (PATH0, PATH1)}
    weights = {p: M.new("weights", [P, p.steps]) for p in (PATH0, PATH1)}
    comp = M.new("comp", [P, 8 * 4 * 2 + 32 * 8])
    mask = M.new("relation_mask", [P, 2, max(PATH0.steps, PATH1.steps)])
    after_edges = M.at

    c0 = S.dve.done(dve.memset(ident[:], 0.0))
    c1 = S.dve.done(dve.memset(ones[:], 1.0))
    zero_ready = S.dve.done(dve.memset(zero[:], 0.0))
    wait(pool, c0)
    ident_ready = S.pool.done(pool.affine_select(
        out=ident[:], in_=ident[:], compare_op=ALU.not_equal, fill=1.0, base=0, pattern=[[-1, P]],
        channel_multiplier=1))
    iota_i = M.new("iota_int", [P, NP], I32)
    k1 = S.pool.done(pool.iota(iota_i[:], pattern=[[1, NP]], base=0, channel_multiplier=0))
    wait(dve, k1)
    iota_ready = S.dve.done(dve.tensor_copy(iota[:], iota_i[:, 0:2 * P]))
    group_i = M.new("group_int", [P, 2], I32)
    group = M.new("group", [P, 2])
    t = S.pool.done(pool.iota(group_i[:], pattern=[[P, 2]], base=0, channel_multiplier=1))
    wait(dve, t)
    group_ready = S.dve.done(dve.tensor_copy(group[:], group_i[:]))

    at = 0
    for name, n in (("L0_gnn_comp0", 32), ("L0_gnn_comp1", 32), ("L1_gnn_w_comp", 256)):
        row = A[name].rearrange("r b -> (r b)").rearrange("(a n) -> a n", a=1)
        misc_in.done(sp.dma_start(comp[:, at:at + n], bass.AP(
            tensor=row.tensor, offset=row.offset, ap=[[0, P], [1, n]])))
        at += n

    def chunks(groups):
        return [(c, min(P, groups - c * P)) for c in range(-(-groups // P))]

    raw = {}
    for name in EDGE_INPUTS:
        dtype = F32 if "weight" in name else I32
        raw[name] = M.new(name, [P, 2, P], dtype), M.new(name + "_float", [P, 2, P]), dtype
    for name in ("src", "dst"):
        raw[name, "group"] = (M.new(name + "_groups", [P, PATHC.tiles, P], I32),
                              M.new(name + "_groups_float", [P, PATHC.tiles, P]), I32)
    ends = {}
    for path in (PATH0, PATHC):
        ends[path] = M.new("last_dst", [P, 2, 2], I32)
        wait(sp, S.dve.done(dve.memset(ends[path][:], 0)))
    ends[PATH1] = ends[PATH0]

    def load_edges(lists, track):
        for name in EDGE_INPUTS:
            for c, rows in chunks(T):
                track.done(sp.dma_start(raw[name][0][0:rows, c, :],
                                        lists[name][c * P * P:(c * P + rows) * P].rearrange("(t e) -> t e", e=P)))
        for name in ("src", "dst"):
            track.done(sp.dma_start(raw[name, "group"][0][0:PATHC.groups],
                                    lists[name][0:T * P].rearrange("(t q e) -> t q e", e=P, q=PATHC.tiles)))
        for path in (PATH0, PATHC):
            flat = lists["dst"][0:T * P].rearrange("(g s) -> g s", s=path.tiles * P)
            for c, rows in chunks(path.groups):
                for before in range(2):
                    skip = 1 if before and c == 0 else 0
                    t = track.done(sp.dma_start(
                        ends[path][skip:rows, c, before:before + 1],
                        flat[c * P + skip - before:c * P + rows - before, path.tiles * P - 1:path.tiles * P],
                        allow_slow_non_contiguous=True))
        return t

    this, after = (M.new(n, [P, 2, P], I32) for n in ("dst_this", "dst_after"))
    broken = M.new("out_of_order", [P, 2])
    descents = M.new("descents", [P, 2, P])
    for c, rows in chunks(T):
        for n, tile in enumerate((this, after)):
            t = order_in.done(sp.dma_start(tile[0:rows, c, :], A["dst"][c * P * P + n:(c * P + rows) * P + n].rearrange(
                "(t e) -> t e", e=P)))
    edges_loaded = load_edges(A, misc_in)
    wait(dve, t)
    this_f, after_f = (M.new(n, [P, 2, P]) for n in ("dst_this_float", "dst_after_float"))
    for c, rows in chunks(T):
        S.dve.done(dve.tensor_copy(this_f[0:rows, c, :], this[0:rows, c, :]))
        a = S.dve.done(dve.tensor_copy(after_f[0:rows, c, :], after[0:rows, c, :]))
    wait(dve, a)
    for c, rows in chunks(T):
        a = S.dve.done(dve.tensor_tensor(descents[0:rows, c, :], this_f[0:rows, c, :], after_f[0:rows, c, :], ALU.is_gt))
    wait(dve, a)
    for c, rows in chunks(T):
        a = S.dve.done(dve.reduce_sum(broken[0:rows, c:c + 1], descents[0:rows, c, :], AX.X))
    wait(pe, a)
    for c, rows in chunks(T):
        ins = pe.matmul(bank[0][0:1, 0:1], ones[0:rows, 0:1], broken[0:rows, c:c + 1], start=c == 0, stop=c == 1)
    wait(dve, S.pe.done(ins))
    flag_ready = S.dve.done(dve.tensor_copy(flag[:], bank[0][0:1, 0:1]))
    for engine in (pe, act, dve, pool, sp):
        wait(engine, flag_ready)
    wait(sp, edges_loaded)
    unsorted = nc.values_load_multi_w_load_instructions(flag[0:1, 0:1], min_val=0, max_val=E)[1][0]
    with nc.If(unsorted > 0):
        space = M.at
        sort_edges(nc, A, M, counts.setdefault("sort", {}), load_edges)
        M.at = space
    wait(dve, edges_loaded)
    edges = {}
    for key, (i_, f_, dtype) in raw.items():
        if dtype is F32:
            edges[key] = i_
        else:
            for c, rows in [(slice(None), PATHC.groups)] if isinstance(key, tuple) else chunks(T):
                t = S.dve.done(dve.tensor_copy(f_[0:rows, c, :], i_[0:rows, c, :]))
            edges[key] = f_
    edges_ready = t

    wait(dve, group_ready, iota_ready)
    banks_left = {}
    used = [0]

    def by_step(lhs, onehot, path, out):
        b = used[0] % 8
        used[0] += 1
        wait(pe, *([banks_left[b]] if b in banks_left else []))
        parts = chunks(path.groups)
        for c, rows in parts:
            ins = pe.matmul(bank[b][:, 0:path.steps], lhs(c, rows), onehot(c, rows), start=c == 0, stop=c == len(parts) - 1)
        wait(dve, S.pe.done(ins))
        banks_left[b] = out(bank[b][:, 0:path.steps])
        return banks_left[b]

    for path in (PATHC, PATH0, PATH1):
        window = M.new("window_of_group", [P, 2, 2], I32)
        key = M.new("key", [P, 2, 2])
        hit = M.new("passed", [P, 2, 2, path.steps])
        onehot = M.new("tile_of_step_onehot", [P, 2, path.steps])
        start = M.new("window_start", [P, path.steps])
        steps = path.steps
        a = S.dve.done(dve.tensor_single_scalar(window[:], ends[path][:], path.shift, ALU.arith_shift_right))
        wait(dve, a)
        a = S.dve.done(dve.tensor_copy(key[:], window[:]))
        wait(dve, a)
        S.dve.done(dve.tensor_tensor(key[:, :, 0], key[:, :, 0], group[:], ALU.add))
        a = S.dve.done(dve.scalar_tensor_tensor(key[:, :, 1], key[:, :, 1], -1.0, group[:], ALU.add, ALU.add))
        wait(dve, a)
        for c, rows in chunks(path.groups):
            for before in range(2):
                a = S.dve.done(dve.tensor_scalar(hit[0:rows, c, before, :], iota[0:rows, 0:steps],
                                                 key[0:rows, c, before:before + 1], None, ALU.is_gt))
            wait(dve, a)
            a = S.dve.done(dve.tensor_tensor(onehot[0:rows, c, :], hit[0:rows, c, 1, :], hit[0:rows, c, 0, :],
                                             ALU.subtract))
        wait(pe, a, c1, edges_ready)

        def windows(tiles_passed):
            a = S.dve.done(dve.tensor_tensor(start[:], iota[:, 0:steps], tiles_passed, ALU.subtract))
            wait(dve, a)
            wait(dve, S.dve.done(dve.tensor_copy(window_of_step[path][:], start[0:1, :])))
            a = S.dve.done(dve.tensor_scalar(start[:], start[:], float(path.nodes), None, ALU.mult))
            wait(dve, a)
            return a

        by_step(lambda c, rows: ones[0:rows, :], lambda c, rows: hit[0:rows, c, 0, :], path, windows)

        def gather_steps(data, out, minus=None):
            return by_step(lambda c, rows: data(c, rows), lambda c, rows: onehot[0:rows, c, :], path,
                           lambda got: S.dve.done(dve.tensor_tensor(out, got, minus, ALU.subtract) if minus is not None
                                                  else dve.tensor_copy(out, got)))

        if path is PATHC:
            for q in range(path.tiles):
                pick = lambda t: t[:].rearrange("p (s q) -> p s q", q=path.tiles)[:, :, q]
                gather_steps(lambda c, rows: edges["src", "group"][0:rows, q, :], pick(src_f))
                by_step_done = gather_steps(lambda c, rows: edges["dst", "group"][0:rows, q, :], pick(place[path]), start[:])
        else:
            kind = ("_8", "edge_weight") if path is PATH0 else ("_32", "edge_weight1")
            for key_, out_ in (("src", src_i[path]), ("edge_type" + kind[0], types[path]), (kind[1], weights[path])):
                gather_steps(lambda c, rows: edges[key_][0:rows, c, :], out_[:])
            by_step_done = gather_steps(lambda c, rows: edges["dst"][0:rows, c, :], place[path][:], start[:])
    wait(dve, by_step_done)
    S.meet()


    def coefficients(path, relations, outs):
        first = [S.dve.done(dve.memset(o[:], 0.0)) for o, _, _ in outs]
        wait(dve, *first)
        for r in range(relations):
            m = S.dve.done(dve.scalar_tensor_tensor(mask[:, r % 2, 0:path.steps], types[path][:], float(r),
                                                    weights[path][:], ALU.is_equal, ALU.mult))
            wait(dve, m)
            for o, table, nb in outs:
                for b in range(nb):
                    at = table + r * nb + b
                    t = S.dve.done(dve.scalar_tensor_tensor(o[:, b, :], mask[:, r % 2, 0:path.steps], comp[:, at:at + 1],
                                                            o[:, b, :], ALU.mult, ALU.add))
            yield t

    M.at = after_edges

    def windows_of_steps(path, i):
        n = path.unroll
        return nc.values_load_multi_w_load_instructions(
            window_of_step[path][0:1, ds(i * n, n)], engines=[DVE], min_val=0, max_val=path.windows)[1]

    count_rows = nc.dram_tensor("count_rows", (P, NT * NP), F32, kind="Internal").ap()

    class CountSteps:
        def __init__(self):
            self.oh_src = M.new("onehot_src", [P, PATHC.tiles, NP], BF16)
            self.oh_dst = M.new("onehot_dst", [P, PATHC.tiles, P], BF16)
            self.iota16 = M.new("node_iota_16bit", [P, NP], F16)
            self.at = M.at
            self.count = M.new("count", [P, NT + 1, NP])
            S.pool.done(pool.iota(self.iota16[:], pattern=[[1, NP]], base=0, channel_multiplier=0,
                                  allow_small_or_imprecise_dtypes=True))
            S.pool.done(pool.memset(self.count[:], 0.0))
            self.made, self.counted, self.added = {}, {}, {}

        def begin(self, i):
            self.i = i

        def registers(self):
            self.windows = windows_of_steps(PATHC, self.i)

        def one_hot(self, n):
            c, q = divmod(n, PATHC.tiles)
            step_tile = ds(self.i * (PATHC.unroll * PATHC.tiles) + n, 1)
            if c == 0:
                prev(dve, S.pe, f"counted{PATHC.unroll * PATHC.tiles - PATHC.tiles + q}")
            else:
                wait(dve, self.counted[n - PATHC.tiles])
            S.dve.done(dve.tensor_scalar(self.oh_src[:, q, :], self.iota16[:, 0:NP], src_f[:, step_tile],
                                         None, ALU.is_equal))
            self.made[n] = S.dve.done(dve.tensor_scalar(self.oh_dst[:, q, :], self.iota16[:, 0:P],
                                                        place[PATHC][:, step_tile], None, ALU.is_equal))

        def multiply(self, n):
            c, q = divmod(n, PATHC.tiles)
            if q == 0:
                if c >= 2:
                    wait(pe, self.added[c - 2])
                else:
                    prev(pe, S.dve, f"group{PATHC.unroll - 2 + c}_added")
            wait(pe, self.made[n])
            for m, (col, width) in enumerate(SPANS):
                ins = pe.matmul(bank[2 + 3 * (c % 2) + m][:, 0:width], self.oh_dst[:, q, :],
                                self.oh_src[:, q, col:col + width], start=q == 0, stop=q == PATHC.tiles - 1)
            self.counted[n] = S.pe.done(ins, f"counted{n}")

        def add(self, c, m):
            col, width = SPANS[m]
            wait(dve, self.counted[c * PATHC.tiles + PATHC.tiles - 1])
            if c == 0:
                prev(dve, S.dve, f"group{PATHC.unroll - 1}_added")
            else:
                wait(dve, self.added[c - 1])
            dst = self.count[:, ds(self.windows[c], 1), col:col + width].rearrange("p a n -> p (a n)")
            self.added[c] = S.dve.done(dve.tensor_tensor(dst, dst, bank[2 + 3 * (c % 2) + m][:, 0:width], ALU.add),
                                       f"group{c}_added")

        def store(self):
            self.stored = count_out.done(act.dma_start(count_rows, self.count[:, 0:NT, :].rearrange("p j n -> p (j n)")))

    def transpose_tile(src, dstT, j, b, ready, after=()):
        wait(pe, *ready)
        for k in range(KC):
            ins = pe.transpose(bank[b][:, k * P:(k + 1) * P], src[:, k * P:(k + 1) * P], ident[:])
        a = S.pe.done(ins)
        eng, tr = ((act, S.act), (dve, S.dve))[j % 2]
        wait(eng, a, *after)
        o = dstT[:, :, j * P:(j + 1) * P]
        i = bank[b][:].rearrange("p (k n) -> p k n", k=KC)
        return tr.done(act.copy(o, i) if eng is act else dve.tensor_copy(o, i))

    def normalize(tiles, ready, outs, free=()):
        n = len(tiles)
        wait(dve, *ready)
        for j in range(n):
            a = S.dve.done(dve.bn_stats(stat[:, j, :], tiles[j]))
        wait(dve, a)
        for j in range(n):
            a = S.dve.done(dve.bn_aggr(mv[:, j, :], stat[:, j, :]))
        wait(dve, a)
        a = S.dve.done(dve.tensor_scalar_add(rstd[:, 0:n, :], mv[:, 0:n, 1:2], EPS))
        wait(act, a)
        a = S.act.done(act.activation(rstd[:, 0:n, :], rstd[:, 0:n, :], ACT.Sqrt))
        wait(dve, a)
        a = S.dve.done(dve.reciprocal(rstd[:, 0:n, :], rstd[:, 0:n, :]))
        wait(dve, a, *free)
        return [S.dve.done(dve.tensor_scalar(outs[j], tiles[j], mv[:, j, 0:1], rstd[:, j, :],
                                             ALU.subtract, ALU.mult)) for j in range(n)]

    def aggregate(path, nb, co, rows, G, other=None):
        U, space, ahead = path.unroll, M.at, SLOTS - 2
        banks = 2 if other else 8
        xs = M.new("gathered", [P, SLOTS, D])
        sel = M.new("selector", [P, SLOTS, P])
        idx = M.new("gather_index", [P, SLOTS], I32)
        if not other:
            S.meet()
        a, b = (path.windows + 1) * 3 // 10, (path.windows + 1) * 13 // 20
        S.dve.done(dve.memset(G[:, 0:a, :], 0.0))
        S.act.done(act.copy(G[:, a:b, :], zero[:].rearrange("p (n d) -> p n d", n=1).to_broadcast([P, b - a, D])))
        S.pool.done(pool.memset(G[:, b:, :], 0.0))
        S.meet()

        def last(u, ring):
            return u % ring + (U - 1 - u % ring) // ring * ring

        with S.loop(path.steps // U) as i:
            gathered, selected, multiplied, adds = {}, {}, {}, {}

            def slot_free(engine, u):
                if u < SLOTS:
                    prev(engine, S.pe, f"step{last(u, SLOTS)}")
                else:
                    wait(engine, multiplied[u - SLOTS])

            def gather(u):
                s = u % SLOTS
                slot_free(act, u)
                wait(pool, S.act.done(act.copy(idx[:, s:s + 1], src_i[path][:, ds(i * U + u, 1)])))
                gathered[u] = gather_in[s].done(pool.indirect_dma_start(
                    xs[:, s, :], None, rows, bass.IndirectOffsetOnAxis(ap=idx[:, s:s + 1], axis=0)))

            def select(u):
                slot_free(dve, u)
                selected[u] = S.dve.done(dve.scalar_tensor_tensor(
                    sel[:, u % SLOTS, :].rearrange("p (n b) -> p n b", b=nb),
                    iota[:, 0:path.nodes].rearrange("p (n b) -> p n b", b=1)
                    .to_broadcast([P, path.nodes, nb]),
                    place[path][:, ds(i * U + u, 1)],
                    co[:, :, ds(i * U + u, 1)].rearrange("p b t -> p t b").to_broadcast([P, path.nodes, nb]),
                    ALU.is_equal, ALU.mult))

            def add(u):
                wait(dve, multiplied[u])
                if u == 0:
                    prev(dve, S.dve, f"added{U - 1}")
                else:
                    wait(dve, adds[u - 1])
                g = G[:, ds(windows[u], 1), :].rearrange("p w d -> p (w d)")
                adds[u] = S.dve.done(dve.tensor_tensor(g, g, bank[u % banks][:], ALU.add), f"added{u}")

            for u in range(SLOTS):
                gather(u)
            if other:
                other.begin(i)
            for u in range(ahead):
                select(u)
            windows = windows_of_steps(path, i)
            if other:
                other.registers()
            for u in range(U):
                if other:
                    other.one_hot(u)
                wait(pe, gathered[u], selected[u])
                if u < banks:
                    prev(pe, S.dve, f"added{last(u, banks)}")
                else:
                    wait(pe, adds[u - banks])
                multiplied[u] = S.pe.done(pe.matmul(bank[u % banks][:], sel[:, u % SLOTS, :], xs[:, u % SLOTS, :],
                                                    start=True, stop=True), f"step{u}")
                if other:
                    other.multiply(u)
                if u + SLOTS < U:
                    gather(u + SLOTS)
                if u + ahead < U:
                    select(u + ahead)
                add(u)
                if other:
                    c, m = divmod(u, PATHC.tiles)
                    if c and m < len(SPANS):
                        other.add(c - 1, m)
            if other:
                for m in range(len(SPANS)):
                    other.add(PATHC.unroll - 1, m)
            added = adds[U - 1]
        S.meet()
        if other:
            other.store()
        M.at = space
        done = []
        per = P // path.nodes
        assert per == nb
        nbk = per // 4
        for n in range(NT * KC):
            j, k = divmod(n, KC)
            b0 = 4 + (n * nbk) % 4
            wait(pe, added, *([done[n - 4 // nbk]] if n >= 4 // nbk else []))
            for v in range(per):
                ins = pe.transpose(bank[b0 + v // 4][:, (v % 4) * P:(v % 4 + 1) * P],
                                   G[:, j * per + v, k * P:(k + 1) * P], ident[:])
            a = S.pe.done(ins)
            eng, tr = ((act, S.act), (dve, S.dve))[n % 2]
            wait(eng, a)
            for q in range(nbk):
                o = G[:, j * nb:(j + 1) * nb, k * P + q * 4 * path.nodes:k * P + (q + 1) * 4 * path.nodes]
                i_ = bank[b0 + q][:].rearrange("p (m b) -> p b m", b=nb)
                t = tr.done(act.copy(o, i_) if eng is act else dve.tensor_copy(o, i_))
            done.append(t)
        return done[-2:]

    def basis_lhs(nb, G, b):
        return lambda k, js: G[:, js[0] * nb:(js[0] + len(js)) * nb, k * P:(k + 1) * P].rearrange(
            "p (j b) n -> p j b n", b=nb)[:, :, b, :]

    def plain_lhs(xT):
        return lambda k, js: xT[:, k, js[0] * P:(js[0] + len(js)) * P].rearrange("p (j n) -> p j n", n=P)

    def split(src, hi, lo, low_engine, ready, free):
        wait(act, *ready, *free)
        a = S.act.done(act.copy(hi, src))
        engine, track = low_engine
        wait(engine, a)
        return track.done(engine.tensor_tensor(lo, src, hi.bitcast(F32), ALU.subtract))

    def split_matmul(acc, lhs, rhs, start, stop):
        pe.matmul(acc, lhs[0], rhs[0], start=start, stop=False)
        pe.matmul(acc, lhs[0], rhs[1], start=False, stop=False)
        return pe.matmul(acc, lhs[1], rhs[0], start=False, stop=stop)

    def transform(products, biases, ready, epilogue, before={}, beside=iter(())):
        ring = M.new("weight_ring", [P, 4, D])
        weight_parts = M.new("weight_parts", [P, 2, 2, D], F32R)
        lhs_parts = M.new("lhs_parts", [P, 2, 2, HALF, P], F32R)
        ring_free, parts_free = [None] * 4, [None] * 2
        banks_free, finish, prepared = None, None, {}
        wait(act, *ready)
        steps = [(half, m, k) for half in range(2) for m in range(len(products)) for k in range(KC)]

        def prepare(n):
            half, m, k = steps[n]
            if (half, k) == (0, 0) and m in before:
                before[m]()
            lhs, weight = products[m]
            r, s = n % 4, n % 2
            if ring_free[r]:
                wait(sp, ring_free[r])
            loaded = chunk_in[r].done(sp.dma_start(ring[:, r, :], weight[k * P:(k + 1) * P, :]))
            free = [parts_free[s]] if parts_free[s] else []
            lo = split(lhs(k, range(half * HALF, (half + 1) * HALF)), lhs_parts[:, s, 0], lhs_parts[:, s, 1],
                       (dve, S.dve), [], free)
            ring_free[r] = split(ring[:, r, :], weight_parts[:, s, 0, :], weight_parts[:, s, 1, :], (pool, S.pool),
                                 [loaded], free)
            next(beside, None)
            prepared[n] = lo, ring_free[r]

        prepare(0)
        for half in range(2):
            js = range(half * HALF, (half + 1) * HALF)
            for n in range(half * len(steps) // 2, (half + 1) * len(steps) // 2):
                _, m, k = steps[n]
                s = n % 2
                if n + 1 < len(steps):
                    prepare(n + 1)
                if finish and n == len(steps) // 2 + 1:
                    finish()
                wait(pe, *prepared[n])
                for j in js:
                    if m == 0 and k == 0 and banks_free:
                        wait(pe, banks_free[j % HALF])
                    ins = split_matmul(bank[j % HALF][:], [lhs_parts[:, s, q, j % HALF, :] for q in range(2)],
                                       [weight_parts[:, s, q, :] for q in range(2)], m == 0 and k == 0, False)
                parts_free[s] = S.pe.done(ins)
            for m, bias in enumerate(biases):
                wait(sp, *([free_row] if (half, m) != (0, 0) else []))
                a = misc_in.done(sp.dma_start(brow[:], bias.rearrange("(a d) -> a d", a=1)))
                wait(pe, a, *ready)
                for j in js:
                    ins = pe.matmul(bank[j % HALF][:], ones[0:1, :], brow[:], start=False,
                                    stop=m == len(biases) - 1)
                free_row = S.pe.done(ins)
            banks_free, finish = epilogue(list(js), free_row)
        if finish:
            finish()
        done = [S.now(t) for t in (S.pe, S.act, S.dve)]
        for engine in (pe, act, dve):
            wait(engine, *done)
        return done

    rows_of = lambda r, j: r[j * P:(j + 1) * P, :]

    M.at = after_edges
    G = M.new("G", [P, PATH0.windows + 1, D])
    after_G = M.at
    M.at = after_G + RINGS
    counting = CountSteps()
    for t in coefficients(PATH0, 8, [(coef["L0a"], 0, 4)]):
        pass
    wait(dve, t)
    M.at = after_G
    GT_done = aggregate(PATH0, 4, coef["L0a"], A["x"], G, counting)
    M.at = counting.at
    x = M.new("x", [P, NT, D])
    xT = M.new("xT", [P, KC, NP])
    h = M.new("h", [P, 2, D])
    wait(act, counting.stored)
    x_loaded = x_in.done(act.dma_start(x[:], A["x"].rearrange("(j p) d -> p j d", p=P)))
    xT_done = []
    hT = xT
    h_free = [None, None]
    h_stored, hT_done = [], []

    def transpose_x():
        wait(act, counting.stored)
        wait(dve, counting.stored)
        for j in range(NT):
            xT_done.append(transpose_tile(x[:, j, :], xT, j, 5 + j % 3, [x_loaded, ident_ready] +
                                          xT_done[max(0, j - 3):max(0, j - 2)]))
        wait(pe, *xT_done[-2:])

    def hidden(js, ready):
        freed = []
        for j in js:
            s = j % 2
            wait(act, ready, *([h_free[s][0], h_free[s][1]] if h_free[s] else []))
            freed.append(S.act.done(act.activation(h[:, s, :], bank[j % HALF][:], ACT.Relu)))
            wait(sp, freed[-1])
            o = tile_out[s].done(sp.dma_start(rows_of(hidden_rows, j), h[:, s, :]))
            h_stored.append(o)
            t = transpose_tile(h[:, s, :], hT, j, 6 + s, [freed[-1]] + (hT_done[-2:-1]))
            hT_done.append(t)
            h_free[s] = (o, t)
        return freed, None

    M.at = after_G
    products = [(basis_lhs(4, G, b), A["L0_gnn_basis0"][b]) for b in range(4)]
    hid = transform(products + [(plain_lhs(xT), A["L0_gnn_loop0"])], [A["L0_gnn_bias0"]], GT_done, hidden,
                    {4: transpose_x}, coefficients(PATH0, 8, [(coef["L0b"], 32, 4)]))
    assert M.at <= counting.at
    M.at = after_G

    GT_done = aggregate(PATH0, 4, coef["L0b"], hidden_rows, G)
    x_stored = []

    def residual_norm(rows):
        def epilogue(js, ready):
            freed = []
            wait(dve, ready)
            for j in js:
                freed.append(S.dve.done(dve.tensor_tensor(x[:, j, :], bank[j % HALF][:], x[:, j, :], ALU.add)))

            def finish():
                for j, t in zip(js, normalize([x[:, j, :] for j in js], freed, [x[:, j, :] for j in js])):
                    wait(act, t)
                    x_stored.append(x_out.done(act.dma_start(rows_of(rows, j), x[:, j, :])))
            return freed, finish
        return epilogue

    products = [(basis_lhs(4, G, b), A["L0_gnn_basis1"][b]) for b in range(4)]
    nrm = transform(products + [(plain_lhs(hT), A["L0_gnn_loop1"])], [A["L0_gnn_bias1"]], GT_done + hT_done[-2:],
                    residual_norm(x1_rows),
                    {}, coefficients(PATH1, 32, [(coef["L1"], 64, 8)]))

    M.at = after_layer1_edges
    S.meet()
    G = M.new("G1", [P, PATH1.windows + 1, D])
    keep1 = M.at
    GT_done = aggregate(PATH1, 8, coef["L1"], x1_rows, G)
    M.at = keep1
    ring_at = M.at
    M.at = after_constants
    xt = M.new("x_tiles", [P, HALF, D])
    assert M.at <= after_layer1_edges
    M.at = ring_at
    x2_stored = {}

    def load_x1(j, free):
        wait(sp, *free)
        return tile_in[j % HALF].done(sp.dma_start(xt[:, j % HALF, :], rows_of(x1_rows, j)))

    x1_loaded = {j: load_x1(j, []) for j in range(HALF)}

    def layer1(js, ready):
        freed = []
        wait(dve, ready)
        for j in js:
            wait(dve, x1_loaded[j])
            freed.append(S.dve.done(dve.tensor_tensor(xt[:, j % HALF, :], bank[j % HALF][:], xt[:, j % HALF, :],
                                                      ALU.add)))

        def finish():
            for j, t in zip(js, normalize([xt[:, j % HALF, :] for j in js], freed, [xt[:, j % HALF, :] for j in js])):
                wait(act, t)
                x2_stored[j] = tile_out[j % HALF].done(act.dma_start(rows_of(x2_rows, j), xt[:, j % HALF, :]))
            for j in js:
                if j + HALF < NT:
                    x1_loaded[j + HALF] = load_x1(j + HALF, [x2_stored[j]])
        return freed, finish

    products = [(basis_lhs(8, G, b), A["L1_gnn_bases"][b]) for b in range(8)]
    fin1 = transform(products, [A["L1_gnn_h_bias"]], GT_done, layer1)

    M.at = after_constants
    x = M.new("x_L2", [P, NT, D])
    condT, condR = split_in_place(M, "condT", [STACKED, NP])
    mod_raw = M.new("modulation_loaded", [STACKED, 2, D])
    count = M.new("count_by_src", [P, NT, NP])
    keep2 = M.at
    counted = M.new("count_by_dst", [P, NT, NP])
    xT = M.new("xT_L2", [P, KC, NP])
    aggT = M.new("aggT", [P, KC, NP])
    rdeg = M.new("rdeg", [P, NT])
    ring = M.new("weight_ring2", [P, 2, KC, D])
    brows = M.new("bias_rows2", [1, 2, D])
    wait(sp, *fin1)
    count_loaded = [count_in[j].done(sp.dma_start(counted[:, j, :], count_rows[:, j * NP:(j + 1) * NP]))
                    for j in range(NT)]
    wait(sp, *x2_stored.values())
    x_loaded = x_in.done(sp.dma_start(x[:], x2_rows.rearrange("(j p) d -> p j d", p=P)))
    w1_in = [chunk_in[m].done(sp.dma_start(ring[:, m, :, :], A[name].rearrange("(k p) d -> p k d", p=P)))
             for m, name in enumerate(("L2_gnn_W1", "L2_gnn_W2"))]
    for m, name in enumerate(("L2_gnn_b1", "L2_gnn_b2")):
        b_in = misc_in.done(sp.dma_start(brows[:, m, :], A[name].rearrange("(a d) -> a d", a=1)))
    turned = []
    for j in range(NT):
        wait(pe, count_loaded[j])
        for i0 in range(0, NT, 4):
            n, many = len(turned), min(4, NT - i0)
            b = 4 + n % 4
            if n >= 4:
                wait(pe, turned[n - 4])
            for q in range(many):
                ins = pe.transpose(bank[b][:, q * P:(q + 1) * P], counted[:, j, (i0 + q) * P:(i0 + q + 1) * P],
                                   ident[:])
            a = S.pe.done(ins)
            eng, tr = ((act, S.act), (dve, S.dve))[n % 2]
            wait(eng, a)
            o = count[:, i0:i0 + many, j * P:(j + 1) * P]
            i_ = bank[b][:, 0:many * P].rearrange("p (q n) -> p q n", n=P)
            turned.append(tr.done(act.copy(o, i_) if eng is act else dve.tensor_copy(o, i_)))
    count_turned = S.now(S.pe)
    xT_done = []
    for j in range(NT):
        xT_done.append(transpose_tile(x[:, j, :], xT, j, j % 4, [x_loaded] + xT_done[max(0, j - 4):max(0, j - 3)]))
    wait(pe, *xT_done[-2:], *turned[-2:])
    for j in range(NT):
        for i in range(NT):
            ins = pe.matmul(bank[0][:, j:j + 1], count[:, i, j * P:(j + 1) * P], ones[:, 0:1],
                            start=i == 0, stop=i == NT - 1)
    a = S.pe.done(ins)
    wait(dve, a)
    a = S.dve.done(dve.tensor_scalar(rdeg[:], bank[0][:, 0:NT], 1.0, None, ALU.max))
    wait(dve, a)
    rdeg_ready = S.dve.done(dve.reciprocal(rdeg[:], rdeg[:]))
    spans = [(c, min(512, NP - c)) for c in range(0, NP, 512)]
    free = {}
    n = 0
    end, M.at = M.at, keep2
    S.dve.done(dve.memset(mod_raw[:], 0.0))
    condition = conditioning(A, S, M, bank, condT, condR, misc_in, [count_turned] + turned[-2:])
    next(condition)
    after_conditioning, M.at = M.at, end
    for k in range(KC):
        if k:
            next(condition, None)
        for c, width in spans:
            b = 1 + n % 3
            if b in free:
                wait(pe, free[b])
            for i in range(NT):
                ins = pe.matmul(bank[b][:, 0:width], x[:, i, k * P:(k + 1) * P], count[:, i, c:c + width],
                                start=i == 0, stop=i == NT - 1)
            a = S.pe.done(ins)
            eng, tr = ((act, S.act), (dve, S.dve))[n % 2]
            wait(eng, a)
            o, i_ = aggT[:, k, c:c + width], bank[b][:, 0:width]
            free[b] = tr.done(act.copy(o, i_) if eng is act else dve.tensor_copy(o, i_))
            n += 1
    agg_done = list(free.values())
    aggregated = S.now(S.pe)
    M.at = after_conditioning
    prepare_mask(S, M, count, [aggregated])
    assert M.at <= keep2 + 4 * NT * NP

    wait(pe, *w1_in, b_in, rdeg_ready, *agg_done, *xT_done[-2:])
    wait(dve, rdeg_ready)
    last_ln = []
    for half in range(2):
        js = list(range(half * HALF, (half + 1) * HALF))
        wait(pe, *last_ln)
        for j in js:
            for k in range(KC):
                pe.matmul(bank[j % HALF][:], xT[:, k, j * P:(j + 1) * P], ring[:, 0, k, :], start=k == 0, stop=False)
            for m in range(2):
                ins = pe.matmul(bank[j % HALF][:], ones[0:1, :], brows[:, m, :], start=False, stop=m == 1)
        a = S.pe.done(ins)
        wait(dve, a)
        for j in js:
            t = S.dve.done(dve.tensor_tensor(x[:, j, :], x[:, j, :], bank[j % HALF][:], ALU.add))
        for n_, j in enumerate(js):
            b = 5 + n_ % 3
            if n_ >= 3:
                wait(pe, scaled[n_ - 3])
            else:
                scaled = scaled if n_ else []
            for k in range(KC):
                ins = pe.matmul(bank[b][:], aggT[:, k, j * P:(j + 1) * P], ring[:, 1, k, :],
                                start=k == 0, stop=k == KC - 1)
            a = S.pe.done(ins)
            wait(dve, a, t)
            scaled.append(S.dve.done(dve.scalar_tensor_tensor(
                x[:, j, :], bank[b][:], rdeg[:, j:j + 1], x[:, j, :], ALU.mult, ALU.add)))
        last_ln = normalize([x[:, j, :] for j in js], scaled, [x[:, j, :] for j in js])
        for j, t in zip(js, last_ln):
            wait(sp, t)
            x_start_stored = out_done.done(sp.dma_start(rows_of(x1_rows, j), x[:, j, :]))

    M.at = keep2
    attention_blocks(nc, A, out, S, M, bank, count, x, ident, mod_raw,
         x1_rows, x_start_stored, condR, weights_in, projected, misc_in, out_done, last_ln, normalize)


def prepare_mask(S, M, count, ready):
    wait, act, dve = S.wait, S.nc.scalar, S.nc.vector
    low, logs = M.new("missing", [P, 2, N]), {}
    wait(dve, *ready)
    for j in range(NT + 1):
        if j < NT:
            c = count[:, j, 0:N]
            a = S.dve.done(dve.tensor_scalar(low[:, j % 2, :], c, 1.0, 1.0, ALU.min, ALU.subtract))
            wait(dve, a)
            b = S.dve.done(dve.tensor_scalar(c, c, 1.0, None, ALU.max))
            wait(act, b)
            logs[j] = S.act.done(act.activation(c, c, ACT.Ln))
        if j:
            c = count[:, j - 1, 0:N]
            wait(dve, logs[j - 1])
            b = S.dve.done(dve.scalar_tensor_tensor(c, low[:, (j - 1) % 2, :], NEG, c, ALU.mult, ALU.add))
            wait(dve, b)


def conditioning(A, S, M, bank, condT, condR, misc_in, ready):
    wait, nc = S.wait, S.nc
    pe, act, dve, pool, sp = nc.tensor, nc.scalar, nc.vector, nc.gpsimd, nc.sync
    spans = SPANS
    ang = M.new("angle", [2 * FREQ, NP])
    turn = M.new("turn", [2 * FREQ, NP])
    emb = M.new("embT", [2 * FREQ, NP])
    kf = M.new("k_float", [2 * FREQ, 1])
    ki = M.new("k_int", [2 * FREQ, 1], I32)
    quarter = M.new("quarter", [2 * FREQ, 1])
    fw1 = M.new("f_w1", [2 * FREQ, COND])
    fw2 = M.new("f_w2", [COND, COND])
    fb = M.new("f_b", [COND, 2])
    hid = M.new("cond_hidden", [COND, NP])
    sig = M.new("cond_sigmoid", [COND, NP])
    for engine in (pool, sp, dve, act):
        wait(engine, *ready)
    for h in range(2):
        a = S.pool.done(pool.iota(ki[h * FREQ:(h + 1) * FREQ, :], pattern=[[0, 1]], base=1, channel_multiplier=1))
    node = A["node_vec1"]
    misc_in.done(sp.dma_start(ang[:], bass.AP(tensor=node.tensor, offset=node.offset, ap=[[0, 2 * FREQ], [1, NP]])))
    misc_in.done(sp.dma_start(fw1[:], A["L3_gnn_f_w1"]))
    misc_in.done(sp.dma_start(fw2[:], A["L3_gnn_f_w2"]))
    misc_in.done(sp.dma_start(fb[:, 0:1], A["L3_gnn_f_b1"].rearrange("(c a) -> c a", a=1)))
    t = misc_in.done(sp.dma_start(fb[:, 1:2], A["L3_gnn_f_b2"].rearrange("(c a) -> c a", a=1)))
    wait(dve, a, t)
    a = S.dve.done(dve.tensor_copy(kf[:], ki[:]))
    b = S.dve.done(dve.memset(quarter[0:FREQ, :], 0.0))
    b = S.dve.done(dve.memset(quarter[FREQ:2 * FREQ, :], 0.25))
    one = S.dve.done(dve.memset(condT[:], 1.0))
    wait(dve, a, b, one)
    a = S.dve.done(dve.tensor_scalar(kf[:], kf[:], 1.0 / 16, None, ALU.mult))
    wait(dve, a)
    a = S.dve.done(dve.tensor_scalar(ang[:], ang[:], kf[:], quarter[:], ALU.mult, ALU.add))
    wait(dve, a)
    magic = 1.5 * 2.0 ** 23
    a = S.dve.done(dve.tensor_scalar(turn[:], ang[:], magic, None, ALU.add))
    wait(dve, a)
    a = S.dve.done(dve.tensor_scalar(turn[:], turn[:], magic, None, ALU.subtract))
    wait(dve, a)
    a = S.dve.done(dve.tensor_tensor(ang[:], ang[:], turn[:], ALU.subtract))
    wait(act, a)
    emb_ready = S.act.done(act.activation(emb[:], ang[:], ACT.Sin, scale=6.283185))
    cond_hi = M.new("condT_hi", [STACKED, NP], F32R)
    yield
    wait(pe, emb_ready, one)
    for m, (wt, src, K) in enumerate(((fw1, emb, 2 * FREQ), (fw2, hid, COND))):
        for n, (c, width) in enumerate(spans):
            ins = pe.matmul(bank[4 + n][0:COND, 0:width], wt[:], src[:, c:c + width], start=True, stop=True)
        a = S.pe.done(ins)
        wait(act, a)
        dst = hid if m == 0 else condT[0:COND, :]
        for n, (c, width) in enumerate(spans):
            t = S.act.done(act.activation(dst[:, c:c + width], bank[4 + n][0:COND, 0:width], ACT.Identity,
                                          bias=fb[:, m:m + 1]))
        if m == 0:
            wait(act, t)
            t = S.act.done(act.activation(sig[:], hid[:], ACT.Exp, scale=-1.0))
            wait(dve, t)
            a = S.dve.done(dve.tensor_scalar(sig[:], sig[:], 1.0, None, ALU.add))
            wait(dve, a)
            a = S.dve.done(dve.reciprocal(sig[:], sig[:]))
            wait(dve, a)
            t = S.dve.done(dve.tensor_tensor(hid[:], hid[:], sig[:], ALU.mult))
        yield
        wait(pe, t)
    wait(sp, t)
    for to in STACK[1:]:
        a = misc_in.done(sp.dma_start(condT[to:to + COND + 1, :], condT[0:COND + 1, :]))
    wait(act, a)
    a = S.act.done(act.copy(cond_hi[:], condT[:]))
    wait(dve, a)
    mid = slice(STACK[1], STACK[2])
    a = S.dve.done(dve.tensor_tensor(condR[mid, :], condT[mid, :], cond_hi[mid, :].bitcast(F32), ALU.subtract))
    for rows in (slice(0, STACK[1]), slice(STACK[2], STACKED)):
        a = S.dve.done(dve.tensor_copy(condR[rows, :], cond_hi[rows, :].bitcast(F32)))
    yield


def attention_blocks(nc, A, out, S, M, bank, count, x, ident, mod_raw,
                     x_start, x_start_stored, condR, weights_in, projected, misc_in, out_done, last_ln, normalize):
    wait, prev = S.wait, S.wait_previous
    pe, act, dve, pool, sp = nc.tensor, nc.scalar, nc.vector, nc.gpsimd, nc.sync
    scale = DH ** -0.5
    spans = [(c, min(512, NP - c)) for c in range(0, NP, 512)]
    seen = [(c, min(512, N - c)) for c in range(0, N, 512)]

    for engine in (pe, act, dve, pool, sp):
        wait(engine, S.now(S.pe), S.now(S.act))
    xin = M.new("x_start", [P, NT, D])
    M.at -= 4 * NT * D
    yT = [M.new("yT_hi", [P, KC, NP], F32R)]
    lhs_place = M.at
    yT.append(M.new("yT_lo", [P, KC, NP], F32R))
    attnT = M.new("attnT", [P, HEADS, NP])
    big, big_lo = ([t, None] for t in split_in_place(M, "product_weights", [P, KC, D]))
    modw = M.new("modulation_parts", [STACKED, 2, D], F32R)
    bias_rows = M.new("bias_rows", [P, 2, D])
    stats = M.new("x_stats", [P, NT, 6])
    means = M.new("x_mean_var", [P, NT, 2])
    rstds = M.new("x_rstd", [P, NT, 1])
    shifts = M.new("x_shift", [P, NT, 1])
    hb = M.new("head_bias_cols", [P, 2])
    mb = M.new("mlp_bias_cols", [P, KC])
    y = M.new("y_tile", [P, 2, D])
    hw, hw_lo = split_in_place(M, "head_weights", [P, 2, KC, DH])
    hw_hi = M.new("head_weights_hi", [P, 2, KC, DH], F32R)
    v_bias = M.new("v_bias_rows", [P, D])
    PT = M.new("probT", [P, NT, P])
    rmax = M.new("row_max", [P, 2])
    nmax = M.new("negated_max", [P, 2])
    smax = M.new("span_max", [P, 2, 3])
    rsum = M.new("row_sum", [P, 2])
    has = M.new("has_edges", [P, 2])
    heads_only = M.at
    qT, kT = M.new("qT", [P, NP]), M.new("kT", [P, NP])
    v = M.new("v", [P, NT, DH])
    prob = M.new("prob", [P, 2, N])
    M.at = heads_only
    big_hi = [M.new("product_weights_hi", [P, KC, D], F32R) for _ in range(2)]
    big[1], big_lo[1] = split_in_place(M, "product_weights", [P, KC, D])
    M.at = lhs_place
    lhs_parts = M.new("lhs_parts", [P, 2, 2, KC, P], F32R)

    def split_weights(src, hi, lo, ready):
        wait(pool, *ready)
        wait(pool, S.pool.done(pool.tensor_copy(hi, src)))
        return S.pool.done(pool.tensor_tensor(lo, src, hi.bitcast(F32), ALU.subtract))

    def split_matmul(acc, lhs, rhs, start, stop):
        pe.matmul(acc, lhs[0], rhs[0], start=start, stop=False)
        pe.matmul(acc, lhs[0], rhs[1], start=False, stop=False)
        return pe.matmul(acc, lhs[1], rhs[0], start=False, stop=stop)

    def load_modulation(stage):
        for m, n in enumerate((("s1", "b1"), ("s2", "b2"))[stage]):
            for to in STACK:
                weights_in["modulation"].done(sp.dma_start(
                    mod_raw[to:to + COND, m, :], A[f"L3_gnn_{n}_w"][ds(i, 1), :, :].rearrange("a c d -> (a c) d")))
                t = weights_in["modulation"].done(sp.dma_start(
                    mod_raw[to + COND:to + COND + 1, m, :], A[f"L3_gnn_{n}_b"][ds(i, 1), :]))
        return t

    def split_modulation(stage, loaded):
        wait(pool, loaded)
        wait(pool, S.pool.done(pool.tensor_copy(modw[:], mod_raw[:])))
        low = slice(STACK[2], STACKED)
        t = S.pool.done(pool.tensor_tensor(modw[low], mod_raw[low], modw[low].bitcast(F32), ALU.subtract),
                        f"modulation{stage}")
        wait(pool, t)
        return t

    def row_statistics(j, ready):
        wait(dve, ready)
        return S.dve.done(dve.bn_stats(stats[:, j, :], x[:, j, :]))

    def finish_statistics(a, b):
        for j in range(a, b):
            t = S.dve.done(dve.bn_aggr(means[:, j, :], stats[:, j, :]))
        wait(dve, t)
        t = S.dve.done(dve.tensor_scalar_add(rstds[:, a:b, :], means[:, a:b, 1:2], EPS))
        wait(act, t)
        t = S.act.done(act.activation(rstds[:, a:b, :], rstds[:, a:b, :], ACT.Sqrt))

        def end():
            wait(dve, t)
            wait(dve, S.dve.done(dve.reciprocal(rstds[:, a:b, :], rstds[:, a:b, :])))
            return S.dve.done(dve.scalar_tensor_tensor(shifts[:, a:b, :], means[:, a:b, 0:1], -1.0, rstds[:, a:b, :],
                                                       ALU.mult, ALU.mult))
        return end

    def modulate(stage, ready, end_statistics):
        wait(pe, modulation_split[stage], *ready)
        wait(act, end_statistics(), *ready)
        conditioned, normed, added, y_free = {}, {}, {}, {}
        xn = [attnT[:, :, :].rearrange("p h n -> p (h n)")[:, j * D:(j + 1) * D] for j in range(NT)]

        def condition(j):
            if j >= 2:
                wait(pe, added[j - 2])
            for m in range(2):
                ins = pe.matmul(bank[2 * (j % 2) + m][:], condR[:, j * P:(j + 1) * P], modw[:, m, :],
                                start=True, stop=True)
            conditioned[j] = S.pe.done(ins, f"conditioned{stage}")

        def norm(j):
            normed[j] = S.act.done(act.activation(xn[j], x[:, j, :], ACT.Identity, bias=shifts[:, j, :],
                                                  scale=rstds[:, j, :]))

        def split_tile(j):
            b, cols = 4 + j % 4, slice(j * P, (j + 1) * P)
            got = bank[b][:].rearrange("p (k n) -> p k n", k=KC)
            wait(act, turned[j])
            wait(dve, S.act.done(act.copy(yT[0][:, :, cols], got)))
            y_free[j] = S.dve.done(dve.tensor_tensor(yT[1][:, :, cols], got, yT[0][:, :, cols].bitcast(F32),
                                                     ALU.subtract))

        turned = {}
        condition(0)
        norm(0)
        norm(1)
        for j in range(NT):
            s = j % 2
            if j + 1 < NT:
                condition(j + 1)
            wait(dve, conditioned[j], normed[j], *([turned[j - 2]] if j >= 2 else []))
            a = S.dve.done(dve.scalar_tensor_tensor(y[:, s, :], bank[2 * s][:], 1.0, xn[j], ALU.add, ALU.mult))
            wait(dve, a)
            added[j] = S.dve.done(dve.tensor_tensor(y[:, s, :], y[:, s, :], bank[2 * s + 1][:], ALU.add))
            wait(pe, added[j], *([y_free[j - 4]] if j >= 4 else []))
            for k in range(KC):
                ins = pe.transpose(bank[4 + j % 4][:, k * P:(k + 1) * P], y[:, s, k * P:(k + 1) * P], ident[:])
            turned[j] = S.pe.done(ins)
            if j + 2 < NT:
                norm(j + 2)
            if j:
                split_tile(j - 1)
        split_tile(NT - 1)
        return y_free, added[NT - 1], conditioned[NT - 1]

    def add_product(stage, lhs, ready, loaded, weights_ready):
        wait(pe, weights_ready)
        wait(dve, *loaded)
        for j in range(NT):
            biased = S.dve.done(dve.tensor_tensor(x[:, j, :], x[:, j, :], bias_rows[:, stage, :], ALU.add),
                                f"biased{stage}")
        done, products = [], []
        for j in range(NT):
            b, s = j % 4, j % 2
            wait(act, *ready(j), *([products[j - 2]] if j >= 2 else []))
            hi, lo = lhs_parts[:, s, 0], lhs_parts[:, s, 1]
            wait(pool, S.act.done(act.copy(hi, lhs[:, :, j * P:(j + 1) * P])))
            a = S.pool.done(pool.tensor_tensor(lo, lhs[:, :, j * P:(j + 1) * P], hi.bitcast(F32), ALU.subtract))
            wait(pe, a, *([done[j - 4]] if j >= 4 else []))
            for k in range(KC):
                ins = split_matmul(bank[b][:], [lhs_parts[:, s, q, k, :] for q in range(2)],
                                   [big_hi[0][:, k, :], big_lo[0][:, k, :]], k == 0, k == KC - 1)
            a = S.pe.done(ins, f"product{stage}")
            products.append(a)
            wait(dve, a, biased)
            done.append(S.dve.done(dve.tensor_tensor(x[:, j, :], x[:, j, :], bank[b][:], ALU.add)))
            if j:
                measured = row_statistics(j - 1, done[j - 1])
            if j == NT - 2:
                wait(dve, measured)
                end_first = finish_statistics(0, j)
        end_first()
        wait(dve, row_statistics(NT - 1, done[NT - 1]))
        return a, done[-1], finish_statistics(NT - 2, NT)

    def load_product_weight(slot, weight, free):
        wait(sp, *free)
        return weights_in[f"product{slot}"].done(sp.dma_start(
            big[slot][:], weight[ds(i, 1), :, :].rearrange("a (k p) d -> p (a k) d", p=P)))

    def broadcast(row, n):
        return bass.AP(tensor=row.tensor, offset=row.offset, ap=[[0, P], [1, n]])

    def load_queries_keys(h):
        for m, n in enumerate("qk"):
            wt = A[f"L3_gnn_w{n}"][ds(i, 1), :, ds(h * DH, DH)].rearrange("a (k p) d -> p (a k) d", p=P)
            weights_in["queries_keys"].done(sp.dma_start(hw[:, m, :, :], wt))
            t = weights_in["queries_keys"].done(sp.dma_start(
                hb[:, m:m + 1], A[f"L3_gnn_b{n}"][ds(i, 1), ds(h * DH, DH)].rearrange("a d -> d a"),
                allow_slow_non_contiguous=True))
        return t

    def load_values():
        weights_in["values"].done(sp.dma_start(
            big[1][:], A["L3_gnn_wv"][ds(i, 1), :, :].rearrange("a (k p) d -> p (a k) d", p=P)))
        return weights_in["values"].done(sp.dma_start(v_bias[:], broadcast(A["L3_gnn_bv"][ds(i, 1), :], D)))

    def project_values(loaded, split_ready, y_ready, banks_ready):
        wait(pe, split_ready, banks_ready)
        wait(dve, loaded)
        done = []
        for j in range(NT):
            wait(pe, y_ready[j], *([done[j - 4]] if j >= 4 else []))
            for k in range(KC):
                ins = split_matmul(bank[j % 4][:], [part[:, k, j * P:(j + 1) * P] for part in yT],
                                   [big_hi[1][:, k, :], big_lo[1][:, k, :]], k == 0, k == KC - 1)
            wait(dve, S.pe.done(ins))
            track = projected[1] if j == NT - 1 else S.dve
            done.append(track.done(dve.tensor_tensor(
                attnT[:, :, j * P:(j + 1) * P], bank[j % 4][:].rearrange("p (h n) -> p h n", n=DH),
                v_bias[:].rearrange("p (h n) -> p h n", n=DH), ALU.add), "projected"))
        return done[-4:]

    def scale_query_bias(t):
        wait(dve, t)
        return S.dve.done(dve.tensor_scalar(hb[:, 0:1], hb[:, 0:1], scale, None, ALU.mult))

    def project_queries_keys(parts, split_ready, scaled, free, ready):
        for m, n in parts:
            c, width = spans[n]
            wait(pe, split_ready, *(free[n] if n in free else ready(n)))
            for k in range(KC):
                ins = split_matmul(bank[n][:, 0:width], [hw_hi[:, m, k, :], hw_lo[:, m, k, :]],
                                   [part[:, k, c:c + width] for part in yT], k == 0, k == KC - 1)
            a = S.pe.done(ins)
            wait(act, a, scaled)
            track = projected[0] if (m, n) == (1, 2) else S.act
            free[n] = [track.done(act.activation((qT, kT)[m][:, c:c + width], bank[n][:, 0:width], ACT.Identity,
                                                 bias=hb[:, m:m + 1], scale=(scale, 1.0)[m]), "projected")]

    def attention(h, more):
        begin = S.before if more else S.now
        queries_keys_ready, values_left = begin(projected[0]), begin(S.pe)
        if more:
            wait(sp, queries_keys_ready)
            more_loaded = load_queries_keys(h + 1)
            more_split = split_weights(hw[:], hw_hi[:], hw_lo[:], [more_loaded])

        def scores(j):
            for n_, (c, width) in enumerate(seen):
                ins = pe.matmul(bank[n_][:, 0:width], qT[:, j * P:(j + 1) * P], kT[:, c:c + width],
                                start=True, stop=True)
            return S.pe.done(ins)

        wait(act, values_left)
        v_ready = S.act.done(act.copy(v[:].rearrange("p q n -> p (q n)"),
                                      attnT[:, ds(h, 1), :].rearrange("p a n -> p (a n)")))

        masked, scaled, turned, moved, mult, left = {}, {}, {}, {}, {}, {}
        for t in range(NT + 2):
            if t >= 2:
                j, s = t - 2, t % 2
                wait(pe, scaled[j], *([moved[j - 1]] if j else []))
                for q in range(NT):
                    width = min(P, N - q * P)
                    ins = pe.transpose(bank[3 + q // 4][0:width, (q % 4) * P:(q % 4 + 1) * P],
                                       prob[:, s, q * P:q * P + width], ident[:])
                turned[j] = S.pe.done(ins)
                wait(act, turned[j], *([mult[j - 1]] if j else []))
                for g, w_ in ((0, 4), (1, 4), (2, 1)):
                    S.act.done(act.copy(PT[:, 4 * g:4 * g + w_, :],
                                        bank[3 + g][:, 0:w_ * P].rearrange("p (q n) -> p q n", n=P)))
                w_ = N - (NT - 1) * P
                moved[j] = S.act.done(act.copy(PT[0:w_, NT - 1, :], bank[5][0:w_, P:2 * P]))
            if 1 <= t <= NT:
                j, s = t - 1, (t - 1) % 2
                wait(dve, exped_before)
                a = S.dve.done(dve.reciprocal(rsum[:, s:s + 1], rsum[:, s:s + 1]))
                wait(dve, a)
                a = S.dve.done(dve.tensor_tensor(rsum[:, s:s + 1], rsum[:, s:s + 1], has[:, s:s + 1], ALU.mult))
                wait(dve, a)
                scaled[j] = S.dve.done(dve.tensor_scalar(prob[:, s, :], prob[:, s, :], rsum[:, s:s + 1], None,
                                                         ALU.mult))
            if t < NT:
                j, s = t, t % 2
                wait(pe, masked[j - 1] if j else queries_keys_ready)
                scored = scores(j)
                wait(dve, scored, *([turned[j - 2]] if j >= 2 else []))
                for n_, (c, width) in enumerate(seen):
                    S.dve.done(dve.tensor_tensor_reduce(
                        out=prob[:, s, c:c + width], in0=bank[n_][:, 0:width], in1=count[:, j, c:c + width],
                        scale=1.0, scalar=-2.0 * NEG, op0=ALU.add, op1=ALU.max, accum_out=smax[:, s, n_:n_ + 1]))
                masked[j] = a = Token(S.dve, S.frames[-1], S.dve.base, S.dve.off)
                wait(dve, a)
                a = S.dve.done(dve.reduce_max(rmax[:, s:s + 1], smax[:, s, :], AX.X))
                wait(dve, a)
                S.dve.done(dve.tensor_scalar(has[:, s:s + 1], rmax[:, s:s + 1], -0.5 * NEG, None, ALU.is_gt))
                a = S.dve.done(dve.tensor_scalar(nmax[:, s:s + 1], rmax[:, s:s + 1], -1.0, None, ALU.mult))
                wait(act, a)
                exped = S.act.done(act.activation(prob[:, s, :], prob[:, s, :], ACT.Exp, bias=nmax[:, s:s + 1],
                                                  accum_out=rsum[:, s:s + 1]))
            exped_before = exped
            if more and t >= NT:
                if t == NT:
                    more_scaled, free = scale_query_bias(more_loaded), {}
                    wait(act, scored)
                m = t - NT
                project_queries_keys([(m, n) for n in range(3)], more_split, more_scaled, free,
                                     lambda n: [masked[NT - 1]])
            if t >= 2:
                j, s = t - 2, t % 2
                wait(pe, moved[j], v_ready, *([left[j - 2]] if j >= 2 else []))
                for q in range(NT):
                    width = min(P, N - q * P)
                    ins = pe.matmul(bank[6 + s][:, 0:P], v[0:width, q, :], PT[0:width, q, :],
                                    start=q == 0, stop=q == NT - 1)
                mult[j] = S.pe.done(ins, "values")
                wait(act, mult[j])
                left[j] = S.act.done(act.copy(attnT[:, ds(h, 1), j * P:(j + 1) * P].rearrange("p a n -> p (a n)"),
                                              bank[6 + s][:, 0:P]), "attended")
        return left, scored, turned[NT - 1]

    for j in range(NT):
        t = row_statistics(j, last_ln[-1])
    wait(dve, t)
    finish_statistics(0, NT)()
    wait(dve, x_start_stored)
    with S.loop(BLOCKS) as i:
        prev(sp, S.pool, "modulation1")
        modulation_loaded = load_modulation(0)
        prev(pool, S.pe, "conditioned1")
        modulation_split = [split_modulation(0, modulation_loaded), None]
        wait(sp, S.before(projected[0]), S.before(projected[1]))
        loaded_qk = load_queries_keys(0)
        split_qk = split_weights(hw[:], hw_hi[:], hw_lo[:], [loaded_qk])
        prev(sp, S.pe, "hidden")
        loaded_values = load_values()
        split_values = split_weights(big[1][:], big_hi[1][:], big_lo[1][:], [loaded_values])
        prev(sp, S.pe, "product1")
        loaded = [load_product_weight(0, A["L3_gnn_wo"], []), None]
        prev(sp, S.act, "hidden")
        weights_in["bias"].done(sp.dma_start(
            mb[:], A["L3_gnn_m_b1"][ds(i, 1), :].rearrange("a (k p) -> p (a k)", p=P), allow_slow_non_contiguous=True))
        prev(sp, S.dve, "biased1")
        for stage, n in enumerate(("bo", "m_b2")):
            loaded_bias = weights_in["bias"].done(sp.dma_start(bias_rows[:, stage, :],
                                                               broadcast(A["L3_gnn_" + n][ds(i, 1), :], D)))

        wait(pe, S.before(S.dve), S.before(S.act))
        wait(sp, modulation_split[0])
        modulation_loaded = load_modulation(1)
        y_ready, modulated, conditioned = modulate(0, [], lambda: S.before(S.dve))
        scaled = scale_query_bias(loaded_qk)
        wait(pool, conditioned)
        modulation_split[1] = split_modulation(1, modulation_loaded)
        v_projected = project_values(loaded_values, split_values, y_ready, modulated)
        parts = [(m, n) for n in range(3) for m in range(2)]
        project_queries_keys(parts, split_qk, scaled, {}, lambda n: v_projected)
        with S.loop(HEADS - 1) as h:
            attention(h, True)
        left, scored, turned = attention(HEADS - 1, False)
        hidden_loaded = load_product_weight(1, A["L3_gnn_m_w1"], [turned])
        wo_split = split_weights(big[0][:], big_hi[0][:], big_lo[0][:], [loaded[0], scored])
        product, added, end_statistics = add_product(0, attnT, lambda j: [left[j], left[NT - 1]], [loaded_bias], wo_split)
        w1_split = split_weights(big[1][:], big_hi[1][:], big_lo[1][:], [hidden_loaded, left[NT - 1]])
        wait(sp, product)
        w2_split = split_weights(big[0][:], big_hi[0][:], big_lo[0][:], [load_product_weight(0, A["L3_gnn_m_w2"], []), product])

        y_ready, modulated, conditioned = modulate(1, [added], end_statistics)
        wait(pe, w1_split, modulated)
        wait(act, loaded_bias)
        n, free = 0, {}
        for m, (c, width) in enumerate(spans):
            wait(pe, y_ready[min(4 * m + 3, NT - 1)])
            for o in range(KC):
                b = n % 4
                if b in free:
                    wait(pe, free[b])
                for k in range(KC):
                    cols = slice(o * P, (o + 1) * P)
                    ins = split_matmul(bank[b][:, 0:width], [big_hi[1][:, k, cols], big_lo[1][:, k, cols]],
                                       [part[:, k, c:c + width] for part in yT], k == 0, k == KC - 1)
                a = S.pe.done(ins, "hidden")
                wait(act, a)
                free[b] = relu = S.act.done(act.activation(attnT[:, o, c:c + width], bank[b][:, 0:width], ACT.Relu,
                                                           bias=mb[:, o:o + 1]), "hidden")
                n += 1
            hidden_done = {**(hidden_done if m else {}), m: relu}
        _, added, end_statistics = add_product(1, attnT, lambda j: [hidden_done[j // 4]] + list(free.values()),
                                               [loaded_bias], w2_split)
        end_statistics()

    wait(sp, S.now(S.pe), S.now(S.act))
    t = misc_in.done(sp.dma_start(xin[:], x_start.rearrange("(j p) d -> p j d", p=P)))
    wait(dve, t, S.now(S.dve))
    a = S.dve.done(dve.tensor_tensor(x[:], x[:], xin[:], ALU.add))
    for half in range(2):
        js = list(range(half * HALF, (half + 1) * HALF))
        for j, t in zip(js, normalize([x[:, j, :] for j in js], [a], [x[:, j, :] for j in js])):
            rows = min(P, N - j * P)
            wait(sp, t)
            o = out_done.done(sp.dma_start(out[j * P:j * P + rows, :], x[0:rows, j, :]))
            a = t
    wait(sp, o)


EDGE_INPUTS = ("src", "dst", "edge_type_8", "edge_type_32", "edge_weight", "edge_weight1")


def kernel(**inputs):
    import numpy as np
    import concourse.bacc as bacc
    from concourse.bass_utils import run_bass_kernel_spmd

    arrays = {}
    for name, a in inputs.items():
        a = np.ascontiguousarray(a)
        if name in EDGE_INPUTS:
            flat = np.full(T * P + (name == "dst"), PAD_DST if name == "dst" else 0, a.dtype)
            flat[:E] = a.reshape(-1)
            a = flat
        elif name in ("x", "node_vec1"):
            padded = np.zeros((NP, a.shape[1]), a.dtype)
            padded[:N] = a
            a = padded.reshape(-1) if name == "node_vec1" else padded
        elif name in ("L2_gnn_W1", "L2_gnn_W2"):
            a = np.ascontiguousarray(a.T)
        arrays[name] = a

    counts = {}
    for final in (False, True):
        nc = bacc.Bacc("TRN2", target_bir_lowering=False, num_devices=1)
        A = {n: nc.dram_tensor(f"in_{n}", a.shape, mybir.dt.from_np(a.dtype), kind="ExternalInput").ap()
             for n, a in arrays.items()}
        out = nc.dram_tensor("out_x", (N, D), F32, kind="ExternalOutput").ap()
        build(nc, A, out, counts)
    r = run_bass_kernel_spmd(nc, [{f"in_{n}": a for n, a in arrays.items()}], core_ids=[0])
    return r.results[0]["out_x"]
```
